# Optimizing a Trainium2 kernel written in Bass

```python
import numpy as np
import jax
import jax.numpy as jnp

def _softmax(x, axis=-1):
    return jax.nn.softmax(x, axis=axis)

def _gelu(x):
    return jax.nn.gelu(x, approximate=True)

def _silu(x):
    return jax.nn.silu(x)

def _sigmoid(x):
    return jax.nn.sigmoid(x)

def _layernorm(x, axis=-1, eps=1e-05):
    m = jnp.mean(x, axis=axis, keepdims=True)
    v = jnp.var(x, axis=axis, keepdims=True)
    return (x - m) / jnp.sqrt(v + eps)

def _scatter_add(tgt, idx, src, axis=0):
    return tgt.at[idx].add(src)

def _segment_sum(src, seg, n):
    return jax.ops.segment_sum(src, seg, n)
kernel_name = 'mk_adaln_attn_ffn_d1_seqx_r4_589c89'

def setup_inputs(seed: int=0):
    np.random.seed(seed)
    _w = jnp.asarray

    def _rec_inputs():
        import jax
        import jax.numpy as jnp
        _rk = jax.random.key(seed)
        x = -0.0002928 + 1 * jax.random.normal(jax.random.fold_in(_rk, 1), (8, 512, 256), jnp.float32)
        _lenS = 512 - jax.random.randint(jax.random.fold_in(_rk, 7), (8,), 0, max(1, 512 // 4) + 1, jnp.int32)
        _lenS2 = 512 - jax.random.randint(jax.random.fold_in(_rk, 8), (8,), 0, max(1, 512 // 4) + 1, jnp.int32)
        fside_16xSxS_0 = -5.72187e-05 + 0.999849 * jax.random.normal(jax.random.fold_in(_rk, 11), (16, 512, 512), jnp.float32)
        cond_64 = -0.0265395 + 0.99382 * jax.random.normal(jax.random.fold_in(_rk, 13), (8, 64), jnp.float32)
        _validS = jnp.arange(512)[None, :] < _lenS[:, None]
        _validS2 = jnp.arange(512)[None, :] < _lenS2[:, None]
        _causal = jnp.tril(jnp.ones((512, 512), dtype=bool))
        mask_BxS_bk0 = jnp.logical_not(jnp.broadcast_to(_validS[:, :], (8, 512)))
        return (x, fside_16xSxS_0, cond_64, mask_BxS_bk0)
    x, fside_16xSxS_0, cond_64, mask_BxS_bk0 = _rec_inputs()

    def _L0_cond_setup():
        import jax, jax.numpy as jnp
        import numpy as np
        B, N, DIM, H, DH = (2, 512, 256, 16, 64)
        INNER = H * DH
        EPS = 1e-05

        def layernorm(x, g):
            mean = jnp.mean(x, axis=-1, keepdims=True)
            var = jnp.var(x, axis=-1, keepdims=True)
            return (x - mean) * jax.lax.rsqrt(var + EPS) * g
        key = jax.random.key(seed)
        ks = jax.random.split(key, 10)
        x = jax.random.normal(ks[0], (B, N, DIM), dtype=jnp.float32)
        attn_bias = jax.random.normal(ks[1], (H, N, N), dtype=jnp.float32)
        mask = jax.random.randint(ks[2], (B, N), 0, 2).astype(bool)
        g_in = jnp.ones((DIM,), dtype=jnp.float32)
        null_attn_bias = jax.random.normal(ks[3], (H,), dtype=jnp.float32)
        null_kv = jax.random.normal(ks[4], (2, DH), dtype=jnp.float32)
        Wq = jax.random.normal(ks[5], (DIM, INNER), dtype=jnp.float32) * 0.02
        Wkv = jax.random.normal(ks[6], (DIM, 2 * DH), dtype=jnp.float32) * 0.02
        Wo = jax.random.normal(ks[7], (INNER, DIM), dtype=jnp.float32) * 0.02
        g_out = jnp.ones((DIM,), dtype=jnp.float32)
        return {'x': x, 'attn_bias': attn_bias, 'mask': mask, 'g_in': g_in, 'null_attn_bias': null_attn_bias, 'null_kv': null_kv, 'Wq': Wq, 'Wkv': Wkv, 'Wo': Wo, 'g_out': g_out}
    _L0_cond_all = _L0_cond_setup()
    _L0_cond_in = {k: v for k, v in _L0_cond_all.items() if k in ('g_in', 'null_attn_bias', 'Wq', 'Wkv', 'Wo', 'g_out')}
    del _L0_cond_all

    def _L0_attn_setup():
        import jax, jax.numpy as jnp
        import numpy as np
        D_MODEL = 256
        N_HEADS = 16
        D_LATENT = 64
        HEAD_DIM = D_MODEL // N_HEADS

        def apply_rope(x):
            B, T, H, D = x.shape
            inv_freq = 1.0 / 10000.0 ** (jnp.arange(0, D, 2, dtype=jnp.float32) / D)
            t = jnp.arange(T, dtype=jnp.float32)
            freqs = t[:, None] * inv_freq[None, :]
            sin_f = jnp.sin(freqs)[None, :, None, :]
            cos_f = jnp.cos(freqs)[None, :, None, :]
            x1, x2 = jnp.split(x, 2, axis=-1)
            return jnp.concatenate([x1 * cos_f - x2 * sin_f, x1 * sin_f + x2 * cos_f], axis=-1)
        key = jax.random.key(seed)
        ks = jax.random.split(key, 10)
        B, T = (4, 1024)
        s = lambda fan_in: 1.0 / np.sqrt(fan_in)
        return {'x': jax.random.normal(ks[0], (B, T, D_MODEL), dtype=jnp.float32), 'Wq': jax.random.normal(ks[1], (D_MODEL, D_MODEL), dtype=jnp.float32) * s(D_MODEL), 'bq': jnp.zeros((D_MODEL,), jnp.float32), 'Wdown': jax.random.normal(ks[2], (D_MODEL, D_LATENT), dtype=jnp.float32) * s(D_MODEL), 'bdown': jnp.zeros((D_LATENT,), jnp.float32), 'Wup': jax.random.normal(ks[3], (D_LATENT, 2 * D_MODEL), dtype=jnp.float32) * s(D_LATENT), 'bup': jnp.zeros((2 * D_MODEL,), jnp.float32), 'Wout': jax.random.normal(ks[4], (D_MODEL, D_MODEL), dtype=jnp.float32) * s(D_MODEL), 'bout': jnp.zeros((D_MODEL,), jnp.float32)}
    _L0_attn_all = _L0_attn_setup()
    _L0_attn_in = {k: v for k, v in _L0_attn_all.items() if k in ('Wq', 'bq', 'Wdown', 'bdown', 'Wup', 'bup', 'Wout', 'bout')}
    del _L0_attn_all

    def _L0_cond2_setup():
        import jax, jax.numpy as jnp
        import numpy as np
        B, S, H = (4, 512, 256)
        E = 8
        M = 128
        K = 2
        N_SHARED = 2
        SM = M * N_SHARED
        G = 64
        GE_TEMP = 1.0
        ALPHA = 0.001
        SEQ_AUX = True
        NORM_TOPK = True
        COS_TEMP = 0.78
        CONS_ALPHA = 0.01
        LEAKY_SLOPE = 0.01
        EPS_COS = 1e-08

        def _leaky(x):
            return jnp.where(x >= 0, x, LEAKY_SLOPE * x)

        def _moe_forward(hidden_states, g, wt, wg, w_gate, w_up, w_down, sw_gate, sw_up, sw_down):
            b, s, h = hidden_states.shape
            x = hidden_states.reshape(-1, h)
            T = x.shape[0]
            logits_h = x @ wt.T
            logits_g = g @ wg.T
            logits_g = jnp.repeat(logits_g, s, axis=0)
            logits = (logits_h + logits_g / GE_TEMP) / (1.0 + 1.0 / GE_TEMP)
            scores = jax.nn.softmax(logits, axis=-1)
            topk_w, topk_idx = jax.lax.top_k(scores, K)
            if K > 1 and NORM_TOPK:
                topk_w = topk_w / (topk_w.sum(-1, keepdims=True) + 1e-20)
            onehot = jax.nn.one_hot(topk_idx.reshape(b, s * K), E, dtype=jnp.float32)
            ce = onehot.sum(1) / (s * K / E)
            aux_loss = (ce * scores.reshape(b, s, E).mean(1)).sum(1).mean() * ALPHA
            gp = _leaky(jnp.einsum('th,ehm->etm', x, w_gate))
            up = jnp.einsum('th,ehm->etm', x, w_up)
            y_all = jnp.einsum('etm,emh->eth', gp * up, w_down)
            y_sel = y_all[topk_idx, jnp.arange(T)[:, None], :]
            y = (y_sel * topk_w[..., None]).sum(1).reshape(b, s, h)
            p = _leaky(hidden_states @ sw_gate) * (hidden_states @ sw_up) @ sw_down
            y = y + p
            num = jnp.sum(y * p, -1)
            den = jnp.maximum(jnp.linalg.norm(y, axis=-1), EPS_COS) * jnp.maximum(jnp.linalg.norm(p, axis=-1), EPS_COS)
            closs = CONS_ALPHA * jnp.mean(num / den / (1.0 + COS_TEMP))
            return (y, aux_loss + closs)
        key = jax.random.key(seed)
        ks = jax.random.split(key, 12)
        sh = 1.0 / np.sqrt(H)
        sm = 1.0 / np.sqrt(M)
        ssm = 1.0 / np.sqrt(SM)
        sg = 1.0 / np.sqrt(G)
        return {'hidden_states': jax.random.normal(ks[0], (B, S, H), jnp.float32), 'g': jax.random.normal(ks[1], (B, G), jnp.float32), 'wt': jax.random.uniform(ks[2], (E, H), jnp.float32, -sh, sh), 'wg': jax.random.uniform(ks[3], (E, G), jnp.float32, -sg, sg), 'w_gate': jax.random.uniform(ks[4], (E, H, M), jnp.float32, -sh, sh), 'w_up': jax.random.uniform(ks[5], (E, H, M), jnp.float32, -sh, sh), 'w_down': jax.random.uniform(ks[6], (E, M, H), jnp.float32, -sm, sm), 'sw_gate': jax.random.uniform(ks[7], (H, SM), jnp.float32, -sh, sh), 'sw_up': jax.random.uniform(ks[8], (H, SM), jnp.float32, -sh, sh), 'sw_down': jax.random.uniform(ks[9], (SM, H), jnp.float32, -ssm, ssm)}
    _L0_cond2_all = _L0_cond2_setup()
    _L0_cond2_in = {k: v for k, v in _L0_cond2_all.items() if k in ('wt', 'wg', 'w_gate', 'w_up', 'w_down', 'sw_gate', 'sw_up', 'sw_down')}
    del _L0_cond2_all

    def _L0_ffn_setup():
        import jax, jax.numpy as jnp
        import numpy as np
        NHEAD = 16
        NUM_GROUPS = 4
        EXPERTS_PER_GROUP = 2
        LN_EPS = 1e-05

        def _layernorm(x, g, b):
            mu = jnp.mean(x, axis=-1, keepdims=True)
            var = jnp.mean(jnp.square(x - mu), axis=-1, keepdims=True)
            return (x - mu) * jax.lax.rsqrt(var + LN_EPS) * g + b

        def _mha(x, wi, bi, wo, bo):
            B, S, D = x.shape
            hd = D // NHEAD
            qkv = x @ wi.T + bi
            q, k, v = jnp.split(qkv, 3, axis=-1)

            def heads(t):
                return t.reshape(B, S, NHEAD, hd).transpose(0, 2, 1, 3)
            q, k, v = (heads(q), heads(k), heads(v))
            scores = jnp.einsum('bhqd,bhkd->bhqk', q, k) / jnp.sqrt(jnp.asarray(hd, x.dtype))
            attn = jax.nn.softmax(scores, axis=-1)
            o = jnp.einsum('bhqk,bhkd->bhqd', attn, v)
            o = o.transpose(0, 2, 1, 3).reshape(B, S, D)
            return o @ wo.T + bo

        def _hier_moe(x, w_group, b_group, w_expert, b_expert, w1, b1, w2, b2):
            B, S, D = x.shape
            xt = x.reshape(B * S, D)
            T = xt.shape[0]
            E = NUM_GROUPS * EXPERTS_PER_GROUP
            gp = jax.nn.softmax(xt @ w_group + b_group, axis=-1)
            g_idx = jnp.argmax(gp, axis=-1)
            g_prob = jnp.max(gp, axis=-1)
            elog = jnp.einsum('td,gde->tge', xt, w_expert) + b_expert
            ep = jax.nn.softmax(elog, axis=-1)
            ep_sel = jnp.take_along_axis(ep, g_idx[:, None, None], axis=1)[:, 0, :]
            e_idx_local = jnp.argmax(ep_sel, axis=-1)
            e_prob = jnp.max(ep_sel, axis=-1)
            flat_e = g_idx * EXPERTS_PER_GROUP + e_idx_local
            combine = jax.nn.one_hot(flat_e, E, dtype=xt.dtype) * (g_prob * e_prob)[:, None]
            h = jax.nn.relu(jnp.einsum('td,edf->etf', xt, w1) + b1[:, None, :])
            y = jnp.einsum('etf,efd->etd', h, w2) + b2[:, None, :]
            out = jnp.einsum('te,etd->td', combine, y)
            return out.reshape(B, S, D)
        key = jax.random.key(seed)
        ks = jax.random.split(key, 8)
        B, S, D, F = (2, 256, 256, 512)
        G, Epg = (NUM_GROUPS, EXPERTS_PER_GROUP)
        E = G * Epg
        sc = lambda fan: 1.0 / np.sqrt(fan)
        return {'x': jax.random.normal(ks[0], (B, S, D), jnp.float32), 'in_proj_w': jax.random.normal(ks[1], (3 * D, D), jnp.float32) * sc(D), 'in_proj_b': jnp.zeros((3 * D,), jnp.float32), 'out_proj_w': jax.random.normal(ks[2], (D, D), jnp.float32) * sc(D), 'out_proj_b': jnp.zeros((D,), jnp.float32), 'ln1_g': jnp.ones((D,), jnp.float32), 'ln1_b': jnp.zeros((D,), jnp.float32), 'ln2_g': jnp.ones((D,), jnp.float32), 'ln2_b': jnp.zeros((D,), jnp.float32), 'w_group': jax.random.normal(ks[3], (D, G), jnp.float32) * sc(D), 'b_group': jnp.zeros((G,), jnp.float32), 'w_expert': jax.random.normal(ks[4], (G, D, Epg), jnp.float32) * sc(D), 'b_expert': jnp.zeros((G, Epg), jnp.float32), 'w1': jax.random.normal(ks[5], (E, D, F), jnp.float32) * sc(D), 'b1': jnp.zeros((E, F), jnp.float32), 'w2': jax.random.normal(ks[6], (E, F, D), jnp.float32) * sc(F), 'b2': jnp.zeros((E, D), jnp.float32)}
    _L0_ffn_all = _L0_ffn_setup()
    _L0_ffn_in = {k: v for k, v in _L0_ffn_all.items() if k in ('in_proj_w', 'in_proj_b', 'out_proj_w', 'out_proj_b', 'ln1_g', 'ln1_b', 'ln2_g', 'ln2_b', 'w_group', 'b_group', 'w_expert', 'b_expert', 'w1', 'b1', 'w2', 'b2')}
    del _L0_ffn_all
    return {'x': x, 'fside_16xSxS_0': fside_16xSxS_0, 'cond_64': cond_64, 'mask_BxS_bk0': mask_BxS_bk0, 'L0_cond_g_in': _L0_cond_in['g_in'], 'L0_cond_null_attn_bias': _L0_cond_in['null_attn_bias'], 'L0_cond_Wq': _L0_cond_in['Wq'], 'L0_cond_Wkv': _L0_cond_in['Wkv'], 'L0_cond_Wo': _L0_cond_in['Wo'], 'L0_cond_g_out': _L0_cond_in['g_out'], 'L0_attn_Wq': _L0_attn_in['Wq'], 'L0_attn_bq': _L0_attn_in['bq'], 'L0_attn_Wdown': _L0_attn_in['Wdown'], 'L0_attn_bdown': _L0_attn_in['bdown'], 'L0_attn_Wup': _L0_attn_in['Wup'], 'L0_attn_bup': _L0_attn_in['bup'], 'L0_attn_Wout': _L0_attn_in['Wout'], 'L0_attn_bout': _L0_attn_in['bout'], 'L0_cond2_wt': _L0_cond2_in['wt'], 'L0_cond2_wg': _L0_cond2_in['wg'], 'L0_cond2_w_gate': _L0_cond2_in['w_gate'], 'L0_cond2_w_up': _L0_cond2_in['w_up'], 'L0_cond2_w_down': _L0_cond2_in['w_down'], 'L0_cond2_sw_gate': _L0_cond2_in['sw_gate'], 'L0_cond2_sw_up': _L0_cond2_in['sw_up'], 'L0_cond2_sw_down': _L0_cond2_in['sw_down'], 'L0_ffn_in_proj_w': _L0_ffn_in['in_proj_w'], 'L0_ffn_in_proj_b': _L0_ffn_in['in_proj_b'], 'L0_ffn_out_proj_w': _L0_ffn_in['out_proj_w'], 'L0_ffn_out_proj_b': _L0_ffn_in['out_proj_b'], 'L0_ffn_ln1_g': _L0_ffn_in['ln1_g'], 'L0_ffn_ln1_b': _L0_ffn_in['ln1_b'], 'L0_ffn_ln2_g': _L0_ffn_in['ln2_g'], 'L0_ffn_ln2_b': _L0_ffn_in['ln2_b'], 'L0_ffn_w_group': _L0_ffn_in['w_group'], 'L0_ffn_b_group': _L0_ffn_in['b_group'], 'L0_ffn_w_expert': _L0_ffn_in['w_expert'], 'L0_ffn_b_expert': _L0_ffn_in['b_expert'], 'L0_ffn_w1': _L0_ffn_in['w1'], 'L0_ffn_b1': _L0_ffn_in['b1'], 'L0_ffn_w2': _L0_ffn_in['w2'], 'L0_ffn_b2': _L0_ffn_in['b2']}

def reference(x, fside_16xSxS_0, cond_64, mask_BxS_bk0, L0_cond_g_in, L0_cond_null_attn_bias, L0_cond_Wq, L0_cond_Wkv, L0_cond_Wo, L0_cond_g_out, L0_attn_Wq, L0_attn_bq, L0_attn_Wdown, L0_attn_bdown, L0_attn_Wup, L0_attn_bup, L0_attn_Wout, L0_attn_bout, L0_cond2_wt, L0_cond2_wg, L0_cond2_w_gate, L0_cond2_w_up, L0_cond2_w_down, L0_cond2_sw_gate, L0_cond2_sw_up, L0_cond2_sw_down, L0_ffn_in_proj_w, L0_ffn_in_proj_b, L0_ffn_out_proj_w, L0_ffn_out_proj_b, L0_ffn_ln1_g, L0_ffn_ln1_b, L0_ffn_ln2_g, L0_ffn_ln2_b, L0_ffn_w_group, L0_ffn_b_group, L0_ffn_w_expert, L0_ffn_b_expert, L0_ffn_w1, L0_ffn_b1, L0_ffn_w2, L0_ffn_b2):
    import jax
    import jax.numpy as jnp

    def _L0_cond_ref(x, attn_bias, mask, g_in, null_attn_bias, null_kv, Wq, Wkv, Wo, g_out):
        import jax, jax.numpy as jnp
        import numpy as np
        B, N, DIM, H, DH = (2, 512, 256, 16, 64)
        INNER = H * DH
        EPS = 1e-05

        def layernorm(x, g):
            mean = jnp.mean(x, axis=-1, keepdims=True)
            var = jnp.var(x, axis=-1, keepdims=True)
            return (x - mean) * jax.lax.rsqrt(var + EPS) * g
        b, n, _ = x.shape
        scale = DH ** (-0.5)
        xn = layernorm(x, g_in)
        q = (xn @ Wq).reshape(b, n, H, DH).transpose(0, 2, 1, 3) * scale
        kv = xn @ Wkv
        k, v = (kv[..., :DH], kv[..., DH:])
        nk = jnp.broadcast_to(null_kv[0], (b, 1, DH))
        nv = jnp.broadcast_to(null_kv[1], (b, 1, DH))
        k = jnp.concatenate([nk, k], axis=1)
        v = jnp.concatenate([nv, v], axis=1)
        sim = jnp.einsum('bhid,bjd->bhij', q, k)
        null_col = jnp.broadcast_to(null_attn_bias[:, None, None], (H, n, 1))
        bias = jnp.concatenate([null_col, attn_bias], axis=-1)
        sim = sim + bias
        neg = -jnp.finfo(sim.dtype).max
        j = n + 1
        causal_mask = jnp.triu(jnp.ones((n, j), dtype=bool), k=j - n + 1)
        sim = jnp.where(causal_mask, neg, sim)
        mask_p = jnp.pad(mask, ((0, 0), (1, 0)), constant_values=True)
        sim = jnp.where(mask_p[:, None, None, :], sim, neg)
        attn = jax.nn.softmax(sim, axis=-1)
        out = jnp.einsum('bhij,bjd->bhid', attn, v)
        out = out.transpose(0, 2, 1, 3).reshape(b, n, INNER)
        out = out @ Wo
        return layernorm(out, g_out)

    def _L0_attn_ref(x, Wq, bq, Wdown, bdown, Wup, bup, Wout, bout):
        import jax, jax.numpy as jnp
        import numpy as np
        D_MODEL = 256
        N_HEADS = 16
        D_LATENT = 64
        HEAD_DIM = D_MODEL // N_HEADS

        def apply_rope(x):
            B, T, H, D = x.shape
            inv_freq = 1.0 / 10000.0 ** (jnp.arange(0, D, 2, dtype=jnp.float32) / D)
            t = jnp.arange(T, dtype=jnp.float32)
            freqs = t[:, None] * inv_freq[None, :]
            sin_f = jnp.sin(freqs)[None, :, None, :]
            cos_f = jnp.cos(freqs)[None, :, None, :]
            x1, x2 = jnp.split(x, 2, axis=-1)
            return jnp.concatenate([x1 * cos_f - x2 * sin_f, x1 * sin_f + x2 * cos_f], axis=-1)
        B, T, D = x.shape
        H, Dh = (N_HEADS, HEAD_DIM)
        q = x @ Wq + bq
        kv_latent = x @ Wdown + bdown
        kv = kv_latent @ Wup + bup
        q = q.reshape(B, T, H, Dh)
        kv = kv.reshape(B, T, H, 2 * Dh)
        k, v = jnp.split(kv, 2, axis=-1)
        q = apply_rope(q)
        k = apply_rope(k)
        att = jnp.einsum('bthd,btgd->bthg', q, k) / jnp.sqrt(jnp.float32(Dh))
        att = jax.nn.softmax(att, axis=-1)
        out = jnp.einsum('bthg,btgd->bthd', att, v)
        out = out.reshape(B, T, D)
        return out @ Wout + bout

    def _L0_cond2_ref(hidden_states, g, wt, wg, w_gate, w_up, w_down, sw_gate, sw_up, sw_down):
        import jax, jax.numpy as jnp
        import numpy as np
        B, S, H = (4, 512, 256)
        E = 8
        M = 128
        K = 2
        N_SHARED = 2
        SM = M * N_SHARED
        G = 64
        GE_TEMP = 1.0
        ALPHA = 0.001
        SEQ_AUX = True
        NORM_TOPK = True
        COS_TEMP = 0.78
        CONS_ALPHA = 0.01
        LEAKY_SLOPE = 0.01
        EPS_COS = 1e-08

        def _leaky(x):
            return jnp.where(x >= 0, x, LEAKY_SLOPE * x)

        def _moe_forward(hidden_states, g, wt, wg, w_gate, w_up, w_down, sw_gate, sw_up, sw_down):
            b, s, h = hidden_states.shape
            x = hidden_states.reshape(-1, h)
            T = x.shape[0]
            logits_h = x @ wt.T
            logits_g = g @ wg.T
            logits_g = jnp.repeat(logits_g, s, axis=0)
            logits = (logits_h + logits_g / GE_TEMP) / (1.0 + 1.0 / GE_TEMP)
            scores = jax.nn.softmax(logits, axis=-1)
            topk_w, topk_idx = jax.lax.top_k(scores, K)
            if K > 1 and NORM_TOPK:
                topk_w = topk_w / (topk_w.sum(-1, keepdims=True) + 1e-20)
            onehot = jax.nn.one_hot(topk_idx.reshape(b, s * K), E, dtype=jnp.float32)
            ce = onehot.sum(1) / (s * K / E)
            aux_loss = (ce * scores.reshape(b, s, E).mean(1)).sum(1).mean() * ALPHA
            gp = _leaky(jnp.einsum('th,ehm->etm', x, w_gate))
            up = jnp.einsum('th,ehm->etm', x, w_up)
            y_all = jnp.einsum('etm,emh->eth', gp * up, w_down)
            y_sel = y_all[topk_idx, jnp.arange(T)[:, None], :]
            y = (y_sel * topk_w[..., None]).sum(1).reshape(b, s, h)
            p = _leaky(hidden_states @ sw_gate) * (hidden_states @ sw_up) @ sw_down
            y = y + p
            num = jnp.sum(y * p, -1)
            den = jnp.maximum(jnp.linalg.norm(y, axis=-1), EPS_COS) * jnp.maximum(jnp.linalg.norm(p, axis=-1), EPS_COS)
            closs = CONS_ALPHA * jnp.mean(num / den / (1.0 + COS_TEMP))
            return (y, aux_loss + closs)
        y, _ = _moe_forward(hidden_states, g, wt, wg, w_gate, w_up, w_down, sw_gate, sw_up, sw_down)
        return y

    def _L0_ffn_ref(x, in_proj_w, in_proj_b, out_proj_w, out_proj_b, ln1_g, ln1_b, ln2_g, ln2_b, w_group, b_group, w_expert, b_expert, w1, b1, w2, b2):
        import jax, jax.numpy as jnp
        import numpy as np
        NHEAD = 16
        NUM_GROUPS = 4
        EXPERTS_PER_GROUP = 2
        LN_EPS = 1e-05

        def _layernorm(x, g, b):
            mu = jnp.mean(x, axis=-1, keepdims=True)
            var = jnp.mean(jnp.square(x - mu), axis=-1, keepdims=True)
            return (x - mu) * jax.lax.rsqrt(var + LN_EPS) * g + b

        def _mha(x, wi, bi, wo, bo):
            B, S, D = x.shape
            hd = D // NHEAD
            qkv = x @ wi.T + bi
            q, k, v = jnp.split(qkv, 3, axis=-1)

            def heads(t):
                return t.reshape(B, S, NHEAD, hd).transpose(0, 2, 1, 3)
            q, k, v = (heads(q), heads(k), heads(v))
            scores = jnp.einsum('bhqd,bhkd->bhqk', q, k) / jnp.sqrt(jnp.asarray(hd, x.dtype))
            attn = jax.nn.softmax(scores, axis=-1)
            o = jnp.einsum('bhqk,bhkd->bhqd', attn, v)
            o = o.transpose(0, 2, 1, 3).reshape(B, S, D)
            return o @ wo.T + bo

        def _hier_moe(x, w_group, b_group, w_expert, b_expert, w1, b1, w2, b2):
            B, S, D = x.shape
            xt = x.reshape(B * S, D)
            T = xt.shape[0]
            E = NUM_GROUPS * EXPERTS_PER_GROUP
            gp = jax.nn.softmax(xt @ w_group + b_group, axis=-1)
            g_idx = jnp.argmax(gp, axis=-1)
            g_prob = jnp.max(gp, axis=-1)
            elog = jnp.einsum('td,gde->tge', xt, w_expert) + b_expert
            ep = jax.nn.softmax(elog, axis=-1)
            ep_sel = jnp.take_along_axis(ep, g_idx[:, None, None], axis=1)[:, 0, :]
            e_idx_local = jnp.argmax(ep_sel, axis=-1)
            e_prob = jnp.max(ep_sel, axis=-1)
            flat_e = g_idx * EXPERTS_PER_GROUP + e_idx_local
            combine = jax.nn.one_hot(flat_e, E, dtype=xt.dtype) * (g_prob * e_prob)[:, None]
            h = jax.nn.relu(jnp.einsum('td,edf->etf', xt, w1) + b1[:, None, :])
            y = jnp.einsum('etf,efd->etd', h, w2) + b2[:, None, :]
            out = jnp.einsum('te,etd->td', combine, y)
            return out.reshape(B, S, D)
        attn_out = _mha(x, in_proj_w, in_proj_b, out_proj_w, out_proj_b)
        x = _layernorm(x + attn_out, ln1_g, ln1_b)
        moe_out = _hier_moe(x, w_group, b_group, w_expert, b_expert, w1, b1, w2, b2)
        x = _layernorm(x + moe_out, ln2_g, ln2_b)
        return x
    x = x + _L0_attn_ref(_L0_cond_ref(x, fside_16xSxS_0, mask_BxS_bk0, L0_cond_g_in, L0_cond_null_attn_bias, cond_64, L0_cond_Wq, L0_cond_Wkv, L0_cond_Wo, L0_cond_g_out), L0_attn_Wq, L0_attn_bq, L0_attn_Wdown, L0_attn_bdown, L0_attn_Wup, L0_attn_bup, L0_attn_Wout, L0_attn_bout)
    x = x + _L0_ffn_ref(_L0_cond2_ref(x, cond_64, L0_cond2_wt, L0_cond2_wg, L0_cond2_w_gate, L0_cond2_w_up, L0_cond2_w_down, L0_cond2_sw_gate, L0_cond2_sw_up, L0_cond2_sw_down), L0_ffn_in_proj_w, L0_ffn_in_proj_b, L0_ffn_out_proj_w, L0_ffn_out_proj_b, L0_ffn_ln1_g, L0_ffn_ln1_b, L0_ffn_ln2_g, L0_ffn_ln2_b, L0_ffn_w_group, L0_ffn_b_group, L0_ffn_w_expert, L0_ffn_b_expert, L0_ffn_w1, L0_ffn_b1, L0_ffn_w2, L0_ffn_b2)
    return x

_drawn_inputs = setup_inputs


def setup_inputs(seed=0):
    import zlib

    import numpy as np

    out = dict(_drawn_inputs(seed))
    spreads = {'L0_cond_g_in': (1.0, 0.2),
     'L0_cond_g_out': (1.0, 0.2),
     'L0_attn_bq': (0.0, 0.1),
     'L0_attn_bdown': (0.0, 0.1),
     'L0_attn_bup': (0.0, 0.1),
     'L0_attn_bout': (0.0, 0.1),
     'L0_ffn_in_proj_b': (0.0, 0.1),
     'L0_ffn_out_proj_b': (0.0, 0.1),
     'L0_ffn_ln1_g': (1.0, 0.2),
     'L0_ffn_ln1_b': (0.0, 0.1),
     'L0_ffn_ln2_g': (1.0, 0.2),
     'L0_ffn_ln2_b': (0.0, 0.1),
     'L0_ffn_b_group': (0.0, 0.1),
     'L0_ffn_b_expert': (0.0, 0.389),
     'L0_ffn_b1': (0.0, 0.532),
     'L0_ffn_b2': (0.0, 0.361)}
    factors = {}
    for name, (base, spread) in spreads.items():
        noise = np.random.default_rng([zlib.crc32(name.encode()), seed]).standard_normal(out[name].shape)
        drawn = base * np.exp(spread * noise) if base else spread * noise
        out[name] = jnp.asarray(drawn.astype(out[name].dtype))
    for name, factor in factors.items():
        out[name] = (out[name] * factor).astype(out[name].dtype)
    return out
```

```python
from contextlib import ExitStack

import numpy as np

import concourse.bass as bass
from concourse import mybir

F32 = mybir.dt.float32
BF16 = mybir.dt.bfloat16
U8 = mybir.dt.uint8
ALU = mybir.AluOpType
ACT = mybir.ActivationFunctionType
AX = mybir.AxisListType.X

P = 128
NB = 8
S = 512
NT = 4
D = 256
H = 16
DH = 64
EPS = 1e-5
NEG = -1.0e30
ENGINES = ("tensor", "vector", "scalar", "gpsimd", "sync")
CAUSAL = [0, 128, 384, 768, 1280]
KEYCOL = [0, 512, 896, 1152, 1280]


class Op:

    def __init__(self, eng, sem, emit, after, inc):
        self.eng, self.sem, self.emit, self.after, self.inc = eng, sem, emit, after, inc
        self.needed = inc == 16
        self.value = None
        self.slot = None


class Prog:

    def __init__(self):
        self.queues = {e: [] for e in ENGINES}
        self.phase = 0

    def fence(self):
        last = {}
        for q in self.queues.values():
            for op in q:
                if op.sem is not None and op.phase == self.phase:
                    last[op.sem] = op
        hs = list(last.values())
        for eng in ENGINES:
            self.wait(eng, hs)
        self.phase += 1

    def op(self, eng, sem, emit, *after):
        return self._put(Op(eng, sem, emit, self._flat(after), 1))

    def dma(self, eng, sem, out, in_, *after):
        return self._put(Op(eng, sem, lambda e: e.dma_start(out, in_), self._flat(after), 16))

    def wait(self, eng, *after):
        self._put(Op(eng, None, None, self._flat(after), 0))

    def _put(self, op):
        for a in op.after:
            a.needed = True
        op.phase = self.phase
        self.queues[op.eng].append(op)
        return op

    def _flat(self, xs):
        out = []
        for x in xs:
            if isinstance(x, (list, tuple)):
                out += self._flat(x)
            elif x is not None:
                out.append(x)
        return out

    def issue(self, nc, ctx):
        count, owner, slots = [], {}, {}
        for phase in range(self.phase + 1):
            used = 0
            for eng in ENGINES:
                for op in self.queues[eng]:
                    if op.phase != phase or op.sem is None or not op.needed:
                        continue
                    assert owner.setdefault((phase, op.sem), eng) == eng, op.sem
                    if (phase, op.sem) not in slots:
                        slots[phase, op.sem] = used
                        used += 1
                        if used > len(count):
                            count.append(0)
                    op.slot = slots[phase, op.sem]
                    count[op.slot] += op.inc
                    op.value = count[op.slot]
        sems = [ctx.enter_context(nc.semaphore(f"s{i}")) for i in range(len(count))]
        block = ctx.enter_context(nc.Block())

        def body(queue):
            def run(e):
                seen = {}
                for op in queue:
                    want = {}
                    for a in op.after:
                        if a.value > max(seen.get(a.slot, 0), want.get(a.slot, 0)):
                            want[a.slot] = a.value
                    for slot, value in want.items():
                        e.wait_ge(sems[slot], value)
                        seen[slot] = value
                    if op.emit is not None:
                        ins = op.emit(e)
                        if op.needed:
                            ins.then_inc(sems[op.slot], op.inc)
            return run

        block.tensor(body(self.queues["tensor"]))
        block.vector(body(self.queues["vector"]))
        block.scalar(body(self.queues["scalar"]))
        block.gpsimd(body(self.queues["gpsimd"]))
        block.sync(body(self.queues["sync"]))


class Buf:

    def __init__(self, ap):
        self.ap = ap
        self.free = []


class Ring:
    def __init__(self, aps):
        self.bufs = [Buf(a) for a in aps]
        self.n = 0

    def take(self):
        b = self.bufs[self.n % len(self.bufs)]
        self.n += 1
        return b


class Arena:
    def __init__(self, nc, start, end):
        self.nc, self.pos, self.end = nc, start, end
        self.high = start

    def __call__(self, name, shape, dt=F32):
        size = int(np.prod(shape[1:])) * mybir.dt.size(dt)
        at = (self.pos + 31) // 32 * 32
        self.pos = at + size
        self.high = max(self.high, self.pos)
        assert self.pos <= self.end, (name, self.pos, self.end)
        return self.nc.alloc_sbuf_tensor_at(name, list(shape), dt, offset=at)


def merge(*streams):
    done = [0] * len(streams)
    total = max(n for _, n in streams)
    for k in range(1, total + 1):
        for i, (g, n) in enumerate(streams):
            while done[i] < n * k // total:
                done[i] += 1
                next(g, None)
    for g, _ in streams:
        for _ in g:
            pass


def bc(ap, shape):
    return ap.broadcast_to(list(shape))


class Kernel:
    def __init__(self, nc, ctx, ins, out):
        self.nc, self.ins, self.out = nc, ins, out
        self.pr = Prog()
        self.ps = ctx.enter_context(nc.psum_tensor("ps", [P, 8, 512], F32))
        self.x1d = nc.dram_tensor("x1_scratch", [NB * NT, P, D], F32).ap()
        self.x2d = nc.dram_tensor("x2_scratch", [NB * NT, P, D], F32).ap()
        self.lo = nc.sbuf_base
        self.hi = nc.sbuf_usable_end
        sb = Arena(nc, self.lo, self.hi)
        pr = self.pr
        self.ident = sb("ident", [P, P])
        self.mhalf = sb("mhalf", [P, NT])
        self.h_ident = pr.dma("sync", "ident", self.ident[:, :], ins["c_ident"])
        self.h_mhalf = pr.op("gpsimd", "mhalf", lambda e: e.memset(self.mhalf[:, :], -0.5))
        self.base = sb.pos

    def banks(self, *ks):
        return Ring([self.ps[:, k, :] for k in ks])

    def load(self, eng, sem, dst, src, *after):
        return self.pr.dma(eng, sem, dst, src, *after)

    def ln_make(self, sb, tag, n):
        return Ring([dict(st=sb(f"{tag}st{i}", [P, NT, 6]), mv=sb(f"{tag}mv{i}", [P, NT, 2]),
                          ve=sb(f"{tag}ve{i}", [P, NT]), rs=sb(f"{tag}rs{i}", [P, NT])) for i in range(n)])

    def ln(self, tag, ring, srcs, outs, src_ready, out_free):
        pr, b = self.pr, ring.take()
        t, n = b.ap, len(srcs)
        hs = []
        for i, s in enumerate(srcs):
            hs.append(pr.op("vector", tag + "_st", lambda e, i=i, s=s: e.bn_stats(t["st"][:, i, :], s),
                            src_ready[i], b.free))
        ha = []
        for i in range(n):
            ha.append(pr.op("vector", tag + "_ag", lambda e, i=i: e.bn_aggr(t["mv"][:, i, :], t["st"][:, i, :]),
                            hs[i], b.free))
        hv = pr.op("vector", tag + "_ve",
                   lambda e: e.tensor_scalar(t["ve"][:, 0:n], t["mv"][:, 0:n, 1], EPS, None, ALU.add), ha, b.free)
        hp = pr.op("gpsimd", tag + "_rs",
                   lambda e: e.tensor_tensor(t["rs"][:, 0:n], t["ve"][:, 0:n], self.mhalf[:, 0:n], ALU.pow),
                   hv, self.h_mhalf, b.free)
        out = []
        for i in range(n):
            out.append(pr.op("vector", tag + "_xn",
                             lambda e, i=i: e.tensor_scalar(outs[i], srcs[i], t["mv"][:, i, 0:1], t["rs"][:, i:i + 1],
                                                            ALU.subtract, ALU.mult),
                             hp, out_free))
        b.free = [out[-1]]
        return out

    def phase1(self):
        nc, pr, ins, ps = self.nc, self.pr, self.ins, self.ps
        sb = Arena(nc, self.base, self.hi)
        W = {}

        def weight(name, shape, src, eng="sync", dt=F32):
            t = sb("w_" + name, shape, dt)
            v = t[tuple(slice(None) for _ in shape)]
            W[name] = t
            return pr.dma(eng, "w_" + name, v, src)

        xin = Buf(sb("xin", [P, NT, D]))
        xv = ins["x"].rearrange("b (t p) d -> b p t d", p=P)
        h_x = {0: pr.dma("sync", "xin", xin.ap[:, :, :], xv[0])}
        h_gin = weight("gin", [P, 2], ins["g_in"])
        h_wq = weight("wq", [P, 2, 1024], ins["cond_wq"].rearrange("(c p) n -> p c n", p=P))
        wk = sb("w_wk", [P, 2, 2, DH])
        wkv = ins["cond_wkv"].rearrange("(c p) n -> p c n", p=P)
        h_wk = [pr.dma("sync", f"w_wk{j}", wk[:, :, j, :], wkv[:, :, 0:DH]) for j in range(2)]
        h_wv = weight("wv", [P, 2, DH], wkv[:, :, DH:2 * DH])
        h_nk = weight("nk", [P, DH], ins["cond"][0:1, :].broadcast_to([P, DH]))
        h_nb = weight("nb", [P, NT, H], ins["null_bias"].rearrange("(o n h) -> o n h", o=1, n=1).broadcast_to([P, NT, H]))
        nv = sb("w_nv", [P, 1])
        nvc = ins["cond"][1:2, :].rearrange("a d -> d a")
        h_nv = [pr.dma("sync", f"w_nv{j}", nv[DH * j:DH * j + DH, :], nvc) for j in range(2)]
        mrow = Ring([sb(f"mrow{i}", [1, S], U8) for i in range(2)])
        bias = sb("bias", [P, H, 1280])
        fv = ins["fside"].rearrange("h (t p) k -> t p h k", p=P)
        h_bias = []
        for g in range(8):
            hd = [pr.dma("scalar", f"bias{g}_{t}", bias[:, 2 * g:2 * g + 2, CAUSAL[t]:CAUSAL[t + 1]],
                         fv[t][:, 2 * g:2 * g + 2, 0:P * (t + 1)]) for t in range(NT)]
            hh = []
            for t in range(NT):
                diag = bias[:, 2 * g:2 * g + 2, CAUSAL[t] + P * t:CAUSAL[t + 1]]
                hh.append(pr.op("gpsimd", "causal",
                                lambda e, d=diag: e.affine_select(out=d, in_=d, compare_op=ALU.is_ge, fill=NEG, base=0,
                                                                  pattern=[[0, 2], [-1, P]], channel_multiplier=1),
                                hd[t]))
            h_bias.append(hh)
        h_wo = weight("wo", [P, 8, D], ins["cond_wo"].rearrange("(c p) n -> p c n", p=P))
        h_gout = weight("gout", [P, 2], ins["g_out"])
        h_awq = weight("awq", [P, 2, D], ins["attn_wq"].rearrange("(c p) n -> p c n", p=P))
        h_bq = weight("bq", [P, D], ins["attn_bq"].rearrange("(o n) -> o n", o=1).broadcast_to([P, D]))
        h_wd = weight("wd", [P, 2, DH], ins["attn_wdown"].rearrange("(c p) n -> p c n", p=P))
        h_bd = weight("bd", [DH, 1], ins["attn_bdown"].rearrange("(n o) -> n o", o=1))
        wup = sb("w_wup", [DH + 1, 512])
        h_wup = [pr.dma("sync", "w_wup0", wup[0:DH, :], ins["attn_wup"]),
                 pr.dma("sync", "w_wup1", wup[DH:DH + 1, :], ins["attn_bup"].rearrange("(o n) -> o n", o=1))]
        h_wout = weight("wout", [P, 2, D], ins["attn_wout"].rearrange("(c p) n -> p c n", p=P))
        h_bout = weight("bout", [P, D], ins["attn_bout"].rearrange("(o n) -> o n", o=1).broadcast_to([P, D]))
        h_cos = weight("cos", [P, NT, 16], ins["c_cos"])
        h_sin = weight("sin", [P, NT, 16], ins["c_sin"])

        maskm = Ring([sb(f"maskm{i}", [P, S], BF16) for i in range(2)])
        onesm = sb("onesm", [P, P], BF16)
        for i, m in enumerate(maskm.bufs):
            m.free = [pr.op("vector", "maskm0", lambda e, m=m: e.memset(m.ap[:, :], 0.0))]
        h_om0 = pr.op("vector", "onesm0", lambda e: e.memset(onesm[:, :], 0.0))
        h_ones = pr.op("vector", "onesm", lambda e: e.memset(onesm[0:1, :], 1.0), h_om0)

        tmpA = sb("prodv", [P, 2048])
        tmpB = sb("prodg", [P, 2048])
        wnull = sb("wnull", [P, 2, H])
        hn = []
        for c in range(2):
            t3 = tmpA[:, c * 1024:(c + 1) * 1024].rearrange("p (h d) -> p h d", h=H)
            q3 = W["wq"][:, c, :].rearrange("p (h d) -> p h d", h=H)
            a = pr.op("vector", "wn0", lambda e, t3=t3, q3=q3: e.tensor_tensor(
                t3, q3, W["nk"][:, :].unsqueeze(1).broadcast_to([P, H, DH]), ALU.mult), h_wq, h_nk)
            b = pr.op("vector", "wn1", lambda e, t3=t3, c=c: e.tensor_reduce(wnull[:, c, :], t3, AX, ALU.add), a)
            hn.append(pr.op("vector", "wn2", lambda e, c=c: e.tensor_scalar(wnull[:, c, :], wnull[:, c, :], 0.125, None,
                                                                            ALU.mult), b))
        h_wnull = hn
        nvb = sb("nvb", [P, 8, H])
        h0 = pr.op("vector", "nvb0", lambda e: e.memset(nvb[:, :, :], 0.0))
        hb = []
        for c in range(8):
            for j in range(2):
                hb.append(pr.op("vector", "nvb", lambda e, c=c, j=j: e.tensor_copy(
                    nvb[DH * j:DH * j + DH, c, 2 * c + j:2 * c + j + 1], nv[DH * j:DH * j + DH, :]), h0, h_nv))
        nvwo = sb("nvwo", [H, D])
        mm = None
        for c in range(8):
            mm = pr.op("tensor", "nvwo_mm", lambda e, c=c: e.matmul(ps[0:H, 7, 0:D], nvb[:, c, :], W["wo"][:, c, :],
                                                                    start=(c == 0), stop=(c == 7)), hb, h_wo)
        h_nvwo = pr.op("vector", "nvwo", lambda e: e.tensor_copy(nvwo[:, :], ps[0:H, 7, 0:D]), mm)

        xnT = Buf(sb("xnT", [P, 2, S]))
        qT = sb("qT", [P, 8, S])
        qbuf = [Buf(qT[:, p, :]) for p in range(8)]
        kz = Ring([sb(f"kz{i}", [P, 2, S]) for i in range(2)])
        vt = Ring([sb(f"vt{i}", [P, NT, DH]) for i in range(2)])
        snl = Ring([sb(f"snl{i}", [P, NT, H]) for i in range(2)])
        pbuf = Ring([sb(f"pb{i}", [P, 1280]) for i in range(3)])
        ptb = Ring([sb(f"ptb{i}", [P, 1280]) for i in range(2)])
        mst = Ring([sb(f"mst{i}", [P, 6, 2, NT]) for i in range(4)])
        pnn = Buf(sb("pnn", [P, NT, H]))
        pnT = Buf(sb("pnT", [H, S]))
        hnb = Buf(sb("hn", [P, NT, D]))
        hT = Buf(sb("hT", [P, 2, S]))
        latT = Buf(sb("latT", [DH + 1, S]))
        qs = Ring([sb(f"qs{i}", [P, D]) for i in range(2)])
        kvs = Ring([sb(f"kvs{i}", [P, H, 32]) for i in range(2)])
        rp = Ring([sb(f"rp{i}", [P, 3, D]) for i in range(1)])
        sc = Ring([sb(f"sc{i}", [P, D]) for i in range(2)])
        sm = Ring([sb(f"sm{i}", [P, 3, H]) for i in range(2)])
        ob = Ring([sb(f"ob{i}", [P, D]) for i in range(2)])
        oT = Ring([sb(f"oT{i}", [P, 2, P]) for i in range(2)])
        xr = Ring([sb(f"xr{i}", [P, D]) for i in range(2)])
        pv, pg = Buf(tmpA), Buf(tmpB)
        lnx = self.ln_make(sb, "lnx", 1)
        lno = self.ln_make(sb, "lno", 2)
        self.high1 = sb.high
        h_latones = pr.op("vector", "latones", lambda e: e.memset(latT.ap[DH:DH + 1, :], 1.0))

        rS = self.banks(0, 1, 2)
        rT = self.banks(3, 4)
        rO = self.banks(5)
        rM = self.banks(6, 7)
        rM.bufs[1].free = [h_nvwo]
        self.ident_ready = self.h_ident
        state = {}
        flip = [0]

        def copy_out(sem, out, in_, *after, again=False):
            flip[0] += 0 if again else 1
            if flip[0] % 2:
                return pr.op("vector", sem + "_v", lambda e: e.tensor_copy(out, in_), *after)
            return pr.op("scalar", sem + "_a", lambda e: e.activation(out, in_, ACT.Copy), *after)

        def stage_pre(b):
            st = state[b] = {}
            x = xin.ap
            hx = h_x[b]
            hxn = self.ln("lnx", lnx, [x[:, t, :] for t in range(NT)], [x[:, t, :] for t in range(NT)], [hx] * NT, [])
            yield
            ev = []
            tr_all = []
            for c in range(2):
                m = rM.take()
                tr = None
                for t in range(NT):
                    tr = pr.op("tensor", "xT", lambda e, c=c, t=t, m=m: e.transpose(
                        m.ap[:, t * P:(t + 1) * P], x[:, t, c * P:(c + 1) * P], self.ident[:, :]),
                        hxn[t], self.h_ident, m.free)
                tr_all.append(tr)
                h = pr.op("scalar", "xnT", lambda e, c=c, m=m: e.activation(
                    xnT.ap[:, c, :], m.ap, ACT.Identity, scale=W["gin"][:, c:c + 1]), tr, h_gin, xnT.free)
                m.free = [h]
                ev.append(h)
                yield
            if b + 1 < NB:
                h_x[b + 1] = pr.dma("sync", "xin", xin.ap[:, :, :], xv[b + 1], tr_all)
            users = []
            i = mrow.n % 2
            m8, mk = mrow.take(), maskm.take()
            hm8 = pr.dma("sync", f"mrow{i}", m8.ap[:, :], ins["mask"][b:b + 1, :].bitcast(U8), m8.free)
            hmk = pr.op("vector", "maskm", lambda e, mk=mk, m8=m8: e.tensor_scalar(
                mk.ap[0:1, :], m8.ap[:, :], 1.0, -NEG, ALU.subtract, ALU.mult), hm8, mk.free)
            m8.free, mk.free = [hmk], []
            st["mk"], st["hmk"] = mk, hmk
            m = rM.take()
            for c in range(2):
                mm = pr.op("tensor", "kmm", lambda e, c=c, m=m: e.matmul(
                    m.ap, wk[:, c, :, :], xnT.ap[:, c, :], start=(c == 0), stop=(c == 1)), ev, h_wk, m.free)
            users.append(mm)
            k = kz.take()
            if b < 2:
                k.free = [pr.op("vector", "kz0", lambda e, k=k: e.memset(k.ap[:, :, :], 0.0))]
            hk = [pr.op("scalar", "kcp", lambda e, j=j, m=m, k=k: e.activation(
                k.ap[DH * j:DH * j + DH, j, :], m.ap[DH * j:DH * j + DH, :], ACT.Copy), mm, k.free) for j in range(2)]
            m.free = hk
            k.free = []
            st["k"], st["hk"] = k, hk
            yield
            m = rM.take()
            for t in range(NT):
                for c in range(2):
                    mm = pr.op("tensor", "vmm", lambda e, c=c, t=t, m=m: e.matmul(
                        m.ap[:, t * DH:(t + 1) * DH], xnT.ap[:, c, t * P:(t + 1) * P], W["wv"][:, c, :],
                        start=(c == 0), stop=(c == 1)), ev, h_wv, m.free)
                for c in range(2):
                    mm = pr.op("tensor", "vmm", lambda e, c=c, t=t, m=m: e.matmul(
                        m.ap[:, 256 + t * H:256 + (t + 1) * H], xnT.ap[:, c, t * P:(t + 1) * P], wnull[:, c, :],
                        start=(c == 0), stop=(c == 1)), h_wnull)
            users.append(mm)
            v, sn = vt.take(), snl.take()
            hv = pr.op("vector", "vcp", lambda e, m=m, v=v: e.tensor_copy(v.ap[:, :, :], m.ap[:, 0:256]), mm, v.free)
            hs = pr.op("vector", "snl", lambda e, m=m, sn=sn: e.tensor_tensor(
                sn.ap[:, :, :], m.ap[:, 256:256 + NT * H], W["nb"][:, :, :], ALU.add), mm, h_nb, sn.free)
            m.free = [hv, hs]
            v.free, sn.free = [], []
            st["v"], st["hv"], st["sn"], st["hs"] = v, hv, sn, hs
            yield
            st["ev"], st["hq"], st["users"] = ev, [], users

        def queries(b, p):
            st = state[b]
            m = rM.take()
            for c in range(2):
                mm = pr.op("tensor", "qmm", lambda e, c=c: e.matmul(
                    m.ap, W["wq"][:, c, p * P:(p + 1) * P], xnT.ap[:, c, :], start=(c == 0), stop=(c == 1)),
                    st["ev"], h_wq, m.free)
            flip[0] += 1
            if flip[0] % 2:
                h = pr.op("vector", "qcp_v", lambda e: e.tensor_scalar(
                    qbuf[p].ap, m.ap, 0.125, None, ALU.mult), mm, qbuf[p].free)
            else:
                h = pr.op("scalar", "qcp_a", lambda e: e.activation(
                    qbuf[p].ap, m.ap, ACT.Copy, scale=0.125), mm, qbuf[p].free)
            m.free = [h]
            qbuf[p].free = []
            st["hq"].append(h)
            if p == 7:
                xnT.free = st["users"] + [mm]

        def scores(b, h):
            st = state[b]
            p, j = h // 2, h % 2
            if j == 0:
                st["ms", p] = mst.take()
            ms = st["ms", p]
            mx, nm, dn, pn, rs, rc = [ms.ap[:, i, :, :] for i in range(6)]
            pb = pbuf.take()
            k, sn = st["k"], st["sn"]
            hm, hmm = [], []
            for t in range(NT):
                n = P * (t + 1)
                m = rS.take()
                pr.op("tensor", "S", lambda e, t=t, n=n, m=m: e.matmul(
                    m.ap[:, 0:n], qbuf[p].ap[:, t * P:(t + 1) * P], k.ap[:, j, 0:n], start=True, stop=False),
                    st["hq"][p], st["hk"], m.free)
                mm = pr.op("tensor", "S", lambda e, n=n, m=m: e.matmul(
                    m.ap[:, 0:n], onesm[:, :], st["mk"].ap[:, 0:n], start=False, stop=True), st["hmk"], h_ones)
                hh = pr.op("vector", "ttr", lambda e, t=t, n=n, m=m: e.tensor_tensor_reduce(
                    pb.ap[:, CAUSAL[t]:CAUSAL[t + 1]], m.ap[:, 0:n], bias[:, h, CAUSAL[t]:CAUSAL[t + 1]],
                    1.0, sn.ap[:, t, h:h + 1], ALU.add, ALU.max, mx[:, j, t:t + 1]),
                    mm, h_bias[h // 2], st["hs"], pb.free, ms.free)
                m.free = [hh]
                hm.append(hh)
            k.free.append(mm)
            st["mk"].free.append(mm)
            qbuf[p].free.append(mm)
            hn_ = pr.op("vector", "nm", lambda e: e.tensor_scalar(nm[:, j, :], mx[:, j, :], -1.0, None, ALU.mult), hm, ms.free)
            hd = pr.op("vector", "dn", lambda e: e.tensor_tensor(dn[:, j, :], sn.ap[:, :, h], nm[:, j, :], ALU.add), hn_, ms.free)
            sn.free.append(hd)
            he = [pr.op("scalar", "exp", lambda e, t=t: e.activation(
                pb.ap[:, CAUSAL[t]:CAUSAL[t + 1]], pb.ap[:, CAUSAL[t]:CAUSAL[t + 1]], ACT.Exp,
                bias=nm[:, j, t:t + 1], accum_out=rs[:, j, t:t + 1]), hm, hn_, ms.free) for t in range(NT)]
            hp = pr.op("scalar", "pn", lambda e: e.activation(pn[:, j, :], dn[:, j, :], ACT.Exp), hd, ms.free)
            st["P", h] = (pb, he, hp)

        def normal(b, h):
            st = state[b]
            p, j = h // 2, h % 2
            ms = st["ms", p]
            mx, nm, dn, pn, rs, rc = [ms.ap[:, i, :, :] for i in range(6)]
            pb, he, hp = st["P", h]
            h1 = pr.op("vector", "den", lambda e: e.tensor_tensor(dn[:, j, :], rs[:, j, :], pn[:, j, :], ALU.add), he, hp)
            h2 = pr.op("vector", "rden", lambda e: e.reciprocal(rc[:, j, :], dn[:, j, :]), h1, ms.free if j == 0 else [])
            h3 = pr.op("vector", "pnn", lambda e: e.tensor_tensor(pnn.ap[:, :, h], pn[:, j, :], rc[:, j, :], ALU.mult),
                       h2, pnn.free)
            st.setdefault("pnn", []).append(h3)
            hg = [pr.op("gpsimd", "pnorm", lambda e, t=t: e.tensor_scalar(
                pb.ap[:, CAUSAL[t]:CAUSAL[t + 1]], pb.ap[:, CAUSAL[t]:CAUSAL[t + 1]], rc[:, j, t:t + 1], 1.0,
                ALU.mult, ALU.mult), h2) for t in range(NT)]
            st["hg", h] = hg
            if j == 1:
                ms.free = [st["h3", p], h3, st["hg", h - 1], hg]
            else:
                st["h3", p] = h3

        def turn(b, h):
            st = state[b]
            pb = st["P", h][0]
            hg = st["hg", h]
            pt = ptb.take()
            out = []
            tr = None
            for lot in ([(0, t) for t in range(4)], [(1, t) for t in range(1, 4)] + [(3, 3)], [(2, 2), (2, 3)]):
                m = rT.take()
                for i, (kt, t) in enumerate(lot):
                    tr = pr.op("tensor", "PT", lambda e, i=i, kt=kt, t=t, m=m: e.transpose(
                        m.ap[:, i * P:(i + 1) * P], pb.ap[:, CAUSAL[t] + kt * P:CAUSAL[t] + (kt + 1) * P],
                        self.ident[:, :]), hg[t], self.h_ident, m.free)
                kt0, t0 = lot[0]
                n0 = len([1 for kt, _ in lot if kt == kt0]) * P
                ho = [copy_out("ptc", pt.ap[:, KEYCOL[kt0]:KEYCOL[kt0] + n0], m.ap[:, 0:n0], tr, pt.free)]
                if n0 < len(lot) * P:
                    ho.append(copy_out("ptc", pt.ap[:, KEYCOL[3]:KEYCOL[4]], m.ap[:, n0:n0 + P], tr, pt.free, again=True))
                m.free = ho
                out += ho
                yield
            pb.free = [tr]
            pt.free = []
            st["PT", h] = (pt, out)

        def values(b, p):
            st = state[b]
            m = rO.take()
            v = st["v"]
            mm = None
            last = []
            for kt in range(NT):
                for j in range(2):
                    pt, hp = st["PT", 2 * p + j]
                    mm = pr.op("tensor", "O", lambda e, kt=kt, j=j, pt=pt, m=m: e.matmul(
                        m.ap[DH * j:DH * j + DH, kt * P:S], v.ap[:, kt, :], pt.ap[:, KEYCOL[kt]:KEYCOL[kt + 1]],
                        start=(kt == 0), stop=(kt == NT - 1), tile_position=(0, DH * j)), hp, st["hv"], m.free)
            for j in range(2):
                st["PT", 2 * p + j][0].free = [mm]
            v.free = [mm]
            h = copy_out("oc", qbuf[p].ap, m.ap, mm, qbuf[p].free)
            m.free = [h]
            st["O", p] = h

        def stage_attn(b):
            st = state[b]
            queries(b, 0)
            yield
            queries(b, 1)
            yield
            for i in range(H + 3):
                if i < H:
                    scores(b, i)
                if i % 2 == 0 and i // 2 + 2 < 8:
                    queries(b, i // 2 + 2)
                yield
                if 1 <= i <= H:
                    normal(b, i - 1)
                yield
                if i >= 4 and i % 2 == 0:
                    values(b, i // 2 - 2)
                yield
                if 2 <= i <= H + 1:
                    yield from turn(b, i - 2)
            pnn.free = []
            m = rM.take()
            tr = None
            for t in range(NT):
                tr = pr.op("tensor", "pnT_t", lambda e, t=t, m=m: e.transpose(
                    m.ap[0:H, t * P:(t + 1) * P], pnn.ap[:, t, :], self.ident[:, :]), st["pnn"], m.free)
            pnn.free = [tr]
            hp = pr.op("vector", "pnT", lambda e, m=m: e.tensor_copy(pnT.ap[:, :], m.ap[0:H, :]), tr, pnT.free)
            m.free = [hp]
            yield
            hpre = []
            for u in range(2):
                m = rM.take()
                hm = []
                for i in range(2):
                    t = 2 * u + i
                    for p in range(8):
                        pr.op("tensor", "wo", lambda e, t=t, p=p, i=i, m=m: e.matmul(
                            m.ap[:, i * D:(i + 1) * D], qbuf[p].ap[:, t * P:(t + 1) * P], W["wo"][:, p, :],
                            start=(p == 0), stop=False), st["O", p], h_wo, m.free)
                    mm = pr.op("tensor", "wo", lambda e, t=t, i=i, m=m: e.matmul(
                        m.ap[:, i * D:(i + 1) * D], pnT.ap[:, t * P:(t + 1) * P], nvwo[:, :], start=False, stop=True),
                        hp, h_nvwo)
                    hm.append(mm)
                yield
                hx = self.ln("lno", lno, [m.ap[:, 0:D], m.ap[:, D:2 * D]],
                             [hnb.ap[:, 2 * u, :], hnb.ap[:, 2 * u + 1, :]], [mm, mm], hnb.free)
                m.free = hx
                hpre += hx
                yield
            for p in range(8):
                qbuf[p].free = [mm]
            pnT.free = [mm]
            st["hn"] = hpre

        def stage_heads(b):
            st = state[b]
            ev, trs = [], []
            for c in range(2):
                m = rM.take()
                for t in range(NT):
                    tr = pr.op("tensor", "hT_t", lambda e, c=c, t=t, m=m: e.transpose(
                        m.ap[:, t * P:(t + 1) * P], hnb.ap[:, t, c * P:(c + 1) * P], self.ident[:, :]), st["hn"], m.free)
                h = pr.op("scalar", "hT", lambda e, c=c, m=m: e.activation(
                    hT.ap[:, c, :], m.ap, ACT.Identity, scale=W["gout"][:, c:c + 1]), tr, h_gout, hT.free)
                m.free = [h]
                ev.append(h)
                yield
            hnb.free = [tr]
            m = rM.take()
            for c in range(2):
                mm = pr.op("tensor", "lat", lambda e, c=c, m=m: e.matmul(
                    m.ap[0:DH, :], W["wd"][:, c, :], hT.ap[:, c, :], start=(c == 0), stop=(c == 1)), ev, h_wd, m.free)
            hl = pr.op("scalar", "latT", lambda e, m=m: e.activation(
                latT.ap[0:DH, :], m.ap[0:DH, :], ACT.Identity, bias=W["bd"][:, :]), mm, h_bd, latT.free)
            m.free = [hl]
            yield
            ho = []
            for t in range(NT):
                m = rM.take()
                for c in range(2):
                    mq = pr.op("tensor", "q2", lambda e, c=c, t=t, m=m: e.matmul(
                        m.ap[:, 0:D], hT.ap[:, c, t * P:(t + 1) * P], W["awq"][:, c, :], start=(c == 0), stop=(c == 1)),
                        ev, h_awq, m.free)
                q = qs.take()
                hq = pr.op("vector", "q2b", lambda e, m=m, q=q: e.tensor_tensor(
                    q.ap[:, :], m.ap[:, 0:D], W["bq"][:, :], ALU.add), mq, h_bq, q.free)
                m.free = [hq]
                m = rM.take()
                mk = pr.op("tensor", "kv2", lambda e, t=t, m=m: e.matmul(
                    m.ap, latT.ap[:, t * P:(t + 1) * P], wup[:, :], start=True, stop=True), hl, h_latones, h_wup, m.free)
                kv = kvs.take()
                hkv = pr.op("scalar", "kv2c", lambda e, m=m, kv=kv: e.activation(kv.ap[:, :, :], m.ap, ACT.Copy), mk, kv.free)
                m.free = [hkv]
                yield
                r = rp.take()
                cosb = W["cos"][:, t, :].unsqueeze(1).broadcast_to([P, H, 16])
                sin = W["sin"][:, t, :]
                rot = []
                for i, (src, ready) in enumerate(((q.ap[:, :].rearrange("p (h d) -> p h d", h=H), hq),
                                                  (kv.ap[:, :, 0:16], hkv))):
                    t1 = r.ap[:, i, :].rearrange("p (h d) -> p h d", h=H)
                    t2 = r.ap[:, 2, :].rearrange("p (h d) -> p h d", h=H)
                    a = pr.op("gpsimd", "rot1", lambda e, t1=t1, src=src, cosb=cosb: e.tensor_tensor(t1, src, cosb, ALU.mult),
                              ready, h_cos, r.free)
                    bb = [pr.op("gpsimd", "rot2", lambda e, t2=t2, src=src, u=u, sin=sin: e.tensor_tensor(
                        t2[:, :, 8 * u:8 * u + 8], src[:, :, 8 - 8 * u:16 - 8 * u],
                        sin[:, 8 * u:8 * u + 8].unsqueeze(1).broadcast_to([P, H, 8]), ALU.mult),
                        ready, h_sin, r.free, rot) for u in range(2)]
                    rot.append(pr.op("gpsimd", "rot3", lambda e, t1=t1, t2=t2: e.tensor_tensor(t1, t1, t2, ALU.add), a, bb))
                q.free = [rot[0]]
                yield
                q3 = r.ap[:, 0, :].rearrange("p (h d) -> p h d", h=H)
                k3 = r.ap[:, 1, :].rearrange("p (h d) -> p h d", h=H)
                s, mm_ = sc.take(), sm.take()
                s3 = s.ap[:, :].rearrange("p (h g) -> p h g", h=H)
                pva = pv.ap[:, :].rearrange("p (h g d) -> p h g d", h=8, g=H)
                hr = []
                for u in range(2):
                    hm = pr.op("vector", "hs_m", lambda e, q3=q3, k3=k3, u=u: e.tensor_tensor(
                        pva, q3[:, 8 * u:8 * u + 8, :].unsqueeze(2).broadcast_to([P, 8, H, 16]),
                        k3.unsqueeze(1).broadcast_to([P, 8, H, 16]), ALU.mult), rot, pv.free)
                    hr.append(pr.op("vector", "hs_r", lambda e, s3=s3, u=u: e.tensor_reduce(
                        s3[:, 8 * u:8 * u + 8, :], pva, AX, ALU.add), hm, s.free))
                    pv.free = [hr[-1]]
                r.free = [hm]
                yield
                a = pr.op("vector", "hs_x", lambda e, s3=s3, mm_=mm_: e.tensor_reduce(mm_.ap[:, 0, :], s3, AX, ALU.max), hr, mm_.free)
                a = pr.op("vector", "hs_d", lambda e, s3=s3, mm_=mm_: e.tensor_tensor(
                    s3, s3, mm_.ap[:, 0, :].unsqueeze(2).broadcast_to([P, H, H]), ALU.subtract), a)
                he = pr.op("scalar", "hs_e", lambda e, s=s: e.activation(s.ap[:, :], s.ap[:, :], ACT.Exp, scale=0.25), a)
                a = pr.op("vector", "hs_s", lambda e, s3=s3, mm_=mm_: e.tensor_reduce(mm_.ap[:, 1, :], s3, AX, ALU.add), he, mm_.free)
                hrc = pr.op("vector", "hs_c", lambda e, mm_=mm_: e.reciprocal(mm_.ap[:, 2, :], mm_.ap[:, 1, :]), a, mm_.free)
                yield
                pga = pg.ap[:, :].rearrange("p (h d g) -> p h d g", h=8, g=H)
                v3 = kv.ap[:, :, 16:32].rearrange("p g d -> p d g")
                o = ob.take()
                o3 = o.ap[:, :].rearrange("p (h d) -> p h d", h=H)
                hr = []
                for u in range(2):
                    hm = pr.op("gpsimd", "hv_m", lambda e, s3=s3, v3=v3, u=u: e.tensor_tensor(
                        pga, s3[:, 8 * u:8 * u + 8, :].unsqueeze(2).broadcast_to([P, 8, 16, H]),
                        v3.unsqueeze(1).broadcast_to([P, 8, 16, H]), ALU.mult), he, hkv, pg.free)
                    hr.append(pr.op("vector", "hv_r", lambda e, o3=o3, u=u: e.tensor_reduce(
                        o3[:, 8 * u:8 * u + 8, :], pga, AX, ALU.add), hm, o.free))
                    pg.free = [hr[-1]]
                    yield
                s.free = [hm, a]
                kv.free = [hm, rot[1]]
                hn_ = pr.op("vector", "hv_n", lambda e, o3=o3, mm_=mm_: e.tensor_tensor(
                    o3, o3, mm_.ap[:, 2, :].unsqueeze(2).broadcast_to([P, H, 16]), ALU.mult), hr, hrc)
                mm_.free = [hn_]
                m = rM.take()
                for c in range(2):
                    tr = pr.op("tensor", "oT_t", lambda e, c=c, o=o, m=m: e.transpose(
                        m.ap[:, c * P:(c + 1) * P], o.ap[:, c * P:(c + 1) * P], self.ident[:, :]), hn_, m.free)
                o.free = [tr]
                ot = oT.take()
                hc = pr.op("scalar", "oT", lambda e, ot=ot, m=m: e.activation(
                    ot.ap[:, :, :], m.ap[:, 0:D].rearrange("p (c k) -> p c k", c=2), ACT.Copy), tr, ot.free)
                m.free = [hc]
                yield
                xb = xr.take()
                i = b * NT + t
                hx = pr.dma("sync", f"xr{i % 2}", xb.ap[:, :], ins["x"][b, t * P:(t + 1) * P, :], xb.free)
                hx = pr.op("gpsimd", "xb", lambda e, xb=xb: e.tensor_tensor(xb.ap[:, :], xb.ap[:, :], W["bout"][:, :], ALU.add),
                           hx, h_bout)
                m = rM.take()
                for c in range(2):
                    mm = pr.op("tensor", "wout", lambda e, c=c, ot=ot, m=m: e.matmul(
                        m.ap[:, 0:D], ot.ap[:, c, :], W["wout"][:, c, :], start=(c == 0), stop=(c == 1)),
                        hc, h_wout, m.free)
                ot.free = [mm]
                h1 = pr.op("vector", "x1", lambda e, m=m, xb=xb: e.tensor_tensor(
                    xb.ap[:, :], m.ap[:, 0:D], xb.ap[:, :], ALU.add), mm, hx)
                m.free = [h1]
                hd = pr.dma("sync", f"x1d{i % 2}", self.x1d[i], xb.ap[:, :], h1)
                xb.free = [hd]
                ho.append(hd)
                yield
            hT.free = [mq]
            latT.free = [mk]
            self.x1_done[b] = ho

        self.x1_done = {}
        for _ in stage_pre(0):
            pass
        for b in range(NB):
            streams = [(stage_attn(b), 120)]
            if b > 0:
                streams.append((stage_heads(b - 1), 35))
            if b + 1 < NB:
                streams.append((self.delayed(stage_pre, b + 1, 16), 21))
            merge(*streams)
        for _ in stage_heads(NB - 1):
            pass

    def delayed(self, stage, b, n):
        for _ in range(n):
            yield
        yield from stage(b)

    def row(self, v):
        return v.rearrange("(o n) -> o n", o=1).broadcast_to([P, v.shape[0]])

    def phase2(self):
        self.pr.fence()
        self.experts()
        self.pr.fence()
        self.mha()

    def experts(self):
        nc, pr, ins, ps = self.nc, self.pr, self.ins, self.ps
        sb = Arena(nc, self.base, self.hi)
        self.yd = nc.dram_tensor("y_scratch", [NB * NT, P, D], F32).ap()
        E, M = 8, 128

        def weight(name, shape, src, eng="sync"):
            t = sb("ew_" + name, shape)
            return t, pr.dma(eng, "ew_" + name, t[tuple(slice(None) for _ in shape)], src)

        wt, h_wt = weight("wt", [P, 2, E], ins["moe_wt"].rearrange("(c p) e -> p c e", p=P))
        wg, h_wg = weight("wg", [DH, E], ins["moe_wg"])
        cT, h_cT = weight("cT", [DH, NB], ins["condT"][:, 0:NB])
        before, h_before = weight("before", [P, E, E], ins["c_before"])
        gate = sb("e_gate", [P, E, 2, M])
        up = sb("e_up", [P, E, 2, M])
        down = sb("e_down", [P, E, D])
        h_gate, h_up, h_down = [], [], []
        sg, h_sg = weight("sg", [P, 2, 2 * M], ins["sh_gate"].rearrange("(c p) m -> p c m", p=P), "scalar")
        su, h_su = weight("su", [P, 2, 2 * M], ins["sh_up"].rearrange("(c p) m -> p c m", p=P), "scalar")
        sd, h_sd = weight("sd", [P, 2, D], ins["sh_down"].rearrange("(c p) m -> p c m", p=P), "scalar")
        for x in range(E):
            h_gate.append(pr.dma("scalar", f"e_gate{x}", gate[:, x, :, :], ins["moe_gate"][x].rearrange("(c p) m -> p c m", p=P)))
            h_up.append(pr.dma("scalar", f"e_up{x}", up[:, x, :, :], ins["moe_up"][x].rearrange("(c p) m -> p c m", p=P)))
            h_down.append(pr.dma("scalar", f"e_down{x}", down[:, x, :], ins["moe_down"][x]))
        xb = Ring([sb(f"e_x{i}", [P, NT, D]) for i in range(2)])
        xT = Ring([sb(f"e_xT{i}", [P, 2, S]) for i in range(2)])
        lg = Ring([sb(f"e_lg{i}", [P, NT, E]) for i in range(2)])
        sm = Ring([sb(f"e_sm{i}", [P, 4, NT]) for i in range(2)])
        cmp_ = Buf(sb("e_cmp", [P, 2, NT, E, E]))
        gt = Ring([sb(f"e_gt{i}", [P, 2, NT, E]) for i in range(2)])
        lk = Ring([sb(f"e_lk{i}", [P, 2, S]) for i in range(2)])
        aT = Ring([sb(f"e_aT{i}", [P, S]) for i in range(3)])
        yb = Ring([sb(f"e_y{i}", [P, NT, D]) for i in range(2)])
        gb = sb("e_gb", [DH, NB, P])
        h_gb = pr.op("vector", "e_gb", lambda e: e.tensor_copy(
            gb[:, :, :], cT[:, :].unsqueeze(2).broadcast_to([DH, NB, P])), h_cT)
        rR, rG, rU, rD = self.banks(0, 1), self.banks(2, 3), self.banks(4, 5), self.banks(6, 7)
        state = {}

        def route(b):
            st = state[b] = {}
            x, xt = xb.take(), xT.take()
            hx = pr.dma("sync", f"e_x{b % 2}", x.ap[:, :, :], self.x1d[b * NT:(b + 1) * NT].rearrange("t p d -> p t d"),
                        x.free, self.x1_done[b])
            yield
            ev = []
            for c in range(2):
                m = rR.take()
                for t in range(NT):
                    tr = pr.op("tensor", "e_tr", lambda e, c=c, t=t, m=m: e.transpose(
                        m.ap[:, t * P:(t + 1) * P], x.ap[:, t, c * P:(c + 1) * P], self.ident[:, :]), hx, m.free)
                h = pr.op("scalar", "e_xT", lambda e, c=c, m=m: e.activation(xt.ap[:, c, :], m.ap, ACT.Copy), tr, xt.free)
                m.free = [h]
                ev.append(h)
                yield
            x.free, xt.free = [tr], []
            st["xt"], st["ev"] = xt, ev
            m = rR.take()
            for t in range(NT):
                for c in range(2):
                    pr.op("tensor", "e_lg", lambda e, c=c, t=t, m=m: e.matmul(
                        m.ap[:, t * E:(t + 1) * E], xt.ap[:, c, t * P:(t + 1) * P], wt[:, c, :], start=(c == 0), stop=False),
                        ev, h_wt, m.free)
                mm = pr.op("tensor", "e_lg", lambda e, t=t, m=m: e.matmul(
                    m.ap[:, t * E:(t + 1) * E], gb[:, b, :], wg[:, :], start=False, stop=True), h_gb, h_wg)
            l, s_, g = lg.take(), sm.take(), gt.take()
            lv = l.ap[:, :, :]
            h = pr.op("scalar", "e_lgc", lambda e, m=m: e.activation(
                lv, m.ap[:, 0:NT * E].rearrange("p (t e) -> p t e", t=NT), ACT.Copy, scale=0.5), mm, l.free)
            m.free = [h]
            yield
            col = lambda k: s_.ap[:, k, :]
            wide = lambda k: s_.ap[:, k, :].unsqueeze(2).broadcast_to([P, NT, E])
            a = pr.op("vector", "e_r", lambda e: e.tensor_reduce(col(0), lv, AX, ALU.max), h, s_.free)
            a = pr.op("vector", "e_r", lambda e: e.tensor_tensor(lv, lv, wide(0), ALU.subtract), a)
            h = pr.op("scalar", "e_exp", lambda e: e.activation(lv, lv, ACT.Exp), a)
            a = pr.op("vector", "e_r", lambda e: e.tensor_reduce(col(1), lv, AX, ALU.add), h)
            a = pr.op("vector", "e_r", lambda e: e.reciprocal(col(2), col(1)), a)
            a = pr.op("vector", "e_r", lambda e: e.tensor_tensor(lv, lv, wide(2), ALU.mult), a)
            yield
            four = [P, NT, E, E]
            c0, c1 = cmp_.ap[:, 0, :, :, :], cmp_.ap[:, 1, :, :, :]
            for t in range(NT):
                oth = lv[:, t, :].unsqueeze(1).broadcast_to([P, E, E])
                own = lv[:, t, :].unsqueeze(2).broadcast_to([P, E, E])
                k1 = pr.op("vector", "e_r", lambda e, t=t, oth=oth, own=own: e.tensor_tensor(c0[:, t, :, :], oth, own, ALU.is_gt),
                           a, cmp_.free)
                k2 = pr.op("vector", "e_r", lambda e, t=t, oth=oth, own=own: e.tensor_tensor(c1[:, t, :, :], oth, own, ALU.is_equal),
                           a, cmp_.free)
                k3 = pr.op("vector", "e_r", lambda e, t=t: e.tensor_tensor(c1[:, t, :, :], c1[:, t, :, :], before[:, :, :], ALU.mult),
                           k2, h_before)
                k4 = pr.op("vector", "e_r", lambda e, t=t: e.tensor_tensor(c0[:, t, :, :], c0[:, t, :, :], c1[:, t, :, :], ALU.add),
                           k1, k3)
            gv, sel = g.ap[:, 0, :, :], g.ap[:, 1, :, :]
            a = pr.op("vector", "e_r", lambda e: e.tensor_reduce(sel, c0, AX, ALU.add), k4, g.free)
            cmp_.free = [a]
            yield
            a = pr.op("vector", "e_r", lambda e: e.tensor_scalar(sel, sel, 1.5, None, ALU.is_lt), a)
            a = pr.op("vector", "e_r", lambda e: e.tensor_tensor(gv, sel, lv, ALU.mult), a)
            l.free = [a]
            a = pr.op("vector", "e_r", lambda e: e.tensor_reduce(col(3), gv, AX, ALU.add), a)
            a = pr.op("vector", "e_r", lambda e: e.tensor_scalar(col(3), col(3), 1e-20, None, ALU.add), a)
            a = pr.op("vector", "e_r", lambda e: e.reciprocal(col(2), col(3)), a)
            a = pr.op("vector", "e_r", lambda e: e.tensor_tensor(gv, gv, wide(2), ALU.mult), a)
            s_.free = [a]
            g.free = []
            st["g"], st["hg"] = g, a
            yield

        def body(b, wgate, wup, wdown, ready_in, ready_out):
            st = state[b]
            xt = st["xt"]
            mg, mu = rG.take(), rU.take()
            for c in range(2):
                m1 = pr.op("tensor", "e_g", lambda e, c=c: e.matmul(
                    mg.ap, wgate(c), xt.ap[:, c, :], start=(c == 0), stop=(c == 1)), st["ev"], ready_in, mg.free)
            for c in range(2):
                m2 = pr.op("tensor", "e_u", lambda e, c=c: e.matmul(
                    mu.ap, wup(c), xt.ap[:, c, :], start=(c == 0), stop=(c == 1)), mu.free)
            k, a = lk.take(), aT.take()
            h1 = pr.op("scalar", "e_lk", lambda e: e.activation(k.ap[:, 0, :], mg.ap, ACT.Copy, scale=0.01), m1, k.free)
            h2 = pr.op("vector", "e_mx", lambda e: e.tensor_tensor(k.ap[:, 1, :], mg.ap, k.ap[:, 0, :], ALU.max), h1, k.free)
            h3 = pr.op("vector", "e_ml", lambda e: e.tensor_tensor(a.ap[:, :], mu.ap, k.ap[:, 1, :], ALU.mult), m2, h2, a.free)
            mg.free, mu.free, k.free, a.free = [h2], [h3], [h3], []
            xt.free.append(m2)
            return a, h3

        def run(b):
            st = state[b]
            y = yb.take()
            parts = []
            for u in range(2):
                parts.append(body(b, lambda c, u=u: sg[:, c, u * M:(u + 1) * M], lambda c, u=u: su[:, c, u * M:(u + 1) * M],
                                  None, [h_sg, h_su], None))
                yield
            hy = {}
            for v in range(2):
                m = rD.take()
                for i in range(2):
                    t = 2 * v + i
                    for u in range(2):
                        a, ha = parts[u]
                        mm = pr.op("tensor", "e_d", lambda e, a=a, t=t, i=i, u=u, m=m: e.matmul(
                            m.ap[:, i * D:(i + 1) * D], a.ap[:, t * P:(t + 1) * P], sd[:, u, :], start=(u == 0), stop=(u == 1)),
                            ha, h_sd, m.free)
                h = pr.op("scalar", "e_y0", lambda e, v=v, m=m: e.activation(
                    y.ap[:, 2 * v:2 * v + 2, :], m.ap.rearrange("p (t d) -> p t d", t=2), ACT.Copy), mm, y.free)
                m.free = [h]
                hy[2 * v] = hy[2 * v + 1] = h
                yield
            for a, _ in parts:
                a.free = [mm]
            wait = []
            for x in range(E + 1):
                if x < E:
                    wait.append((x, body(b, lambda c, x=x: gate[:, x, c, :], lambda c, x=x: up[:, x, c, :], None,
                                         [h_gate[x], h_up[x]], None)))
                    yield
                if x >= 1:
                    z, (a, ha) = wait.pop(0)
                    for v in range(2):
                        m = rD.take()
                        for i in range(2):
                            t = 2 * v + i
                            mm = pr.op("tensor", "e_d", lambda e, a=a, t=t, i=i, z=z, m=m: e.matmul(
                                m.ap[:, i * D:(i + 1) * D], a.ap[:, t * P:(t + 1) * P], down[:, z, :], start=True, stop=True),
                                ha, h_down[z], m.free)
                        hs = []
                        for i in range(2):
                            t = 2 * v + i
                            hy[t] = pr.op("vector", "e_acc", lambda e, t=t, i=i, z=z, m=m: e.scalar_tensor_tensor(
                                y.ap[:, t, :], m.ap[:, i * D:(i + 1) * D], st["g"].ap[:, 0, t, z:z + 1], y.ap[:, t, :],
                                ALU.mult, ALU.add), mm, st["hg"], hy[t])
                            hs.append(hy[t])
                        m.free = hs
                    a.free = [mm]
                    yield
            st["g"].free = list(hy.values())
            hd = pr.dma("sync", f"e_yd{b % 2}", self.yd[b * NT:(b + 1) * NT].rearrange("t p d -> p t d"), y.ap[:, :, :],
                        list(hy.values()))
            y.free = [hd]
            self.y_done[b] = [hd]

        self.y_done = {}
        for _ in route(0):
            pass
        for b in range(NB):
            streams = [(run(b), 22)]
            if b + 1 < NB:
                streams.append((route(b + 1), 8))
            merge(*streams)
        self.high2 = sb.high

    def mha(self):
        nc, pr, ins, ps = self.nc, self.pr, self.ins, self.ps
        sb = Arena(nc, self.base, self.hi)
        F32R = mybir.dt.float32r
        scr = nc.dram_tensor("qk_scratch", [2, 4, D, S], F32).ap()

        def weight(name, shape, src, eng="sync"):
            t = sb("mw_" + name, shape)
            return t, pr.dma(eng, "mw_" + name, t[tuple(slice(None) for _ in shape)], src)

        wi, h_wi = weight("wi", [P, 2, 3 * D], ins["wi"].rearrange("(c p) n -> p c n", p=P))
        bic, h_bic = weight("bic", [P, 6], ins["bic"])
        bv, h_bv = weight("bv", [P, D], self.row(ins["bi"][2 * D:3 * D]))
        wo, h_wo = weight("wo", [P, 2, D], ins["wo2"].rearrange("(c p) n -> p c n", p=P))
        bo, h_bo = weight("bo", [P, D], self.row(ins["bo2"]))
        g1, h_g1 = weight("g1", [P, D], self.row(ins["ln1_g"]))
        b1, h_b1 = weight("b1", [P, D], self.row(ins["ln1_b"]))
        bq = sb("m_bq", [P, 2])
        h_bq = pr.op("vector", "m_bq", lambda e: e.tensor_scalar(bq[:, :], bic[:, 0:2], 0.25, None, ALU.mult), h_bic)
        G4 = 4
        KS = 50
        xb = Buf(sb("m_x", [P, NT, D]))
        yT = Buf(sb("m_yT", [P, 2, S]))
        full = Buf(sb("m_full", [P, S]))
        part = Ring([sb(f"m_part{i}", [P, 2, S], F32R) for i in range(2)])
        qst = [Buf(sb(f"m_qs{i}", [KS, G4, S], F32R)) for i in range(8)]
        kst = [Buf(sb(f"m_ks{i}", [KS, G4, S], F32R)) for i in range(8)]
        va = Ring([sb(f"m_va{i}", [P, NT, H, 32]) for i in range(2)])
        mx = Ring([sb(f"m_mx{i}", [P, NT, H]) for i in range(2)])
        mrow = Buf(sb("m_mrow", [H, S]))
        mhl = Buf(sb("m_mhl", [H, 2, S], F32R))
        pt = Ring([sb(f"m_pt{i}", [P, G4, S]) for i in range(2)])
        of = Ring([sb(f"m_of{i}", [P, S]) for i in range(1)])
        rc = Ring([sb(f"m_rc{i}", [P, NT, G4]) for i in range(1)])
        ot = Buf(sb("m_ot", [P, NT, H, 16]))
        oT = Ring([sb(f"m_oT{i}", [P, 2, P]) for i in range(1)])
        zb = Ring([sb(f"m_z{i}", [P, D]) for i in range(2)])
        lnr = self.ln_make(sb, "m_ln", 1)
        ones = sb("m_one", [2, S], F32R)
        self.high3 = sb.high
        o1 = pr.op("vector", "m_one", lambda e: e.memset(ones[:, :].bitcast(F32), 1.0))
        o1 = pr.op("vector", "m_one", lambda e: e.tensor_copy(ones[:, :], ones[:, :].bitcast(F32)), o1)
        for i, k in enumerate(kst):
            k.free = [pr.dma("sync", f"m_kone{i}_{j}", k.ap[48:50, j, :].bitcast(F32), ones[:, :].bitcast(F32), o1)
                      for j in range(G4)]
        for i, v in enumerate(va.bufs):
            v.free = [pr.op("vector", "m_va1", lambda e, v=v: e.memset(v.ap[:, :, :, :], 1.0))]
        rM, rS, rO = self.banks(0), self.banks(1, 2), self.banks(7)
        rE = Ring([ps[:, 3:5, :], ps[:, 5:7, :]])
        state = {}

        def project(b):
            st = state[b] = {}
            hx = pr.dma("sync", "m_x", xb.ap[:, :, :], self.yd[b * NT:(b + 1) * NT].rearrange("t p d -> p t d"),
                        xb.free, self.y_done[b])
            yield
            ev = []
            for c in range(2):
                m = rM.take()
                for t in range(NT):
                    tr = pr.op("tensor", "m_tr", lambda e, c=c, t=t, m=m: e.transpose(
                        m.ap[:, t * P:(t + 1) * P], xb.ap[:, t, c * P:(c + 1) * P], self.ident[:, :]), hx, m.free)
                h = pr.op("scalar", "m_yT", lambda e, c=c, m=m: e.activation(yT.ap[:, c, :], m.ap, ACT.Copy), tr, yT.free)
                m.free = [h]
                ev.append(h)
                yield
            xb.free = [tr]
            hst = []
            for w in range(2):
                hi, lo = part.take(), part.take()
                for c in range(2):
                    m = rM.take()
                    for k in range(2):
                        mm = pr.op("tensor", "m_qk", lambda e, c=c, k=k, w=w, m=m: e.matmul(
                            m.ap, wi[:, k, w * D + c * P:w * D + (c + 1) * P], yT.ap[:, k, :], start=(k == 0), stop=(k == 1)),
                            ev, h_wi, m.free)
                    if w == 0:
                        h = pr.op("scalar", "m_qc", lambda e, c=c, m=m: e.activation(
                            full.ap[:, :], m.ap, ACT.Identity, bias=bq[:, c:c + 1], scale=0.25), mm, h_bq, full.free)
                    else:
                        h = pr.op("scalar", "m_kc", lambda e, c=c, m=m: e.activation(
                            full.ap[:, :], m.ap, ACT.Identity, bias=bic[:, 2 + c:3 + c]), mm, h_bic, full.free)
                    m.free = [h]
                    hh = pr.op("gpsimd", "m_hi", lambda e, c=c, hi=hi: e.tensor_scalar(
                        hi.ap[:, c, :], full.ap[:, :], 1.0, 1.0, ALU.mult, ALU.mult), h, hi.free)
                    hl = pr.op("gpsimd", "m_lo", lambda e, c=c, hi=hi, lo=lo: e.tensor_tensor(
                        lo.ap[:, c, :], full.ap[:, :], hi.ap[:, c, :].bitcast(F32), ALU.subtract), hh, lo.free)
                    full.free = [hl]
                    yield
                for i, (u, hu) in enumerate(((hi, [hh, hl]), (lo, [hl]))):
                    hd = pr.dma("sync", f"m_sc{2 * w + i}", scr[b % 2, 2 * w + i].rearrange("(c p) t -> p c t", p=P),
                                u.ap[:, :, :].bitcast(F32), hu, state[b - 2]["loaded"] if b >= 2 else [])
                    u.free = [hd]
                    hst.append(hd)
            st["stored"] = hst
            v = va.take()
            hv = []
            for u in range(2):
                m = rM.take()
                for i in range(2):
                    for k in range(2):
                        mm = pr.op("tensor", "m_v", lambda e, t=2 * u + i, i=i, k=k, m=m: e.matmul(
                            m.ap[:, i * D:(i + 1) * D], yT.ap[:, k, t * P:(t + 1) * P], wi[:, k, 2 * D:3 * D],
                            start=(k == 0), stop=(k == 1)), ev, h_wi, m.free)
                h = [pr.op("vector", "m_vc", lambda e, t=2 * u + i, i=i, m=m: e.tensor_tensor(
                    v.ap[:, t, :, 0:16], m.ap[:, i * D:(i + 1) * D].rearrange("p (h d) -> p h d", h=H),
                    bv[:, :].rearrange("p (h d) -> p h d", h=H), ALU.add), mm, h_bv, v.free) for i in range(2)]
                m.free = h
                hv += h
                yield
            yT.free = [mm]
            v.free = []
            st["v"], st["hv"] = v, hv

        def load(b):
            st = state[b]
            st["stack"] = {}
            st["loaded"] = []
            for g in range(4):
                i = (b % 2) * 4 + g
                hs = []
                for nm, bufs, order in (("q", qst, (0, 0, 1)), ("k", kst, (2, 3, 2))):
                    for s_, p_ in enumerate(order):
                        hs.append(pr.dma("sync", f"m_st{nm}{s_}_{i}", bufs[i].ap[16 * s_:16 * s_ + 16, :, :].bitcast(F32),
                                         scr[b % 2, p_, 64 * g:64 * g + 64].rearrange("(h d) t -> d h t", d=16),
                                         st["stored"], bufs[i].free))
                kst[i].free, qst[i].free = [], []
                st["stack"][g] = hs
                st["loaded"] += hs

        def maxima(b):
            st = state[b]
            x = mx.take()
            hm = []
            for h in range(H):
                i = (b % 2) * 4 + h // 4
                for t in range(NT):
                    m = rS.take()
                    mm = pr.op("tensor", "m_S", lambda e, h=h, t=t, i=i, m=m: e.matmul(
                        m.ap, qst[i].ap[0:48, h % 4, t * P:(t + 1) * P], kst[i].ap[0:48, h % 4, :], start=True, stop=True),
                        st["stack"][h // 4], m.free)
                    r = pr.op("vector", "m_max", lambda e, h=h, t=t, m=m: e.tensor_reduce(
                        x.ap[:, t, h:h + 1], m.ap, AX, ALU.max), mm, x.free)
                    m.free = [r]
                    hm.append(r)
                    yield
            m = rM.take()
            for t in range(NT):
                tr = pr.op("tensor", "m_mT", lambda e, t=t, m=m: e.transpose(
                    m.ap[0:H, t * P:(t + 1) * P], x.ap[:, t, :], self.ident[:, :]), hm, m.free)
            x.free = [tr]
            h = pr.op("vector", "m_neg", lambda e, m=m: e.tensor_scalar(
                mrow.ap[:, :], m.ap[0:H, :], -1.0, None, ALU.mult), tr, mrow.free)
            m.free = [h]
            h1 = pr.op("vector", "m_nhi", lambda e: e.tensor_copy(mhl.ap[:, 0, :], mrow.ap[:, :]), h, mhl.free)
            h2 = pr.op("vector", "m_nlo", lambda e: e.tensor_tensor(
                mhl.ap[:, 1, :], mrow.ap[:, :], mhl.ap[:, 0, :].bitcast(F32), ALU.subtract), h1)
            mrow.free = [h2]
            hs = []
            for g in range(4):
                i = (b % 2) * 4 + g
                for u in range(2):
                    hs.append(pr.dma("sync", f"m_mr{i}_{u}", qst[i].ap[48 + u:49 + u, :, :].bitcast(F32),
                                     mhl.ap[4 * g:4 * g + 4, u, :].bitcast(F32), h2, mm))
            mhl.free = hs
            st["neg"] = hs
            yield

        def attend(b):
            st = state[b]
            v = st["v"]
            ho = []
            for g in range(4):
                i = (b % 2) * 4 + g
                o = rO.take()
                pend = []
                for kt in range(NT + 1):
                    if kt < NT:
                        p = pt.take()
                        he = []
                        for w in range(2):
                            m = rE.take()
                            for j in range(2):
                                mm = pr.op("tensor", "m_ST", lambda e, kt=kt, w=w, j=j, m=m, i=i: e.matmul(
                                    m.ap[:, j, :], kst[i].ap[:, 2 * w + j, kt * P:(kt + 1) * P], qst[i].ap[:, 2 * w + j, :],
                                    start=True, stop=True), st["stack"][g], st["neg"], m.free)
                            h = pr.op("scalar", "m_exp", lambda e, w=w, m=m, p=p: e.activation(
                                p.ap[:, 2 * w:2 * w + 2, :], m.ap, ACT.Exp), mm, p.free)
                            m.free = [h]
                            he.append(h)
                            yield
                        p.free = []
                        pend.append((kt, p, he))
                    if kt >= 1:
                        k0, p0, h0 = pend.pop(0)
                        for j in range(4):
                            av = pr.op("tensor", "m_AV", lambda e, k0=k0, p0=p0, j=j, o=o, g=g: e.matmul(
                                o.ap[32 * j:32 * j + 32, :], v.ap[:, k0, 4 * g + j, :], p0.ap[:, j, :],
                                start=(k0 == 0), stop=(k0 == NT - 1), tile_position=(0, 32 * j)), h0, st["hv"], o.free)
                        p0.free = [av]
                        yield
                qst[i].free, kst[i].free = [mm], [mm]
                f = of.take()
                h = pr.op("vector", "m_of", lambda e, f=f, o=o: e.tensor_copy(f.ap[:, :], o.ap), av, f.free)
                o.free = [h]
                m = rM.take()
                for t in range(NT):
                    tr = pr.op("tensor", "m_ofT", lambda e, t=t, m=m, f=f: e.transpose(
                        m.ap[:, t * P:(t + 1) * P], f.ap[:, t * P:(t + 1) * P], self.ident[:, :]), h, m.free)
                f.free = [tr]
                r = rc.take()
                m4 = m.ap.rearrange("p (t h d) -> p t h d", t=NT, h=G4)
                hr = pr.op("vector", "m_rc", lambda e, r=r, m4=m4: e.reciprocal(r.ap[:, :, :], m4[:, :, :, 16]), tr, r.free)
                hn = pr.op("vector", "m_on", lambda e, r=r, m4=m4, g=g: e.tensor_tensor(
                    ot.ap[:, :, 4 * g:4 * g + 4, :], m4[:, :, :, 0:16],
                    r.ap[:, :, :].unsqueeze(3).broadcast_to([P, NT, G4, 16]), ALU.mult), hr, ot.free)
                m.free = [hn]
                r.free = [hn]
                ho.append(hn)
                yield
            v.free = [av]
            done = []
            for t in range(NT):
                m = rM.take()
                for c in range(2):
                    tr = pr.op("tensor", "m_oT_t", lambda e, c=c, t=t, m=m: e.transpose(
                        m.ap[:, c * P:(c + 1) * P], ot.ap[:, t, 8 * c:8 * c + 8, :], self.ident[:, :]), ho, m.free)
                q = oT.take()
                h = pr.op("scalar", "m_oT", lambda e, q=q, m=m: e.activation(
                    q.ap[:, :, :], m.ap[:, 0:D].rearrange("p (c k) -> p c k", c=2), ACT.Copy), tr, q.free)
                m.free = [h]
                z = zb.take()
                n = b * NT + t
                hz = pr.dma("sync", f"m_z{n % 2}", z.ap[:, :], self.yd[n], z.free, self.y_done[b])
                hz = pr.op("gpsimd", "m_zb", lambda e, z=z: e.tensor_tensor(z.ap[:, :], z.ap[:, :], bo[:, :], ALU.add), hz, h_bo)
                yield
                m = rM.take()
                for c in range(2):
                    mm = pr.op("tensor", "m_wo", lambda e, c=c, q=q, m=m: e.matmul(
                        m.ap[:, 0:D], q.ap[:, c, :], wo[:, c, :], start=(c == 0), stop=(c == 1)), h, h_wo, m.free)
                q.free = [mm]
                a = pr.op("vector", "m_zs", lambda e, z=z, m=m: e.tensor_tensor(
                    z.ap[:, :], m.ap[:, 0:D], z.ap[:, :], ALU.add), mm, hz)
                m.free = [a]
                a = self.ln("m_ln", lnr, [z.ap[:, :]], [z.ap[:, :]], [a], [])
                a = pr.op("gpsimd", "m_lg", lambda e, z=z: e.tensor_tensor(z.ap[:, :], z.ap[:, :], g1[:, :], ALU.mult), a, h_g1)
                a = pr.op("gpsimd", "m_lb", lambda e, z=z: e.tensor_tensor(z.ap[:, :], z.ap[:, :], b1[:, :], ALU.add), a, h_b1)
                hd = pr.dma("sync", f"m_x2{n % 2}", self.x2d[n], z.ap[:, :], a)
                z.free = [hd]
                done.append(hd)
                yield
            ot.free = [tr]
            self.x2_done[b] = done

        self.x2_done = {}
        for _ in project(0):
            pass
        load(0)
        for _ in maxima(0):
            pass
        if NB > 1:
            for _ in project(1):
                pass
            load(1)
        for b in range(NB):
            streams = [(attend(b), 60)]
            if b + 1 < NB:
                streams.append((maxima(b + 1), 65))
            merge(*streams)
            if b + 2 < NB:
                for _ in project(b + 2):
                    pass
                load(b + 2)

    def gating(self, tag, l, s_, w, ready, before, h_before, l_free):
        pr = self.pr
        v = lambda fn, *after: pr.op("vector", tag, fn, *after)
        G, X = 4, 2
        gl = l[:, :, 0:4]
        xl = l[:, :, 4:12].rearrange("p t (g x) -> p t g x", g=G)
        col = lambda k: s_[:, k, :, 0]
        wide = lambda k: s_[:, k, :, 0].unsqueeze(2).broadcast_to([P, NT, G])
        quad = lambda k: s_[:, k, :, :]
        qwide = lambda k: s_[:, k, :, :].unsqueeze(3).broadcast_to([P, NT, G, X])
        a1 = v(lambda e: e.tensor_reduce(col(0), gl, AX, ALU.max), ready, l_free)
        a2 = v(lambda e: e.tensor_reduce(quad(1), xl, AX, ALU.max), ready, l_free)
        a1 = v(lambda e: e.tensor_tensor(gl, gl, wide(0), ALU.subtract), a1)
        a2 = v(lambda e: e.tensor_tensor(xl, xl, qwide(1), ALU.subtract), a2)
        h = pr.op("scalar", tag + "_e", lambda e: e.activation(l[:, :, :], l[:, :, :], ACT.Exp), a1, a2)
        a1 = v(lambda e: e.tensor_reduce(col(2), gl, AX, ALU.add), h)
        a2 = v(lambda e: e.tensor_reduce(quad(3), xl, AX, ALU.add), h)
        a1 = v(lambda e: e.reciprocal(col(4), col(2)), a1)
        a2 = v(lambda e: e.reciprocal(quad(5), quad(3)), a2)
        a1 = v(lambda e: e.tensor_tensor(gl, gl, wide(4), ALU.mult), a1)
        a2 = v(lambda e: e.tensor_tensor(xl, xl, qwide(5), ALU.mult), a2)
        b1 = v(lambda e: e.tensor_reduce(col(6), gl, AX, ALU.max), a1)
        b2 = v(lambda e: e.tensor_tensor(quad(7), gl, wide(6), ALU.is_ge), b1)
        pairs = w.rearrange("p t (g x) -> p t g x", g=G)
        cnt = []
        for g in range(G):
            c = v(lambda e, g=g: e.tensor_tensor(s_[:, 9:13, :, g].rearrange("p j t -> p t j"), quad(7),
                                                 before[:, g, 0:G].unsqueeze(1).broadcast_to([P, NT, G]), ALU.mult), b2, h_before)
            cnt.append(c)
        for g in range(G):
            cnt[g] = v(lambda e, g=g: e.tensor_reduce(s_[:, 8, :, g], s_[:, 9:13, :, g].rearrange("p j t -> p t j"), AX, ALU.add), cnt[g])
        c = v(lambda e: e.tensor_scalar(quad(8), quad(8), 0.5, None, ALU.is_lt), cnt)
        c = v(lambda e: e.tensor_tensor(quad(7), quad(7), quad(8), ALU.mult), c)
        c = v(lambda e: e.tensor_tensor(quad(7), quad(7), wide(6), ALU.mult), c)
        d1 = v(lambda e: e.tensor_reduce(quad(1), xl, AX, ALU.max), a2)
        c = v(lambda e: e.tensor_tensor(quad(7), quad(7), quad(1), ALU.mult), c, d1)
        d2 = v(lambda e: e.tensor_tensor(quad(3), xl[:, :, :, 0], xl[:, :, :, 1], ALU.is_ge), a2)
        e1 = v(lambda e: e.tensor_tensor(pairs[:, :, :, 0], quad(7), quad(3), ALU.mult), c, d2)
        return [v(lambda e: e.tensor_tensor(pairs[:, :, :, 1], quad(7), pairs[:, :, :, 0], ALU.subtract), e1)]

    def phase3(self):
        self.pr.fence()
        nc, pr, ins, ps = self.nc, self.pr, self.ins, self.ps
        sb = Arena(nc, self.base, self.hi)
        E, F = 8, 512

        def weight(name, shape, src, eng="sync"):
            t = sb("hw_" + name, shape)
            return t, pr.dma(eng, "hw_" + name, t[tuple(slice(None) for _ in shape)], src)

        wgx = sb("hw_gx", [P, 2, 12])
        bgx = sb("hw_bgx", [P, 12])
        h_gx = [pr.dma("sync", "hw_g", wgx[:, :, 0:4], ins["w_group"].rearrange("(c p) g -> p c g", p=P)),
                pr.dma("sync", "hw_bg", bgx[:, 0:4], self.row(ins["b_group"])),
                pr.dma("sync", "hw_bx", bgx[:, 4:12], self.row(ins["b_expert"]))]
        h_gx += [pr.dma("sync", f"hw_x{g}_{c}", wgx[:, c, 4 + 2 * g:6 + 2 * g], ins["w_expert"][g, c * P:(c + 1) * P, :])
                 for g in range(4) for c in range(2)]
        before, h_before = weight("before", [P, E, E], ins["c_before"])
        b1, h_b1 = weight("b1", [P, E, 4], ins["b1c"])
        b2, h_b2 = weight("b2", [E, D], ins["b2"])
        g2, h_g2 = weight("g2", [P, D], self.row(ins["ln2_g"]))
        c2, h_c2 = weight("c2", [P, D], self.row(ins["ln2_b"]))
        w1 = sb("hw_w1", [P, E, 2, F])
        w2 = sb("hw_w2", [P, E, 4, D])
        h_w1, h_w2 = [], []
        for x in range(E):
            h_w1.append(pr.dma("scalar", f"hw_w1{x}", w1[:, x, :, :], ins["w1"][x].rearrange("(c p) f -> p c f", p=P)))
            h_w2.append(pr.dma("scalar", f"hw_w2{x}", w2[:, x, :, :], ins["w2"][x].rearrange("(c p) d -> p c d", p=P)))
        xb = Ring([sb(f"h_x{i}", [P, NT, D]) for i in range(2)])
        xT = Ring([sb(f"h_xT{i}", [P, 2, S]) for i in range(2)])
        lg = Ring([sb(f"h_lg{i}", [P, NT, 12]) for i in range(2)])
        sm = Ring([sb(f"h_sm{i}", [P, 13, NT, 4]) for i in range(2)])
        cw = Ring([sb(f"h_cw{i}", [P, NT, E]) for i in range(2)])
        cT = Ring([sb(f"h_cT{i}", [E, S]) for i in range(2)])
        hT = Ring([sb(f"h_hT{i}", [P, 4, S]) for i in range(2)])
        rr = Ring([sb(f"h_r{i}", [P, D]) for i in range(2)])
        lnr = self.ln_make(sb, "h_ln", 2)
        rR, rH, rD = self.banks(0, 1), self.banks(2, 3, 4), self.banks(5, 6, 7)
        state = {}

        def route(b):
            st = state[b] = {}
            x, xt = xb.take(), xT.take()
            hx = pr.dma("sync", f"h_x{b % 2}", x.ap[:, :, :], self.x2d[b * NT:(b + 1) * NT].rearrange("t p d -> p t d"),
                        x.free, self.x2_done[b])
            yield
            ev = []
            for c in range(2):
                m = rR.take()
                for t in range(NT):
                    tr = pr.op("tensor", "h_tr", lambda e, c=c, t=t, m=m: e.transpose(
                        m.ap[:, t * P:(t + 1) * P], x.ap[:, t, c * P:(c + 1) * P], self.ident[:, :]), hx, m.free)
                h = pr.op("scalar", "h_xT", lambda e, c=c, m=m: e.activation(xt.ap[:, c, :], m.ap, ACT.Copy), tr, xt.free)
                m.free = [h]
                ev.append(h)
                yield
            xt.free = []
            st["x"], st["xt"], st["ev"] = x, xt, ev
            m = rR.take()
            for t in range(NT):
                for c in range(2):
                    mm = pr.op("tensor", "h_lg", lambda e, c=c, t=t, m=m: e.matmul(
                        m.ap[:, t * 12:(t + 1) * 12], xt.ap[:, c, t * P:(t + 1) * P], wgx[:, c, :], start=(c == 0), stop=(c == 1)),
                        ev, h_gx, m.free)
            l, s_, w = lg.take(), sm.take(), cw.take()
            h = pr.op("vector", "h_lgb", lambda e, m=m: e.tensor_tensor(
                l.ap[:, :, :], m.ap[:, 0:NT * 12].rearrange("p (t e) -> p t e", t=NT),
                bgx[:, :].unsqueeze(1).broadcast_to([P, NT, 12]), ALU.add), mm, h_gx, l.free)
            m.free = [h]
            yield
            hw = self.gating("h_gate", l.ap, s_.ap, w.ap[:, :, :], h, before, h_before, [s_.free, w.free])
            s_.free, l.free, w.free = hw, hw, []
            st["w"], st["hw"] = w, hw
            yield
            m = rR.take()
            for t in range(NT):
                tr2 = pr.op("tensor", "h_cT_t", lambda e, t=t, m=m: e.transpose(
                    m.ap[0:E, t * P:(t + 1) * P], w.ap[:, t, :], self.ident[:, :]), hw, m.free)
            c_ = cT.take()
            h = pr.op("scalar", "h_cT", lambda e, m=m: e.activation(c_.ap[:, :], m.ap[0:E, :], ACT.Copy), tr2, c_.free)
            m.free = [h]
            hy = {}
            for v in range(2):
                m = rR.take()
                for i in range(2):
                    mm = pr.op("tensor", "h_b2", lambda e, t=2 * v + i, i=i, m=m: e.matmul(
                        m.ap[:, i * D:(i + 1) * D], c_.ap[:, t * P:(t + 1) * P], b2[:, :], start=True, stop=True), h, h_b2, m.free)
                hh = pr.op("vector", "h_y0", lambda e, v=v, m=m: e.tensor_tensor(
                    x.ap[:, 2 * v:2 * v + 2, :], m.ap.rearrange("p (t d) -> p t d", t=2), x.ap[:, 2 * v:2 * v + 2, :],
                    ALU.add), mm, tr, hx)
                m.free = [hh]
                hy[2 * v] = hy[2 * v + 1] = hh
                yield
            c_.free = [mm]
            st["hy"] = hy

        def run(b):
            st = state[b]
            y, xt, hy = st["x"], st["xt"], st["hy"]
            wait = []
            for x in range(E + 1):
                if x < E:
                    ht = hT.take()
                    hs = []
                    for f in range(4):
                        m = rH.take()
                        for c in range(2):
                            mm = pr.op("tensor", "h_h", lambda e, f=f, c=c, x=x, m=m: e.matmul(
                                m.ap, w1[:, x, c, f * P:(f + 1) * P], xt.ap[:, c, :], start=(c == 0), stop=(c == 1)),
                                st["ev"], h_w1[x], m.free)
                        h = pr.op("scalar", "h_relu", lambda e, f=f, x=x, m=m, ht=ht: e.activation(
                            ht.ap[:, f, :], m.ap, ACT.Relu, bias=b1[:, x, f:f + 1]), mm, h_b1, ht.free)
                        m.free = [h]
                        hs.append(h)
                        yield
                    ht.free = []
                    wait.append((x, ht, hs))
                if x >= 1:
                    z, ht, hs = wait.pop(0)
                    for v in range(2):
                        m = rD.take()
                        for i in range(2):
                            for f in range(4):
                                mo = pr.op("tensor", "h_o", lambda e, t=2 * v + i, i=i, f=f, z=z, m=m, ht=ht: e.matmul(
                                    m.ap[:, i * D:(i + 1) * D], ht.ap[:, f, t * P:(t + 1) * P], w2[:, z, f, :],
                                    start=(f == 0), stop=(f == 3)), hs, h_w2[z], m.free)
                        hh = []
                        for i in range(2):
                            t = 2 * v + i
                            hy[t] = pr.op("vector", "h_acc", lambda e, t=t, i=i, z=z, m=m: e.scalar_tensor_tensor(
                                y.ap[:, t, :], m.ap[:, i * D:(i + 1) * D], st["w"].ap[:, t, z:z + 1], y.ap[:, t, :],
                                ALU.mult, ALU.add), mo, st["hw"], hy[t])
                            hh.append(hy[t])
                        m.free = hh
                        yield
                    ht.free = [mo]
            xt.free = [mm]
            st["w"].free = list(hy.values())
            hl = self.ln("h_ln", lnr, [y.ap[:, t, :] for t in range(NT)], [y.ap[:, t, :] for t in range(NT)],
                         [hy[t] for t in range(NT)], [])
            ho = []
            for t in range(NT):
                n = b * NT + t
                r = rr.take()
                hr = pr.dma("sync", f"h_r{n % 2}", r.ap[:, :], self.x1d[n], r.free)
                a = pr.op("gpsimd", "h_ng", lambda e, t=t: e.tensor_tensor(y.ap[:, t, :], y.ap[:, t, :], g2[:, :], ALU.mult),
                          hl[t], h_g2)
                a = pr.op("gpsimd", "h_nb", lambda e, t=t: e.tensor_tensor(y.ap[:, t, :], y.ap[:, t, :], c2[:, :], ALU.add), a, h_c2)
                a = pr.op("gpsimd", "h_res", lambda e, t=t, r=r: e.tensor_tensor(r.ap[:, :], r.ap[:, :], y.ap[:, t, :], ALU.add), a, hr)
                hd = pr.dma("sync", f"h_out{n % 2}", self.out[b, t * P:(t + 1) * P, :], r.ap[:, :], a)
                r.free = [hd]
                ho.append(hd)
                yield
            y.free = [a]
            self.out_done += ho

        self.out_done = []
        for _ in route(0):
            pass
        for b in range(NB):
            streams = [(run(b), 55)]
            if b + 1 < NB:
                streams.append((route(b + 1), 8))
            merge(*streams)
        pr.wait("sync", self.out_done)


def build(nc, ins, out):
    with ExitStack() as ctx:
        k = Kernel(nc, ctx, ins, out)
        k.phase1()
        k.phase2()
        k.phase3()
        k.pr.issue(nc, ctx)


def constants():
    inv = (np.float32(1.0) / np.power(np.float32(10000.0), np.arange(0, 16, 2, dtype=np.float32) / np.float32(16))).astype(np.float32)
    ang = (np.arange(S, dtype=np.float32)[:, None] * inv[None, :]).astype(np.float32).astype(np.float64)
    cos, sin = np.cos(ang).astype(np.float32), np.sin(ang).astype(np.float32)
    cos2 = np.concatenate([cos, cos], 1).reshape(NT, P, 16).transpose(1, 0, 2)
    sin2 = np.concatenate([-sin, sin], 1).reshape(NT, P, 16).transpose(1, 0, 2)
    before = np.tril(np.ones((8, 8), np.float32), -1)
    return {
        "c_ident": np.eye(P, dtype=np.float32),
        "c_cos": np.ascontiguousarray(cos2),
        "c_sin": np.ascontiguousarray(sin2),
        "c_before": np.ascontiguousarray(np.broadcast_to(before, (P, 8, 8))),
    }


def layout(inputs):
    a = {k: np.ascontiguousarray(v) for k, v in inputs.items()}
    col = lambda v, n: np.ascontiguousarray(v.reshape(n, P).T)
    t = {
        "x": a["x"], "fside": a["fside_16xSxS_0"], "cond": a["cond_64"], "mask": a["mask_BxS_bk0"].view(np.int32),
        "g_in": col(a["L0_cond_g_in"], 2), "g_out": col(a["L0_cond_g_out"], 2),
        "null_bias": a["L0_cond_null_attn_bias"], "cond_wq": a["L0_cond_Wq"], "cond_wkv": a["L0_cond_Wkv"],
        "cond_wo": a["L0_cond_Wo"],
        "attn_wq": a["L0_attn_Wq"], "attn_bq": a["L0_attn_bq"], "attn_wdown": a["L0_attn_Wdown"],
        "attn_bdown": a["L0_attn_bdown"], "attn_wup": a["L0_attn_Wup"], "attn_bup": a["L0_attn_bup"],
        "attn_wout": a["L0_attn_Wout"], "attn_bout": a["L0_attn_bout"],
        "condT": np.ascontiguousarray(a["cond_64"].T),
        "moe_wt": np.ascontiguousarray(a["L0_cond2_wt"].T), "moe_wg": np.ascontiguousarray(a["L0_cond2_wg"].T),
        "moe_gate": a["L0_cond2_w_gate"], "moe_up": a["L0_cond2_w_up"], "moe_down": a["L0_cond2_w_down"],
        "sh_gate": a["L0_cond2_sw_gate"], "sh_up": a["L0_cond2_sw_up"], "sh_down": a["L0_cond2_sw_down"],
        "wi": np.ascontiguousarray(a["L0_ffn_in_proj_w"].T), "bi": a["L0_ffn_in_proj_b"],
        "bic": col(a["L0_ffn_in_proj_b"], 6),
        "wo2": np.ascontiguousarray(a["L0_ffn_out_proj_w"].T), "bo2": a["L0_ffn_out_proj_b"],
        "ln1_g": a["L0_ffn_ln1_g"], "ln1_b": a["L0_ffn_ln1_b"], "ln2_g": a["L0_ffn_ln2_g"], "ln2_b": a["L0_ffn_ln2_b"],
        "w_group": a["L0_ffn_w_group"], "b_group": a["L0_ffn_b_group"],
        "w_expert": a["L0_ffn_w_expert"], "b_expert": a["L0_ffn_b_expert"].reshape(8),
        "w1": a["L0_ffn_w1"], "b1c": np.ascontiguousarray(a["L0_ffn_b1"].reshape(8, 4, P).transpose(2, 0, 1)), "w2": a["L0_ffn_w2"], "b2": a["L0_ffn_b2"],
    }
    t.update(constants())
    return t


def kernel(**inputs):
    import concourse.bacc as bacc
    from concourse.bass_utils import run_bass_kernel_spmd

    arrays = layout({k: np.asarray(v) for k, v in inputs.items()})
    nc = bacc.Bacc("TRN2", target_bir_lowering=False, num_devices=1, dynamic_dma_scratch_size=2048)
    ins = {k: nc.dram_tensor("in_" + k, v.shape, mybir.dt.from_np(v.dtype), kind="ExternalInput").ap()
           for k, v in arrays.items()}
    out = nc.dram_tensor("out_y", (NB, S, D), F32, kind="ExternalOutput").ap()
    build(nc, ins, out)
    r = run_bass_kernel_spmd(nc, [{"in_" + k: v for k, v in arrays.items()}], core_ids=[0])
    return r.results[0]["out_y"]
```

```python
from contextlib import ExitStack

import numpy as np

import concourse.bass as bass
from concourse import mybir

F32 = mybir.dt.float32
BF16 = mybir.dt.bfloat16
U8 = mybir.dt.uint8
ALU = mybir.AluOpType
ACT = mybir.ActivationFunctionType
AX = mybir.AxisListType.X

P = 128
NB = 8
S = 512
NT = 4
D = 256
H = 16
DH = 64
EPS = 1e-5
NEG = -1.0e30
ENGINES = ("tensor", "vector", "scalar", "gpsimd", "sync")
CAUSAL = [0, 128, 384, 768, 1280]
KEYCOL = [0, 512, 896, 1152, 1280]
HS_ENG = [("vector", "v"), ("gpsimd", "g"), ("vector", "v"), ("gpsimd", "g")]
HV_ENG = [("gpsimd", "g"), ("gpsimd", "g"), ("gpsimd", "g"), ("gpsimd", "g")]


class Op:

    def __init__(self, eng, sem, emit, after, inc):
        self.eng, self.sem, self.emit, self.after, self.inc = eng, sem, emit, after, inc
        self.needed = inc == 16
        self.value = None
        self.slot = None


class Prog:

    def __init__(self):
        self.queues = {e: [] for e in ENGINES}
        self.phase = 0

    def fence(self):
        last = {}
        for q in self.queues.values():
            for op in q:
                if op.sem is not None and op.phase == self.phase:
                    last[op.sem] = op
        hs = list(last.values())
        for eng in ENGINES:
            self.wait(eng, hs)
        self.phase += 1

    def op(self, eng, sem, emit, *after):
        return self._put(Op(eng, sem, emit, self._flat(after), 1))

    def dma(self, eng, sem, out, in_, *after):
        return self._put(Op(eng, sem, lambda e: e.dma_start(out, in_), self._flat(after), 16))

    def put(self, eng, sem, emit, inc, *after):
        return self._put(Op(eng, sem, emit, self._flat(after), inc))

    def wait(self, eng, *after):
        self._put(Op(eng, None, None, self._flat(after), 0))

    def _put(self, op):
        for a in op.after:
            a.needed = True
        op.phase = self.phase
        self.queues[op.eng].append(op)
        return op

    def _flat(self, xs):
        out = []
        for x in xs:
            if isinstance(x, (list, tuple)):
                out += self._flat(x)
            elif x is not None:
                out.append(x)
        return out

    def issue(self, nc, ctx):
        count, owner, slots = [], {}, {}
        own = []
        for phase in range(self.phase + 1):
            used = 0
            for eng in ENGINES:
                for op in self.queues[eng]:
                    if op.phase != phase or op.sem is None or not op.needed:
                        continue
                    key = (phase, op.sem)
                    assert owner.setdefault(key, eng) == eng, op.sem
                    if key not in slots:
                        if eng == "gpsimd" and op.inc == 16:
                            slots[key] = len(count)
                            own.append(len(count))
                            count.append(0)
                        else:
                            while used in own:
                                used += 1
                            if used == len(count):
                                count.append(0)
                            slots[key] = used
                            used += 1
                    op.slot = slots[key]
                    count[op.slot] += op.inc
                    op.value = count[op.slot]
        sems = [ctx.enter_context(nc.semaphore(f"s{i}")) for i in range(len(count))]
        block = ctx.enter_context(nc.Block())

        def body(queue):
            def run(e):
                seen = {}
                for op in queue:
                    want = {}
                    for a in op.after:
                        if a.value > max(seen.get(a.slot, 0), want.get(a.slot, 0)):
                            want[a.slot] = a.value
                    for slot, value in want.items():
                        e.wait_ge(sems[slot], value)
                        seen[slot] = value
                    if op.emit is not None:
                        ins = op.emit(e)
                        if op.needed:
                            ins.then_inc(sems[op.slot], op.inc)
            return run

        block.tensor(body(self.queues["tensor"]))
        block.vector(body(self.queues["vector"]))
        block.scalar(body(self.queues["scalar"]))
        block.gpsimd(body(self.queues["gpsimd"]))
        block.sync(body(self.queues["sync"]))


class Buf:

    def __init__(self, ap):
        self.ap = ap
        self.held = False
        self._free = []

    @property
    def free(self):
        return self._free

    @free.setter
    def free(self, ops):
        self._free = ops
        self.held = False


class Ring:
    def __init__(self, aps):
        self.bufs = [Buf(a) for a in aps]
        self.n = 0

    def take(self):
        b = self.bufs[self.n % len(self.bufs)]
        self.n += 1
        assert not b.held, "taken again before its last reader was queued"
        b.held = True
        return b


class Arena:
    def __init__(self, nc, start, end):
        self.nc, self.pos, self.end = nc, start, end
        self.high = start

    def __call__(self, name, shape, dt=F32):
        size = int(np.prod(shape[1:])) * mybir.dt.size(dt)
        at = (self.pos + 31) // 32 * 32
        self.pos = at + size
        self.high = max(self.high, self.pos)
        assert self.pos <= self.end, (name, self.pos, self.end)
        return self.nc.alloc_sbuf_tensor_at(name, list(shape), dt, offset=at)


def merge(*streams):
    done = [0] * len(streams)
    total = max(n for _, n in streams)
    for k in range(1, total + 1):
        for i, (g, n) in enumerate(streams):
            while done[i] < n * k // total:
                done[i] += 1
                next(g, None)
    for g, _ in streams:
        for _ in g:
            pass


def weave(*streams):
    done = [0] * len(streams)
    total = max(n for _, n in streams)
    for k in range(1, total + 1):
        for i, (g, n) in enumerate(streams):
            while done[i] < n * k // total:
                done[i] += 1
                next(g, None)
        yield
    for g, _ in streams:
        for _ in g:
            pass


def bc(ap, shape):
    return ap.broadcast_to(list(shape))


class Kernel:
    def __init__(self, nc, ctx, ins, out):
        self.nc, self.ins, self.out = nc, ins, out
        self.pr = Prog()
        self.ps = ctx.enter_context(nc.psum_tensor("ps", [P, 8, 512], F32))
        self.x1d = nc.dram_tensor("x1_scratch", [NB * NT, P, D], F32).ap()
        self.x2d = nc.dram_tensor("x2_scratch", [NB * NT, P, D], F32).ap()
        self.xsd = nc.dram_tensor("xs_scratch", [(NB * NT + 7) * P, D], F32).ap()
        self.lo = nc.sbuf_base
        self.hi = nc.sbuf_usable_end
        sb = Arena(nc, self.lo, self.hi)
        pr = self.pr
        self.ident = sb("ident", [P, P])
        self.mhalf = sb("mhalf", [P, NT])
        self.h_ident = pr.dma("sync", "ident", self.ident[:, :], ins["c_ident"])
        self.h_mhalf = pr.op("gpsimd", "mhalf", lambda e: e.memset(self.mhalf[:, :], -0.5))
        self.base = sb.pos

    def clear_slots(self, zero):
        hz = self.pr.op("gpsimd", "zero", lambda e: e.memset(zero[:, :], 0.0))
        n = NB * NT + 7
        self.zeroed = [self.pr.dma("sync", "zeroed", self.xsd.rearrange("(n p) d -> p n d", p=P),
                                   zero[:, :].unsqueeze(1).broadcast_to([P, n, D]), hz)]

    def banks(self, *ks):
        return Ring([self.ps[:, k, :] for k in ks])

    def load(self, eng, sem, dst, src, *after):
        return self.pr.dma(eng, sem, dst, src, *after)

    def ln_make(self, sb, tag, n):
        return Ring([dict(st=sb(f"{tag}st{i}", [P, NT, 6]), mv=sb(f"{tag}mv{i}", [P, NT, 2]),
                          ve=sb(f"{tag}ve{i}", [P, NT]), rs=sb(f"{tag}rs{i}", [P, NT])) for i in range(n)])

    def ln(self, tag, ring, srcs, outs, src_ready, out_free, later=False):
        pr, b = self.pr, ring.take()
        t, n = b.ap, len(srcs)
        hs = []
        for i, s in enumerate(srcs):
            hs.append(pr.op("vector", tag + "_st", lambda e, i=i, s=s: e.bn_stats(t["st"][:, i, :], s),
                            src_ready[i], b.free))
        ha = []
        for i in range(n):
            ha.append(pr.op("vector", tag + "_ag", lambda e, i=i: e.bn_aggr(t["mv"][:, i, :], t["st"][:, i, :]),
                            hs[i], b.free))
        hv = pr.op("vector", tag + "_ve",
                   lambda e: e.tensor_scalar(t["ve"][:, 0:n], t["mv"][:, 0:n, 1], EPS, None, ALU.add), ha, b.free)
        hp = pr.op("gpsimd", tag + "_rs",
                   lambda e: e.tensor_tensor(t["rs"][:, 0:n], t["ve"][:, 0:n], self.mhalf[:, 0:n], ALU.pow),
                   hv, self.h_mhalf, b.free)

        def scale():
            out = []
            for i in range(n):
                out.append(pr.op("vector", tag + "_xn",
                                 lambda e, i=i: e.tensor_scalar(outs[i], srcs[i], t["mv"][:, i, 0:1], t["rs"][:, i:i + 1],
                                                                ALU.subtract, ALU.mult),
                                 hp, out_free))
            b.free = [out[-1]]
            return out

        return scale if later else scale()

    def phase1(self):
        nc, pr, ins, ps = self.nc, self.pr, self.ins, self.ps
        sb = Arena(nc, self.base, self.hi)
        W = {}

        def weight(name, shape, src, eng="sync", dt=F32):
            t = sb("w_" + name, shape, dt)
            v = t[tuple(slice(None) for _ in shape)]
            W[name] = t
            return pr.dma(eng, "w_" + name, v, src)

        xin = Buf(sb("xin", [P, NT, D]))
        xv = ins["x"].rearrange("b (t p) d -> b p t d", p=P)
        h_x = {0: pr.dma("sync", "xin", xin.ap[:, :, :], xv[0])}
        h_gin = weight("gin", [P, 2], ins["g_in"])
        h_wq = weight("wq", [P, 2, 1024], ins["cond_wq"].rearrange("(c p) n -> p c n", p=P))
        wk = sb("w_wk", [P, 2, 2, DH])
        wkv = ins["cond_wkv"].rearrange("(c p) n -> p c n", p=P)
        h_wk = [pr.dma("sync", f"w_wk{j}", wk[:, :, j, :], wkv[:, :, 0:DH]) for j in range(2)]
        h_wv = weight("wv", [P, 2, DH], wkv[:, :, DH:2 * DH])
        h_nk = weight("nk", [P, DH], ins["cond"][0:1, :].broadcast_to([P, DH]))
        h_nb = weight("nb", [P, NT, H], ins["null_bias"].rearrange("(o n h) -> o n h", o=1, n=1).broadcast_to([P, NT, H]))
        nv = sb("w_nv", [P, 1])
        nvc = ins["cond"][1:2, :].rearrange("a d -> d a")
        h_nv = [pr.dma("sync", f"w_nv{j}", nv[DH * j:DH * j + DH, :], nvc) for j in range(2)]
        mrow = Ring([sb(f"mrow{i}", [1, S], U8) for i in range(2)])
        bias = sb("bias", [P, H, 1280])
        fv = ins["fside"].rearrange("h (t p) k -> t p h k", p=P)
        h_bias, h_bd = [], []
        for g in range(8):
            h_bd.append([pr.dma("scalar", f"bias{g}_{t}", bias[:, 2 * g:2 * g + 2, CAUSAL[t]:CAUSAL[t + 1]],
                                fv[t][:, 2 * g:2 * g + 2, 0:P * (t + 1)]) for t in range(NT)])

        def causal(g):
            hh = []
            for t in range(NT):
                diag = bias[:, 2 * g:2 * g + 2, CAUSAL[t] + P * t:CAUSAL[t + 1]]
                hh.append(pr.op("gpsimd", "causal",
                                lambda e, d=diag: e.affine_select(out=d, in_=d, compare_op=ALU.is_ge, fill=NEG, base=0,
                                                                  pattern=[[0, 2], [-1, P]], channel_multiplier=1),
                                h_bd[g][t]))
            h_bias.append(hh)

        h_wo = weight("wo", [P, 8, D], ins["cond_wo"].rearrange("(c p) n -> p c n", p=P))
        h_gout = weight("gout", [P, 2], ins["g_out"])
        h_awq = weight("awq", [P, 2, D], ins["attn_wq"].rearrange("(c p) n -> p c n", p=P))
        h_bq = weight("bq", [P, D], ins["attn_bq"].rearrange("(o n) -> o n", o=1).broadcast_to([P, D]))
        h_wd = weight("wd", [P, 2, DH], ins["attn_wdown"].rearrange("(c p) n -> p c n", p=P))
        h_bdn = weight("bd", [DH, 1], ins["attn_bdown"].rearrange("(n o) -> n o", o=1))
        wup = sb("w_wup", [DH + 1, 512])
        h_wup = [pr.dma("sync", "w_wup0", wup[0:DH, :], ins["attn_wup"]),
                 pr.dma("sync", "w_wup1", wup[DH:DH + 1, :], ins["attn_bup"].rearrange("(o n) -> o n", o=1))]
        h_wout = weight("wout", [P, 2, D], ins["attn_wout"].rearrange("(c p) n -> p c n", p=P))
        h_bout = weight("bout", [P, D], ins["attn_bout"].rearrange("(o n) -> o n", o=1).broadcast_to([P, D]))
        h_cos = weight("cos", [P, NT, 16], ins["c_cos"])
        h_sin = weight("sin", [P, NT, 16], ins["c_sin"])

        maskm = Ring([sb(f"maskm{i}", [P, S], BF16) for i in range(2)])
        onesm = sb("onesm", [P, P], BF16)
        for i, m in enumerate(maskm.bufs):
            m.free = [pr.op("vector", "maskm0", lambda e, m=m: e.memset(m.ap[:, :], 0.0))]
        h_om0 = pr.op("vector", "onesm0", lambda e: e.memset(onesm[:, :], 0.0))
        h_ones = pr.op("vector", "onesm", lambda e: e.memset(onesm[0:1, :], 1.0), h_om0)

        tmpA = sb("prod", [P, 3072])
        wnull = sb("wnull", [P, 2, H])
        nvb = sb("nvb", [P, 8, H])
        nvwo = sb("nvwo", [H, D])
        h_wnull, h_nvwo = [], []

        zero = sb("zero", [P, D])
        xnTs = Ring([sb(f"xnT{i}", [P, 2, S]) for i in range(2)])
        qring = Ring([sb(f"qT{i}", [P, S]) for i in range(4)])
        oring = Ring([sb(f"oTT{i}", [P, S]) for i in range(2)])
        kz = Ring([sb(f"kz{i}", [P, S]) for i in range(2)])
        vt = Ring([sb(f"vt{i}", [P, NT, DH]) for i in range(2)])
        snl = Ring([sb(f"snl{i}", [P, NT, H]) for i in range(2)])
        pbuf = Ring([sb(f"pb{i}", [P, 1280]) for i in range(4)])
        ptb = Ring([sb(f"ptb{i}", [P, 1280]) for i in range(2)])
        mst = Ring([sb(f"mst{i}", [P, 6, 2, NT]) for i in range(4)])
        pnns = Ring([sb(f"pnn{i}", [P, NT, H]) for i in range(2)])
        pnT = Buf(sb("pnT", [H, S]))
        hnb = Buf(sb("hn", [P, NT, D]))
        hT = Buf(sb("hT", [P, 2, S]))
        latT = Buf(sb("latT", [DH + 1, S]))
        qs = Ring([sb(f"qs{i}", [P, D]) for i in range(2)])
        kvs = Ring([sb(f"kvs{i}", [P, H, 32]) for i in range(3)])
        rp = Ring([sb(f"rp{i}", [P, 2, D]) for i in range(2)])
        rt = Buf(sb("rt", [P, D]))
        sc = Ring([sb(f"sc{i}", [P, D]) for i in range(2)])
        sm = Ring([sb(f"sm{i}", [P, 3, H]) for i in range(2)])
        ob = Ring([sb(f"ob{i}", [P, D]) for i in range(2)])
        oT = Ring([sb(f"oT{i}", [P, 2, P]) for i in range(2)])
        xr = Ring([sb(f"xr{i}", [P, D]) for i in range(2)])
        prod = Ring([tmpA[:, i * 1024:(i + 1) * 1024] for i in range(3)])
        lnx = self.ln_make(sb, "lnx", 1)
        lno = self.ln_make(sb, "lno", 2)
        self.high1 = sb.high
        h_latones = pr.op("vector", "latones", lambda e: e.memset(latT.ap[DH:DH + 1, :], 1.0))

        rS = self.banks(0, 1)
        rT = self.banks(2, 3)
        rM = rO = self.banks(4, 7)
        acc = [Buf(ps[:, k, :]) for k in (5, 6)]
        self.ident_ready = self.h_ident
        state = {}
        flip = [0]

        def fold_key():
            for c in range(2):
                t3 = tmpA[:, c * 1024:(c + 1) * 1024].rearrange("p (h d) -> p h d", h=H)
                q3 = W["wq"][:, c, :].rearrange("p (h d) -> p h d", h=H)
                a = pr.op("vector", "wn0", lambda e, t3=t3, q3=q3: e.tensor_tensor(
                    t3, q3, W["nk"][:, :].unsqueeze(1).broadcast_to([P, H, DH]), ALU.mult), h_wq, h_nk)
                b = pr.op("vector", "wn1", lambda e, t3=t3, c=c: e.tensor_reduce(wnull[:, c, :], t3, AX, ALU.add), a)
                h_wnull.append(pr.op("vector", "wn2", lambda e, c=c: e.tensor_scalar(wnull[:, c, :], wnull[:, c, :], 0.125, None,
                                                                                ALU.mult), b))

        def fold_value():
            h0 = pr.op("vector", "nvb0", lambda e: e.memset(nvb[:, :, :], 0.0))
            hb = []
            for c in range(8):
                for j in range(2):
                    hb.append(pr.op("vector", "nvb", lambda e, c=c, j=j: e.tensor_copy(
                        nvb[DH * j:DH * j + DH, c, 2 * c + j:2 * c + j + 1], nv[DH * j:DH * j + DH, :]), h0, h_nv))
            m = rM.take()
            for c in range(8):
                mm = pr.op("tensor", "nvwo_mm", lambda e, c=c: e.matmul(m.ap[0:H, 0:D], nvb[:, c, :], W["wo"][:, c, :],
                                                                        start=(c == 0), stop=(c == 7)), hb, h_wo, m.free)
            h = pr.op("vector", "nvwo", lambda e: e.tensor_copy(nvwo[:, :], m.ap[0:H, 0:D]), mm)
            m.free = [h]
            h_nvwo.append(h)

        def copy_out(sem, out, in_, *after, again=False):
            flip[0] += 0 if again else 1
            if flip[0] % 2:
                return pr.op("vector", sem + "_v", lambda e: e.tensor_copy(out, in_), *after)
            return pr.op("scalar", sem + "_a", lambda e: e.activation(out, in_, ACT.Copy), *after)

        def stage_pre(b):
            st = state[b] = {}
            x = xin.ap
            hx = h_x[b]
            scale = self.ln("lnx", lnx, [x[:, t, :] for t in range(NT)], [x[:, t, :] for t in range(NT)], [hx] * NT, [], later=True)
            yield
            hxn = scale()
            yield
            ev = []
            tr_all = []
            xnT = st["xnT"] = xnTs.take()
            for c in range(2):
                m = rM.take()
                tr = None
                for t in range(NT):
                    tr = pr.op("tensor", "xT", lambda e, c=c, t=t, m=m: e.transpose(
                        m.ap[:, t * P:(t + 1) * P], x[:, t, c * P:(c + 1) * P], self.ident[:, :]),
                        hxn[t], self.h_ident, m.free)
                tr_all.append(tr)
                h = pr.op("scalar", "xnT", lambda e, c=c, m=m: e.activation(
                    xnT.ap[:, c, :], m.ap, ACT.Identity, scale=W["gin"][:, c:c + 1]), tr, h_gin, xnT.free)
                m.free = [h]
                ev.append(h)
                yield
            if b + 1 < NB:
                h_x[b + 1] = pr.dma("sync", "xin", xin.ap[:, :, :], xv[b + 1], tr_all)
            users = []
            i = mrow.n % 2
            m8, mk = mrow.take(), maskm.take()
            hm8 = pr.dma("sync", f"mrow{i}", m8.ap[:, :], ins["mask"][b:b + 1, :].bitcast(U8), m8.free)
            hmk = pr.op("vector", "maskm", lambda e, mk=mk, m8=m8: e.tensor_scalar(
                mk.ap[0:1, :], m8.ap[:, :], 1.0, -NEG, ALU.subtract, ALU.mult), hm8, mk.free)
            m8.free = [hmk]
            st["mk"], st["hmk"] = mk, hmk
            m = rM.take()
            for c in range(2):
                mm = pr.op("tensor", "kmm", lambda e, c=c, m=m: e.matmul(
                    m.ap, wk[:, c, :, :], xnT.ap[:, c, :], start=(c == 0), stop=(c == 1)), ev, h_wk, m.free)
            users.append(mm)
            k = kz.take()
            hk = [pr.op("scalar", "kcp", lambda e, m=m, k=k: e.activation(k.ap[:, :], m.ap, ACT.Copy), mm, k.free)]
            m.free = hk
            st["k"], st["hk"] = k, hk
            yield
            m = rM.take()
            for t in range(NT):
                for c in range(2):
                    mm = pr.op("tensor", "vmm", lambda e, c=c, t=t, m=m: e.matmul(
                        m.ap[:, t * DH:(t + 1) * DH], xnT.ap[:, c, t * P:(t + 1) * P], W["wv"][:, c, :],
                        start=(c == 0), stop=(c == 1)), ev, h_wv, m.free)
                for c in range(2):
                    mm = pr.op("tensor", "vmm", lambda e, c=c, t=t, m=m: e.matmul(
                        m.ap[:, 256 + t * H:256 + (t + 1) * H], xnT.ap[:, c, t * P:(t + 1) * P], wnull[:, c, :],
                        start=(c == 0), stop=(c == 1)), h_wnull)
            users.append(mm)
            v, sn = vt.take(), snl.take()
            hv = pr.op("vector", "vcp", lambda e, m=m, v=v: e.tensor_copy(v.ap[:, :, :], m.ap[:, 0:256]), mm, v.free)
            hs = pr.op("vector", "snl", lambda e, m=m, sn=sn: e.tensor_tensor(
                sn.ap[:, :, :], m.ap[:, 256:256 + NT * H], W["nb"][:, :, :], ALU.add), mm, h_nb, sn.free)
            m.free = [hv, hs]
            st["v"], st["hv"], st["sn"], st["hs"] = v, hv, sn, hs
            yield
            st["ev"], st["q"], st["hq"], st["users"] = ev, [], [], users
            st["pnn"], st["hpnn"], st["kuse"], st["snuse"] = pnns.take(), [], [], []

        def queries(b, p):
            st = state[b]
            xnT, q = st["xnT"], qring.take()
            st["q"].append(q)
            m = rM.take()
            for c in range(2):
                mm = pr.op("tensor", "qmm", lambda e, c=c: e.matmul(
                    m.ap, W["wq"][:, c, p * P:(p + 1) * P], xnT.ap[:, c, :], start=(c == 0), stop=(c == 1)),
                    st["ev"], h_wq, m.free)
            flip[0] += 1
            if flip[0] % 2:
                h = pr.op("vector", "qcp_v", lambda e: e.tensor_scalar(
                    q.ap[:, :], m.ap, 0.125, None, ALU.mult), mm, q.free)
            else:
                h = pr.op("scalar", "qcp_a", lambda e: e.activation(
                    q.ap[:, :], m.ap, ACT.Copy, scale=0.125), mm, q.free)
            m.free = [h]
            st["hq"].append(h)
            if p == 7:
                xnT.free = st["users"] + [mm]

        def scores(b, h):
            st = state[b]
            p, j = h // 2, h % 2
            if j == 0:
                st["ms", p] = mst.take()
            ms = st["ms", p]
            mx, nm, dn, pn, rs, rc = [ms.ap[:, i, :, :] for i in range(6)]
            pb = pbuf.take()
            k, sn, q = st["k"], st["sn"], st["q"][p]
            hm = []
            for t in range(NT):
                n = P * (t + 1)
                m = rS.take()
                pr.op("tensor", "S", lambda e, t=t, n=n, m=m: e.matmul(
                    m.ap[:, 0:n], q.ap[DH * j:DH * j + DH, t * P:(t + 1) * P], k.ap[DH * j:DH * j + DH, 0:n],
                    start=True, stop=False),
                    st["hq"][p], st["hk"], m.free)
                mm = pr.op("tensor", "S", lambda e, n=n, m=m: e.matmul(
                    m.ap[:, 0:n], onesm[:, :], st["mk"].ap[:, 0:n], start=False, stop=True), st["hmk"], h_ones)
                hh = pr.op("vector", "ttr", lambda e, t=t, n=n, m=m: e.tensor_tensor_reduce(
                    pb.ap[:, CAUSAL[t]:CAUSAL[t + 1]], m.ap[:, 0:n], bias[:, h, CAUSAL[t]:CAUSAL[t + 1]],
                    1.0, sn.ap[:, t, h:h + 1], ALU.add, ALU.max, mx[:, j, t:t + 1]),
                    mm, h_bias[h // 2], st["hs"], pb.free, ms.free)
                m.free = [hh]
                hm.append(hh)
            if j == 1:
                q.free = [mm]
            if h == H - 1:
                k.free, st["mk"].free = [mm], [mm]
            hn_ = pr.op("vector", "nm", lambda e: e.tensor_scalar(nm[:, j, :], mx[:, j, :], -1.0, None, ALU.mult), hm, ms.free)
            hd = pr.op("vector", "dn", lambda e: e.tensor_tensor(dn[:, j, :], sn.ap[:, :, h], nm[:, j, :], ALU.add), hn_, ms.free)
            if h == H - 1:
                sn.free = [hd]
            he = [pr.op("scalar", "exp", lambda e, t=t: e.activation(
                pb.ap[:, CAUSAL[t]:CAUSAL[t + 1]], pb.ap[:, CAUSAL[t]:CAUSAL[t + 1]], ACT.Exp,
                bias=nm[:, j, t:t + 1], accum_out=rs[:, j, t:t + 1]), hm, hn_, ms.free) for t in range(NT)]
            hp = pr.op("scalar", "pn", lambda e: e.activation(pn[:, j, :], dn[:, j, :], ACT.Exp), hd, ms.free)
            st["P", h] = (pb, he, hp)

        def normal(b, h):
            st = state[b]
            p, j = h // 2, h % 2
            ms = st["ms", p]
            mx, nm, dn, pn, rs, rc = [ms.ap[:, i, :, :] for i in range(6)]
            pb, he, hp = st["P", h]
            h1 = pr.op("vector", "den", lambda e: e.tensor_tensor(dn[:, j, :], rs[:, j, :], pn[:, j, :], ALU.add), he, hp)
            h2 = pr.op("vector", "rden", lambda e: e.reciprocal(rc[:, j, :], dn[:, j, :]), h1, ms.free if j == 0 else [])
            h3 = pr.op("vector", "pnn", lambda e: e.tensor_tensor(st["pnn"].ap[:, :, h], pn[:, j, :], rc[:, j, :], ALU.mult),
                       h2, st["pnn"].free)
            st["hpnn"].append(h3)
            hg = [pr.op("scalar", "pnorm", lambda e, t=t: e.activation(
                pb.ap[:, CAUSAL[t]:CAUSAL[t + 1]], pb.ap[:, CAUSAL[t]:CAUSAL[t + 1]], ACT.Identity,
                scale=rc[:, j, t:t + 1]), h2) for t in range(NT)]
            st["hg", h] = hg
            if j == 1:
                ms.free = [st["h3", p], h3, st["hg", h - 1], hg]
            else:
                st["h3", p] = h3

        def turn(b, h):
            st = state[b]
            pb = st["P", h][0]
            hg = st["hg", h]
            pt = ptb.take()
            out = []
            tr = None
            for lot in ([(0, t) for t in range(4)], [(1, t) for t in range(1, 4)] + [(3, 3)], [(2, 2), (2, 3)]):
                m = rT.take()
                for i, (kt, t) in enumerate(lot):
                    tr = pr.op("tensor", "PT", lambda e, i=i, kt=kt, t=t, m=m: e.transpose(
                        m.ap[:, i * P:(i + 1) * P], pb.ap[:, CAUSAL[t] + kt * P:CAUSAL[t] + (kt + 1) * P],
                        self.ident[:, :]), hg[t], self.h_ident, m.free)
                kt0, t0 = lot[0]
                n0 = len([1 for kt, _ in lot if kt == kt0]) * P
                ho = [copy_out("ptc", pt.ap[:, KEYCOL[kt0]:KEYCOL[kt0] + n0], m.ap[:, 0:n0], tr, pt.free)]
                if n0 < len(lot) * P:
                    ho.append(copy_out("ptc", pt.ap[:, KEYCOL[3]:KEYCOL[4]], m.ap[:, n0:n0 + P], tr, pt.free, again=True))
                m.free = ho
                out += ho
                yield
            pb.free = [tr]
            st["PT", h] = (pt, out)

        def values(b, p):
            st = state[b]
            m = rO.take()
            v = st["v"]
            mm = None
            last = []
            for kt in range(NT):
                for j in range(2):
                    pt, hp = st["PT", 2 * p + j]
                    mm = pr.op("tensor", "O", lambda e, kt=kt, j=j, pt=pt, m=m: e.matmul(
                        m.ap[DH * j:DH * j + DH, kt * P:S], v.ap[:, kt, :], pt.ap[:, KEYCOL[kt]:KEYCOL[kt + 1]],
                        start=(kt == 0), stop=(kt == NT - 1), tile_position=(0, DH * j)), hp, st["hv"], m.free)
            for j in range(2):
                st["PT", 2 * p + j][0].free = [mm]
            if p == 7:
                v.free = [mm]
            o = oring.take()
            h = copy_out("oc", o.ap[:, :], m.ap, mm, o.free)
            m.free = [h]
            st["O", p] = (o, h)

        def project(b, p):
            o, h = state[b]["O", p]
            for t in range(NT):
                a = acc[t // 2]
                mm = pr.op("tensor", "wo", lambda e, t=t, a=a: e.matmul(
                    a.ap[:, t % 2 * D:(t % 2 + 1) * D], o.ap[:, t * P:(t + 1) * P], W["wo"][:, p, :],
                    start=(p == 0 and t % 2 == 0), stop=False, skip_group_check=True), h, h_wo, a.free)
            o.free = [mm]

        def finish(b):
            st = state[b]
            pnn = st["pnn"]
            m = rM.take()
            for t in range(NT):
                tr = pr.op("tensor", "pnT_t", lambda e, t=t: e.transpose(
                    m.ap[0:H, t * P:(t + 1) * P], pnn.ap[:, t, :], self.ident[:, :]), st["hpnn"], m.free)
            pnn.free = [tr]
            hp = pr.op("vector", "pnT", lambda e: e.tensor_copy(pnT.ap[:, :], m.ap[0:H, :]), tr, pnT.free)
            m.free = [hp]
            yield
            st["hn"], scale = [], []
            for u in range(2):
                a = acc[u]
                for i in range(2):
                    mm = pr.op("tensor", "wo", lambda e, t=2 * u + i, i=i, a=a: e.matmul(
                        a.ap[:, i * D:(i + 1) * D], pnT.ap[:, t * P:(t + 1) * P], nvwo[:, :], start=False, stop=True,
                        skip_group_check=True), hp, h_nvwo)
                scale.append(self.ln("lno", lno, [a.ap[:, 0:D], a.ap[:, D:2 * D]],
                                     [hnb.ap[:, 2 * u, :], hnb.ap[:, 2 * u + 1, :]], [mm, mm], hnb.free, later=True))
                yield
            for u in range(2):
                acc[u].free = scale[u]()
                st["hn"] += acc[u].free
                yield
            pnT.free = [mm]

        def step(n):
            at = lambda k: (k // H, k % H)
            if n < H // 2:
                causal(n)
            if n < NB * H:
                scores(*at(n))
            yield
            if n % 2 == 0 and n + 4 < NB * H:
                b, h = at(n + 4)
                queries(b, h // 2)
            yield
            if 1 <= n <= NB * H:
                normal(*at(n - 1))
            yield
            if n % 2 == 1 and n >= 5 and n - 4 < NB * H:
                b, h = at(n - 4)
                values(b, h // 2)
            if n % 2 == 0 and n >= 6 and n - 5 < NB * H:
                b, h = at(n - 5)
                project(b, h // 2)
                if h == H - 1:
                    yield from finish(b)
            yield
            if 3 <= n and n - 3 < NB * H:
                yield from turn(*at(n - 3))

        def stage_heads(b):
            st = state[b]
            ev, trs = [], []
            for c in range(2):
                m = rM.take()
                for t in range(NT):
                    tr = pr.op("tensor", "hT_t", lambda e, c=c, t=t, m=m: e.transpose(
                        m.ap[:, t * P:(t + 1) * P], hnb.ap[:, t, c * P:(c + 1) * P], self.ident[:, :]), st["hn"], m.free)
                h = pr.op("scalar", "hT", lambda e, c=c, m=m: e.activation(
                    hT.ap[:, c, :], m.ap, ACT.Identity, scale=W["gout"][:, c:c + 1]), tr, h_gout, hT.free)
                m.free = [h]
                ev.append(h)
                yield
            hnb.free = [tr]
            m = rM.take()
            for c in range(2):
                mm = pr.op("tensor", "lat", lambda e, c=c, m=m: e.matmul(
                    m.ap[0:DH, :], W["wd"][:, c, :], hT.ap[:, c, :], start=(c == 0), stop=(c == 1)), ev, h_wd, m.free)
            hl = pr.op("scalar", "latT", lambda e, m=m: e.activation(
                latT.ap[0:DH, :], m.ap[0:DH, :], ACT.Identity, bias=W["bd"][:, :]), mm, h_bdn, latT.free)
            m.free = [hl]
            yield
            ho = []
            W_ = {}

            def front(t):
                m = rM.take()
                for c in range(2):
                    mq = pr.op("tensor", "q2", lambda e, c=c: e.matmul(
                        m.ap[:, 0:D], hT.ap[:, c, t * P:(t + 1) * P], W["awq"][:, c, :], start=(c == 0), stop=(c == 1)),
                        ev, h_awq, m.free)
                q = qs.take()
                hq = pr.op("vector", "q2b", lambda e, m=m: e.tensor_tensor(
                    q.ap[:, :], m.ap[:, 0:D], W["bq"][:, :], ALU.add), mq, h_bq, q.free)
                m.free = [hq]
                yield
                m2 = rM.take()
                mk = pr.op("tensor", "kv2", lambda e: e.matmul(
                    m2.ap, latT.ap[:, t * P:(t + 1) * P], wup[:, :], start=True, stop=True), hl, h_latones, h_wup, m2.free)
                kv = kvs.take()
                hkv = pr.op("scalar", "kv2c", lambda e: e.activation(kv.ap[:, :, :], m2.ap, ACT.Copy), mk, kv.free)
                m2.free = [hkv]
                W_["mq"], W_["mk"] = mq, mk
                yield
                r = rp.take()
                cosb = W["cos"][:, t, :].unsqueeze(1).broadcast_to([P, H, 16])
                sin = W["sin"][:, t, :]
                rot = []
                t2 = rt.ap[:, :].rearrange("p (h d) -> p h d", h=H)
                for i, (src, ready) in enumerate(((q.ap[:, :].rearrange("p (h d) -> p h d", h=H), hq),
                                                  (kv.ap[:, :, 0:16], hkv))):
                    t1 = r.ap[:, i, :].rearrange("p (h d) -> p h d", h=H)
                    a = pr.op("gpsimd", "rot1", lambda e, t1=t1, src=src: e.tensor_tensor(t1, src, cosb, ALU.mult),
                              ready, h_cos, r.free)
                    bb = [pr.op("gpsimd", "rot2", lambda e, src=src, u=u: e.tensor_tensor(
                        t2[:, :, 8 * u:8 * u + 8], src[:, :, 8 - 8 * u:16 - 8 * u],
                        sin[:, 8 * u:8 * u + 8].unsqueeze(1).broadcast_to([P, H, 8]), ALU.mult),
                        ready, h_sin, rt.free) for u in range(2)]
                    rot.append(pr.op("gpsimd", "rot3", lambda e, t1=t1: e.tensor_tensor(t1, t1, t2, ALU.add), a, bb))
                    rt.free = [rot[-1]]
                    yield
                q.free, r.free, kv.free = [rot[0]], [], [rot[1]]
                W_[t] = dict(kv=kv, hkv=hkv, r=r, rot=rot)

            def middle(t):
                w = W_[t]
                kv, hkv, r, rot = w["kv"], w["hkv"], w["r"], w["rot"]
                q3 = r.ap[:, 0, :].rearrange("p (h d) -> p h d", h=H)
                k3 = r.ap[:, 1, :].rearrange("p (h d) -> p h d", h=H)
                s, mm_ = sc.take(), sm.take()
                s3 = s.ap[:, :].rearrange("p (h g) -> p h g", h=H)
                hr, late = [], None
                for u in range(4):
                    pv = prod.take()
                    pva = pv.ap.rearrange("p (h g d) -> p h g d", h=4, g=H)
                    eng, sem = HS_ENG[u]
                    hm = pr.op(eng, "hs_m" + sem, lambda e, u=u, pva=pva: e.tensor_tensor(
                        pva, q3[:, 4 * u:4 * u + 4, :].unsqueeze(2).broadcast_to([P, 4, H, 16]),
                        k3.unsqueeze(1).broadcast_to([P, 4, H, 16]), ALU.mult), rot, pv.free)
                    r.free.append(hm)

                    def reduce(u=u, pv=pv, pva=pva, hm=hm):
                        hr.append(pr.op("vector", "hs_r", lambda e: e.tensor_reduce(
                            s3[:, 4 * u:4 * u + 4, :], pva, AX, ALU.add), hm, s.free))
                        pv.free = [hr[-1]]

                    if late:
                        late()
                    late = reduce
                    yield
                late()
                a = pr.op("vector", "hs_x", lambda e: e.tensor_reduce(mm_.ap[:, 0, :], s3, AX, ALU.max), hr, mm_.free)
                a = pr.op("vector", "hs_d", lambda e: e.tensor_tensor(
                    s3, s3, mm_.ap[:, 0, :].unsqueeze(2).broadcast_to([P, H, H]), ALU.subtract), a)
                he = pr.op("scalar", "hs_e", lambda e: e.activation(s.ap[:, :], s.ap[:, :], ACT.Exp, scale=0.25), a)
                yield
                a = pr.op("vector", "hs_s", lambda e: e.tensor_reduce(mm_.ap[:, 1, :], s3, AX, ALU.add), he, mm_.free)
                hrc = pr.op("vector", "hs_c", lambda e: e.reciprocal(mm_.ap[:, 2, :], mm_.ap[:, 1, :]), a, mm_.free)
                yield
                v3 = kv.ap[:, :, 16:32].rearrange("p g d -> p d g")
                o = ob.take()
                o3 = o.ap[:, :].rearrange("p (h d) -> p h d", h=H)
                hr, late = [], None
                s.free = [a]
                for u in range(4):
                    pg = prod.take()
                    pga = pg.ap.rearrange("p (h d g) -> p h d g", h=4, g=H)
                    eng, sem = HV_ENG[u]
                    hm = pr.op(eng, "hv_m" + sem, lambda e, u=u, pga=pga: e.tensor_tensor(
                        pga, s3[:, 4 * u:4 * u + 4, :].unsqueeze(2).broadcast_to([P, 4, 16, H]),
                        v3.unsqueeze(1).broadcast_to([P, 4, 16, H]), ALU.mult), he, hkv, pg.free)
                    s.free.append(hm)
                    kv.free.append(hm)

                    def reduce(u=u, pg=pg, pga=pga, hm=hm):
                        hr.append(pr.op("vector", "hv_r", lambda e: e.tensor_reduce(
                            o3[:, 4 * u:4 * u + 4, :], pga, AX, ALU.add), hm, o.free))
                        pg.free = [hr[-1]]

                    if late:
                        late()
                    late = reduce
                    yield
                late()
                hn_ = pr.op("vector", "hv_n", lambda e: e.tensor_tensor(
                    o3, o3, mm_.ap[:, 2, :].unsqueeze(2).broadcast_to([P, H, 16]), ALU.mult), hr, hrc)
                mm_.free = [hn_]
                o.free = []
                w["o"], w["hn"] = o, hn_

            def back(t):
                w = W_[t]
                o, hn_ = w["o"], w["hn"]
                m = rM.take()
                for c in range(2):
                    tr = pr.op("tensor", "oT_t", lambda e, c=c: e.transpose(
                        m.ap[:, c * P:(c + 1) * P], o.ap[:, c * P:(c + 1) * P], self.ident[:, :]), hn_, m.free)
                o.free = [tr]
                ot = oT.take()
                hc = pr.op("scalar", "oT", lambda e, m=m: e.activation(
                    ot.ap[:, :, :], m.ap[:, 0:D].rearrange("p (c k) -> p c k", c=2), ACT.Copy), tr, ot.free)
                m.free = [hc]
                xb = xr.take()
                i = b * NT + t
                hx = pr.dma("sync", f"xr{i % 2}", xb.ap[:, :], ins["x"][b, t * P:(t + 1) * P, :], xb.free)
                hx = pr.op("gpsimd", "xb", lambda e: e.tensor_tensor(xb.ap[:, :], xb.ap[:, :], W["bout"][:, :], ALU.add),
                           hx, h_bout)
                yield
                yield
                m2 = rM.take()
                for c in range(2):
                    mm = pr.op("tensor", "wout", lambda e, c=c: e.matmul(
                        m2.ap[:, 0:D], ot.ap[:, c, :], W["wout"][:, c, :], start=(c == 0), stop=(c == 1)),
                        hc, h_wout, m2.free)
                ot.free = [mm]
                h1 = pr.op("vector", "x1", lambda e: e.tensor_tensor(
                    xb.ap[:, :], m2.ap[:, 0:D], xb.ap[:, :], ALU.add), mm, hx)
                m2.free = [h1]
                hd = pr.dma("sync", f"x1d{i % 2}", self.x1d[i], xb.ap[:, :], h1)
                xb.free = [hd]
                ho.append(hd)
                yield

            for i in range(NT + 2):
                parts = []
                if i >= 2:
                    parts.append((back(i - 2), 3))
                if i < NT:
                    parts.append((front(i), 4))
                if 1 <= i <= NT:
                    parts.append((middle(i - 1), 11))
                yield from weave(*parts)
            mq, mk = W_["mq"], W_["mk"]
            hT.free = [mq]
            latT.free = [mk]
            self.x1_done[b] = ho

        self.x1_done = {}
        self.clear_slots(zero)
        first = stage_pre(0)
        next(first)
        next(first)
        fold_key()
        for _ in first:
            pass
        fold_value()
        queries(0, 0)
        queries(0, 1)
        side, heads = [], None
        for n in range(NB * H + 6):
            if n % H == 1 and n // H + 1 < NB:
                side.append([stage_pre(n // H + 1), 0.14, 0.0])
            if n >= H + 5 and (n - 5) % H == 0:
                for _ in heads[0] if heads else ():
                    pass
                heads = [stage_heads((n - 5) // H - 1), 0.48, 0.0]
                side.append(heads)
            for _ in step(n):
                for x in side:
                    x[2] += x[1]
                    while x[2] >= 1.0:
                        x[2] -= 1.0
                        next(x[0], None)
        for _ in heads[0]:
            pass

    def delayed(self, stage, b, n):
        for _ in range(n):
            yield
        yield from stage(b)

    def row(self, v):
        return v.rearrange("(o n) -> o n", o=1).broadcast_to([P, v.shape[0]])

    def phase2(self):
        self.pr.fence()
        self.experts()
        self.pr.fence()
        self.mha()

    def experts(self):
        nc, pr, ins, ps = self.nc, self.pr, self.ins, self.ps
        sb = Arena(nc, self.base, self.hi)
        self.yd = nc.dram_tensor("y_scratch", [NB * NT, P, D], F32).ap()
        E, M = 8, 128

        def weight(name, shape, src, eng="sync"):
            t = sb("ew_" + name, shape)
            return t, pr.dma(eng, "ew_" + name, t[tuple(slice(None) for _ in shape)], src)

        wt, h_wt = weight("wt", [P, 2, E], ins["moe_wt"].rearrange("(c p) e -> p c e", p=P))
        wg, h_wg = weight("wg", [DH, E], ins["moe_wg"])
        cT, h_cT = weight("cT", [DH, NB], ins["condT"][:, 0:NB])
        before, h_before = weight("before", [P, E, E], ins["c_before"])
        gate = sb("e_gate", [P, E, 2, M])
        up = sb("e_up", [P, E, 2, M])
        down = sb("e_down", [P, E, D])
        h_gate, h_up, h_down = [], [], []
        sg, h_sg = weight("sg", [P, 2, 2 * M], ins["sh_gate"].rearrange("(c p) m -> p c m", p=P), "scalar")
        su, h_su = weight("su", [P, 2, 2 * M], ins["sh_up"].rearrange("(c p) m -> p c m", p=P), "scalar")
        sd, h_sd = weight("sd", [P, 2, D], ins["sh_down"].rearrange("(c p) m -> p c m", p=P), "scalar")
        for x in range(E):
            h_gate.append(pr.dma("scalar", f"e_gate{x}", gate[:, x, :, :], ins["moe_gate"][x].rearrange("(c p) m -> p c m", p=P)))
            h_up.append(pr.dma("scalar", f"e_up{x}", up[:, x, :, :], ins["moe_up"][x].rearrange("(c p) m -> p c m", p=P)))
            h_down.append(pr.dma("scalar", f"e_down{x}", down[:, x, :], ins["moe_down"][x]))
        xb = Ring([sb(f"e_x{i}", [P, NT, D]) for i in range(2)])
        xT = Ring([sb(f"e_xT{i}", [P, 2, S]) for i in range(2)])
        lg = Ring([sb(f"e_lg{i}", [P, NT, E]) for i in range(2)])
        sm = Ring([sb(f"e_sm{i}", [P, 4, NT]) for i in range(2)])
        cmp_ = Buf(sb("e_cmp", [P, 2, NT, E, E]))
        gt = Ring([sb(f"e_gt{i}", [P, 2, NT, E]) for i in range(2)])
        lk = Ring([sb(f"e_lk{i}", [P, 2, S]) for i in range(2)])
        aT = Ring([sb(f"e_aT{i}", [P, S]) for i in range(3)])
        yb = Ring([sb(f"e_y{i}", [P, NT, D]) for i in range(2)])
        gb = sb("e_gb", [DH, NB, P])
        h_gb = pr.op("vector", "e_gb", lambda e: e.tensor_copy(
            gb[:, :, :], cT[:, :].unsqueeze(2).broadcast_to([DH, NB, P])), h_cT)
        rR, rG, rU, rD = self.banks(0, 1), self.banks(2, 3), self.banks(4, 5), self.banks(6, 7)
        state = {}

        def route(b):
            st = state[b] = {}
            x, xt = xb.take(), xT.take()
            hx = pr.dma("sync", f"e_x{b % 2}", x.ap[:, :, :], self.x1d[b * NT:(b + 1) * NT].rearrange("t p d -> p t d"),
                        x.free, self.x1_done[b])
            yield
            ev = []
            for c in range(2):
                m = rR.take()
                for t in range(NT):
                    tr = pr.op("tensor", "e_tr", lambda e, c=c, t=t, m=m: e.transpose(
                        m.ap[:, t * P:(t + 1) * P], x.ap[:, t, c * P:(c + 1) * P], self.ident[:, :]), hx, m.free)
                h = pr.op("scalar", "e_xT", lambda e, c=c, m=m: e.activation(xt.ap[:, c, :], m.ap, ACT.Copy), tr, xt.free)
                m.free = [h]
                ev.append(h)
                yield
            x.free, xt.free = [tr], []
            st["xt"], st["ev"] = xt, ev
            m = rR.take()
            for t in range(NT):
                for c in range(2):
                    pr.op("tensor", "e_lg", lambda e, c=c, t=t, m=m: e.matmul(
                        m.ap[:, t * E:(t + 1) * E], xt.ap[:, c, t * P:(t + 1) * P], wt[:, c, :], start=(c == 0), stop=False),
                        ev, h_wt, m.free)
                mm = pr.op("tensor", "e_lg", lambda e, t=t, m=m: e.matmul(
                    m.ap[:, t * E:(t + 1) * E], gb[:, b, :], wg[:, :], start=False, stop=True), h_gb, h_wg)
            l, s_, g = lg.take(), sm.take(), gt.take()
            lv = l.ap[:, :, :]
            h = pr.op("scalar", "e_lgc", lambda e, m=m: e.activation(
                lv, m.ap[:, 0:NT * E].rearrange("p (t e) -> p t e", t=NT), ACT.Copy, scale=0.5), mm, l.free)
            m.free = [h]
            yield
            col = lambda k: s_.ap[:, k, :]
            wide = lambda k: s_.ap[:, k, :].unsqueeze(2).broadcast_to([P, NT, E])
            a = pr.op("vector", "e_r", lambda e: e.tensor_reduce(col(0), lv, AX, ALU.max), h, s_.free)
            a = pr.op("vector", "e_r", lambda e: e.tensor_tensor(lv, lv, wide(0), ALU.subtract), a)
            h = pr.op("scalar", "e_exp", lambda e: e.activation(lv, lv, ACT.Exp), a)
            a = pr.op("vector", "e_r", lambda e: e.tensor_reduce(col(1), lv, AX, ALU.add), h)
            a = pr.op("vector", "e_r", lambda e: e.reciprocal(col(2), col(1)), a)
            a = pr.op("vector", "e_r", lambda e: e.tensor_tensor(lv, lv, wide(2), ALU.mult), a)
            yield
            four = [P, NT, E, E]
            c0, c1 = cmp_.ap[:, 0, :, :, :], cmp_.ap[:, 1, :, :, :]
            for t in range(NT):
                oth = lv[:, t, :].unsqueeze(1).broadcast_to([P, E, E])
                own = lv[:, t, :].unsqueeze(2).broadcast_to([P, E, E])
                k1 = pr.op("vector", "e_r", lambda e, t=t, oth=oth, own=own: e.tensor_tensor(c0[:, t, :, :], oth, own, ALU.is_gt),
                           a, cmp_.free)
                k2 = pr.op("vector", "e_r", lambda e, t=t, oth=oth, own=own: e.tensor_tensor(c1[:, t, :, :], oth, own, ALU.is_equal),
                           a, cmp_.free)
                k3 = pr.op("vector", "e_r", lambda e, t=t: e.tensor_tensor(c1[:, t, :, :], c1[:, t, :, :], before[:, :, :], ALU.mult),
                           k2, h_before)
                k4 = pr.op("vector", "e_r", lambda e, t=t: e.tensor_tensor(c0[:, t, :, :], c0[:, t, :, :], c1[:, t, :, :], ALU.add),
                           k1, k3)
            gv, sel = g.ap[:, 0, :, :], g.ap[:, 1, :, :]
            a = pr.op("vector", "e_r", lambda e: e.tensor_reduce(sel, c0, AX, ALU.add), k4, g.free)
            cmp_.free = [a]
            yield
            a = pr.op("vector", "e_r", lambda e: e.tensor_scalar(sel, sel, 1.5, None, ALU.is_lt), a)
            a = pr.op("vector", "e_r", lambda e: e.tensor_tensor(gv, sel, lv, ALU.mult), a)
            l.free = [a]
            a = pr.op("vector", "e_r", lambda e: e.tensor_reduce(col(3), gv, AX, ALU.add), a)
            a = pr.op("vector", "e_r", lambda e: e.tensor_scalar(col(3), col(3), 1e-20, None, ALU.add), a)
            a = pr.op("vector", "e_r", lambda e: e.reciprocal(col(2), col(3)), a)
            a = pr.op("vector", "e_r", lambda e: e.tensor_tensor(gv, gv, wide(2), ALU.mult), a)
            s_.free = [a]
            g.free = []
            st["g"], st["hg"] = g, a
            yield

        def body(b, wgate, wup, wdown, ready_in, ready_out):
            st = state[b]
            xt = st["xt"]
            mg, mu = rG.take(), rU.take()
            for c in range(2):
                m1 = pr.op("tensor", "e_g", lambda e, c=c: e.matmul(
                    mg.ap, wgate(c), xt.ap[:, c, :], start=(c == 0), stop=(c == 1)), st["ev"], ready_in, mg.free)
            for c in range(2):
                m2 = pr.op("tensor", "e_u", lambda e, c=c: e.matmul(
                    mu.ap, wup(c), xt.ap[:, c, :], start=(c == 0), stop=(c == 1)), mu.free)
            k, a = lk.take(), aT.take()
            h1 = pr.op("scalar", "e_lk", lambda e: e.activation(k.ap[:, 0, :], mg.ap, ACT.Copy, scale=0.01), m1, k.free)
            h2 = pr.op("vector", "e_mx", lambda e: e.tensor_tensor(k.ap[:, 1, :], mg.ap, k.ap[:, 0, :], ALU.max), h1, k.free)
            h3 = pr.op("vector", "e_ml", lambda e: e.tensor_tensor(a.ap[:, :], mu.ap, k.ap[:, 1, :], ALU.mult), m2, h2, a.free)
            mg.free, mu.free, k.free, a.free = [h2], [h3], [h3], []
            xt.free.append(m2)
            return a, h3

        def run(b):
            st = state[b]
            y = yb.take()
            parts = []
            for u in range(2):
                parts.append(body(b, lambda c, u=u: sg[:, c, u * M:(u + 1) * M], lambda c, u=u: su[:, c, u * M:(u + 1) * M],
                                  None, [h_sg, h_su], None))
                yield
            hy = {}
            for v in range(2):
                m = rD.take()
                for i in range(2):
                    t = 2 * v + i
                    for u in range(2):
                        a, ha = parts[u]
                        mm = pr.op("tensor", "e_d", lambda e, a=a, t=t, i=i, u=u, m=m: e.matmul(
                            m.ap[:, i * D:(i + 1) * D], a.ap[:, t * P:(t + 1) * P], sd[:, u, :], start=(u == 0), stop=(u == 1)),
                            ha, h_sd, m.free)
                h = pr.op("scalar", "e_y0", lambda e, v=v, m=m: e.activation(
                    y.ap[:, 2 * v:2 * v + 2, :], m.ap.rearrange("p (t d) -> p t d", t=2), ACT.Copy), mm, y.free)
                m.free = [h]
                hy[2 * v] = hy[2 * v + 1] = h
                yield
            for a, _ in parts:
                a.free = [mm]
            wait = []
            for x in range(E + 1):
                if x < E:
                    wait.append((x, body(b, lambda c, x=x: gate[:, x, c, :], lambda c, x=x: up[:, x, c, :], None,
                                         [h_gate[x], h_up[x]], None)))
                    yield
                if x >= 1:
                    z, (a, ha) = wait.pop(0)
                    for v in range(2):
                        m = rD.take()
                        for i in range(2):
                            t = 2 * v + i
                            mm = pr.op("tensor", "e_d", lambda e, a=a, t=t, i=i, z=z, m=m: e.matmul(
                                m.ap[:, i * D:(i + 1) * D], a.ap[:, t * P:(t + 1) * P], down[:, z, :], start=True, stop=True),
                                ha, h_down[z], m.free)
                        hs = []
                        for i in range(2):
                            t = 2 * v + i
                            hy[t] = pr.op("vector", "e_acc", lambda e, t=t, i=i, z=z, m=m: e.scalar_tensor_tensor(
                                y.ap[:, t, :], m.ap[:, i * D:(i + 1) * D], st["g"].ap[:, 0, t, z:z + 1], y.ap[:, t, :],
                                ALU.mult, ALU.add), mm, st["hg"], hy[t])
                            hs.append(hy[t])
                        m.free = hs
                    a.free = [mm]
                    yield
            st["g"].free = list(hy.values())
            hd = pr.dma("sync", f"e_yd{b % 2}", self.yd[b * NT:(b + 1) * NT].rearrange("t p d -> p t d"), y.ap[:, :, :],
                        list(hy.values()))
            y.free = [hd]
            self.y_done[b] = [hd]

        self.y_done = {}
        for _ in route(0):
            pass
        for b in range(NB):
            streams = [(run(b), 22)]
            if b + 1 < NB:
                streams.append((route(b + 1), 8))
            merge(*streams)
        self.high2 = sb.high

    def mha(self):
        nc, pr, ins, ps = self.nc, self.pr, self.ins, self.ps
        sb = Arena(nc, self.base, self.hi)
        F32R = mybir.dt.float32r
        scr = nc.dram_tensor("qk_scratch", [2, 4, D, S], F32).ap()

        def weight(name, shape, src, eng="sync"):
            t = sb("mw_" + name, shape)
            return t, pr.dma(eng, "mw_" + name, t[tuple(slice(None) for _ in shape)], src)

        wi, h_wi = weight("wi", [P, 2, 3 * D], ins["wi"].rearrange("(c p) n -> p c n", p=P))
        bic, h_bic = weight("bic", [P, 6], ins["bic"])
        bv, h_bv = weight("bv", [P, D], self.row(ins["bi"][2 * D:3 * D]))
        wo, h_wo = weight("wo", [P, 2, D], ins["wo2"].rearrange("(c p) n -> p c n", p=P))
        bo, h_bo = weight("bo", [P, D], self.row(ins["bo2"]))
        g1, h_g1 = weight("g1", [P, D], self.row(ins["ln1_g"]))
        b1, h_b1 = weight("b1", [P, D], self.row(ins["ln1_b"]))
        bq = sb("m_bq", [P, 2])
        h_bq = pr.op("vector", "m_bq", lambda e: e.tensor_scalar(bq[:, :], bic[:, 0:2], 0.25, None, ALU.mult), h_bic)
        G4 = 4
        KS = 66
        xb = Buf(sb("m_x", [P, NT, D]))
        yT = Buf(sb("m_yT", [P, 2, S]))
        full = Buf(sb("m_full", [P, S]))
        part = Ring([sb(f"m_part{i}", [P, 2, S], F32R) for i in range(2)])
        qst = [Buf(sb(f"m_qs{i}", [KS, G4, S], F32R)) for i in range(8)]
        kst = [Buf(sb(f"m_ks{i}", [KS, G4, S], F32R)) for i in range(8)]
        va = Ring([sb(f"m_va{i}", [P, NT, H, 32]) for i in range(3)])
        mx = Ring([sb(f"m_mx{i}", [P, NT, H]) for i in range(2)])
        mrow = Buf(sb("m_mrow", [H, S]))
        mhl = Buf(sb("m_mhl", [H, 2, S], F32R))
        pt = Ring([sb(f"m_pt{i}", [P, G4, S]) for i in range(2)])
        of = Ring([sb(f"m_of{i}", [P, S]) for i in range(1)])
        rc = Ring([sb(f"m_rc{i}", [P, NT, G4]) for i in range(1)])
        ots = Ring([sb(f"m_ot{i}", [P, NT, H, 16]) for i in range(2)])
        oT = Ring([sb(f"m_oT{i}", [P, 2, P]) for i in range(2)])
        zb = Ring([sb(f"m_z{i}", [P, D]) for i in range(2)])
        lnr = self.ln_make(sb, "m_ln", 1)
        ones = sb("m_one", [2, S], F32R)
        self.high3 = sb.high
        o1 = pr.op("vector", "m_one", lambda e: e.memset(ones[:, :].bitcast(F32), 1.0))
        o1 = pr.op("vector", "m_one", lambda e: e.tensor_copy(ones[:, :], ones[:, :].bitcast(F32)), o1)
        for i, k in enumerate(kst):
            k.free = [pr.dma("sync", f"m_kone{i}", k.ap[64:66, j, :].bitcast(F32), ones[:, :].bitcast(F32), o1)
                      for j in range(G4)]
        for i, v in enumerate(va.bufs):
            v.free = [pr.op("vector", "m_va1", lambda e, v=v: e.memset(v.ap[:, :, :, :], 1.0))]
        rM, rS, rE, rO = self.banks(0, 6), self.banks(1, 2, 3), self.banks(4, 5), self.banks(7)
        state = {}

        def project(b):
            st = state[b] = {}
            hx = pr.dma("sync", "m_x", xb.ap[:, :, :], self.yd[b * NT:(b + 1) * NT].rearrange("t p d -> p t d"),
                        xb.free, self.y_done[b])
            yield
            ev = []
            for c in range(2):
                m = rM.take()
                for t in range(NT):
                    tr = pr.op("tensor", "m_tr", lambda e, c=c, t=t, m=m: e.transpose(
                        m.ap[:, t * P:(t + 1) * P], xb.ap[:, t, c * P:(c + 1) * P], self.ident[:, :]), hx, m.free)
                h = pr.op("scalar", "m_yT", lambda e, c=c, m=m: e.activation(yT.ap[:, c, :], m.ap, ACT.Copy), tr, yT.free)
                m.free = [h]
                ev.append(h)
                yield
            xb.free = [tr]
            hst = []
            for w in range(2):
                hi, lo = part.take(), part.take()
                for c in range(2):
                    m = rM.take()
                    for k in range(2):
                        mm = pr.op("tensor", "m_qk", lambda e, c=c, k=k, w=w, m=m: e.matmul(
                            m.ap, wi[:, k, w * D + c * P:w * D + (c + 1) * P], yT.ap[:, k, :], start=(k == 0), stop=(k == 1)),
                            ev, h_wi, m.free)
                    if w == 0:
                        h = pr.op("scalar", "m_qc", lambda e, c=c, m=m: e.activation(
                            full.ap[:, :], m.ap, ACT.Identity, bias=bq[:, c:c + 1], scale=0.25), mm, h_bq, full.free)
                    else:
                        h = pr.op("scalar", "m_kc", lambda e, c=c, m=m: e.activation(
                            full.ap[:, :], m.ap, ACT.Identity, bias=bic[:, 2 + c:3 + c]), mm, h_bic, full.free)
                    m.free = [h]
                    hh = pr.op("gpsimd", "m_hi", lambda e, c=c, hi=hi: e.tensor_scalar(
                        hi.ap[:, c, :], full.ap[:, :], 1.0, 1.0, ALU.mult, ALU.mult), h, hi.free)
                    hl = pr.op("gpsimd", "m_lo", lambda e, c=c, hi=hi, lo=lo: e.tensor_tensor(
                        lo.ap[:, c, :], full.ap[:, :], hi.ap[:, c, :].bitcast(F32), ALU.subtract), hh, lo.free)
                    full.free = [hl]
                    yield
                for i, (u, hu) in enumerate(((hi, [hh, hl]), (lo, [hl]))):
                    hd = pr.dma("sync", f"m_sc{2 * w + i}", scr[b % 2, 2 * w + i].rearrange("(c p) t -> p c t", p=P),
                                u.ap[:, :, :].bitcast(F32), hu, state[b - 2]["loaded"] if b >= 2 else [])
                    u.free = [hd]
                    hst.append(hd)
            st["stored"] = hst
            v = va.take()
            hv = []
            for u in range(2):
                m = rM.take()
                for i in range(2):
                    for k in range(2):
                        mm = pr.op("tensor", "m_v", lambda e, t=2 * u + i, i=i, k=k, m=m: e.matmul(
                            m.ap[:, i * D:(i + 1) * D], yT.ap[:, k, t * P:(t + 1) * P], wi[:, k, 2 * D:3 * D],
                            start=(k == 0), stop=(k == 1)), ev, h_wi, m.free)
                h = [pr.op("vector", "m_vc", lambda e, t=2 * u + i, i=i, m=m: e.tensor_tensor(
                    v.ap[:, t, :, 0:16], m.ap[:, i * D:(i + 1) * D].rearrange("p (h d) -> p h d", h=H),
                    bv[:, :].rearrange("p (h d) -> p h d", h=H), ALU.add), mm, h_bv, v.free) for i in range(2)]
                m.free = h
                hv += h
                yield
            yT.free = [mm]
            v.free = []
            st["v"], st["hv"] = v, hv

        def load(b):
            st = state[b]
            st["stack"] = {}
            st["loaded"] = []
            for g in range(4):
                i = (b % 2) * 4 + g
                hs = []
                for nm, bufs, order in (("q", qst, (0, 0, 1, 1)), ("k", kst, (2, 3, 2, 3))):
                    for s_, p_ in enumerate(order):
                        hs.append(pr.dma("sync", f"m_st{i}", bufs[i].ap[16 * s_:16 * s_ + 16, :, :].bitcast(F32),
                                         scr[b % 2, p_, 64 * g:64 * g + 64].rearrange("(h d) t -> d h t", d=16),
                                         st["stored"], bufs[i].free))
                kst[i].free, qst[i].free = [], []
                st["stack"][g] = hs
                st["loaded"] += hs

        def maxima(b):
            st = state[b]
            x = mx.take()
            hm = []
            for h in range(H):
                i = (b % 2) * 4 + h // 4
                for t in range(NT):
                    m = rS.take()
                    mm = pr.op("tensor", "m_S", lambda e, h=h, t=t, i=i, m=m: e.matmul(
                        m.ap, qst[i].ap[0:64, h % 4, t * P:(t + 1) * P], kst[i].ap[0:64, h % 4, :], start=True, stop=True),
                        st["stack"][h // 4], m.free)
                    r = pr.op("vector", "m_max", lambda e, h=h, t=t, m=m: e.tensor_reduce(
                        x.ap[:, t, h:h + 1], m.ap, AX, ALU.max), mm, x.free)
                    m.free = [r]
                    hm.append(r)
                    yield
            m = rM.take()
            for t in range(NT):
                tr = pr.op("tensor", "m_mT", lambda e, t=t, m=m: e.transpose(
                    m.ap[0:H, t * P:(t + 1) * P], x.ap[:, t, :], self.ident[:, :]), hm, m.free)
            x.free = [tr]
            h = pr.op("vector", "m_neg", lambda e, m=m: e.tensor_scalar(
                mrow.ap[:, :], m.ap[0:H, :], -1.0, None, ALU.mult), tr, mrow.free)
            m.free = [h]
            h1 = pr.op("vector", "m_nhi", lambda e: e.tensor_copy(mhl.ap[:, 0, :], mrow.ap[:, :]), h, mhl.free)
            h2 = pr.op("vector", "m_nlo", lambda e: e.tensor_tensor(
                mhl.ap[:, 1, :], mrow.ap[:, :], mhl.ap[:, 0, :].bitcast(F32), ALU.subtract), h1)
            mrow.free = [h2]
            hs = []
            for g in range(4):
                i = (b % 2) * 4 + g
                for u in range(2):
                    hs.append(pr.dma("sync", f"m_mr{i}", qst[i].ap[64 + u:65 + u, :, :].bitcast(F32),
                                     mhl.ap[4 * g:4 * g + 4, u, :].bitcast(F32), h2, mm))
            mhl.free = hs
            st["neg"] = hs
            yield

        def turn_back(g, f, h, ot, ho):
            m = rM.take()
            for t in range(NT):
                tr = pr.op("tensor", "m_ofT", lambda e, t=t: e.transpose(
                    m.ap[:, t * P:(t + 1) * P], f.ap[:, t * P:(t + 1) * P], self.ident[:, :]), h, m.free)
            f.free = [tr]
            r = rc.take()
            m4 = m.ap.rearrange("p (t h d) -> p t h d", t=NT, h=G4)
            hr = pr.op("vector", "m_rc", lambda e: e.reciprocal(r.ap[:, :, :], m4[:, :, :, 16]), tr, r.free)
            hn = pr.op("vector", "m_on", lambda e: e.tensor_tensor(
                ot.ap[:, :, 4 * g:4 * g + 4, :], m4[:, :, :, 0:16],
                r.ap[:, :, :].unsqueeze(3).broadcast_to([P, NT, G4, 16]), ALU.mult), hr, ot.free)
            m.free = [hn]
            r.free = [hn]
            ho.append(hn)
            yield

        def attend(b):
            st = state[b]
            v = st["v"]
            ot = ots.take()
            ho = []
            later = None
            for g in range(4):
                i = (b % 2) * 4 + g
                o = rO.take()
                pend = []
                for kt in range(NT + 1):
                    if kt in (1, 2) and later is not None:
                        next(later, None)
                    if kt < NT:
                        p = pt.take()
                        he = []
                        for j in range(4):
                            m = rE.take()
                            mm = pr.op("tensor", "m_ST", lambda e, kt=kt, j=j, m=m, i=i: e.matmul(
                                m.ap, kst[i].ap[:, j, kt * P:(kt + 1) * P], qst[i].ap[:, j, :],
                                start=True, stop=True), st["stack"][g], st["neg"], m.free)
                            h = pr.op("scalar", "m_exp", lambda e, j=j, m=m, p=p: e.activation(
                                p.ap[:, j, :], m.ap, ACT.Exp), mm, p.free)
                            m.free = [h]
                            he.append(h)
                            yield
                        p.free = []
                        pend.append((kt, p, he))
                    if kt >= 1:
                        k0, p0, h0 = pend.pop(0)
                        for j in range(4):
                            av = pr.op("tensor", "m_AV", lambda e, k0=k0, p0=p0, j=j, o=o, g=g: e.matmul(
                                o.ap[32 * j:32 * j + 32, :], v.ap[:, k0, 4 * g + j, :], p0.ap[:, j, :],
                                start=(k0 == 0), stop=(k0 == NT - 1), tile_position=(0, 32 * j)), h0, st["hv"], o.free)
                        p0.free = [av]
                        yield
                qst[i].free, kst[i].free = [mm], [mm]
                f = of.take()
                h = pr.op("vector", "m_of", lambda e, f=f, o=o: e.tensor_copy(f.ap[:, :], o.ap), av, f.free)
                o.free = [h]
                f.free = []
                later = turn_back(g, f, h, ot, ho)
                yield
            for _ in later:
                yield
            v.free = [av]
            ot.free = []
            st["ot"], st["ho"] = ot, ho

        def finish(b):
            st = state[b]
            ot, ho = st["ot"], st["ho"]
            done, held = [], {}
            for k in range(NT + 1):
                if k < NT:
                    m = rM.take()
                    for c in range(2):
                        tr = pr.op("tensor", "m_oT_t", lambda e, c=c, t=k, m=m: e.transpose(
                            m.ap[:, c * P:(c + 1) * P], ot.ap[:, t, 8 * c:8 * c + 8, :], self.ident[:, :]), ho, m.free)
                    q = oT.take()
                    h = pr.op("scalar", "m_oT", lambda e, q=q, m=m: e.activation(
                        q.ap[:, :, :], m.ap[:, 0:D].rearrange("p (c k) -> p c k", c=2), ACT.Copy), tr, q.free)
                    m.free = [h]
                    q.free = []
                    z = zb.take()
                    n = b * NT + k
                    hz = pr.dma("sync", f"m_z{n % 2}", z.ap[:, :], self.yd[n], z.free, self.y_done[b])
                    hz = pr.op("gpsimd", "m_zb", lambda e, z=z: e.tensor_tensor(z.ap[:, :], z.ap[:, :], bo[:, :], ALU.add), hz, h_bo)
                    z.free = []
                    held[k] = (q, h, z, hz)
                    yield
                if k >= 1:
                    t = k - 1
                    q, h, z, hz = held.pop(t)
                    n = b * NT + t
                    m = rM.take()
                    for c in range(2):
                        mm = pr.op("tensor", "m_wo", lambda e, c=c, q=q, m=m: e.matmul(
                            m.ap[:, 0:D], q.ap[:, c, :], wo[:, c, :], start=(c == 0), stop=(c == 1)), h, h_wo, m.free)
                    q.free = [mm]
                    a = pr.op("vector", "m_zs", lambda e, z=z, m=m: e.tensor_tensor(
                        z.ap[:, :], m.ap[:, 0:D], z.ap[:, :], ALU.add), mm, hz)
                    m.free = [a]
                    a = self.ln("m_ln", lnr, [z.ap[:, :]], [z.ap[:, :]], [a], [])
                    a = pr.op("gpsimd", "m_lg", lambda e, z=z: e.tensor_tensor(z.ap[:, :], z.ap[:, :], g1[:, :], ALU.mult), a, h_g1)
                    a = pr.op("gpsimd", "m_lb", lambda e, z=z: e.tensor_tensor(z.ap[:, :], z.ap[:, :], b1[:, :], ALU.add), a, h_b1)
                    hd = pr.dma("sync", f"m_x2{n % 2}", self.x2d[n], z.ap[:, :], a)
                    z.free = [hd]
                    done.append(hd)
                    yield
            ot.free = [tr]
            self.x2_done[b] = done

        self.x2_done = {}
        for _ in project(0):
            pass
        load(0)
        streams = [(maxima(0), 65)]
        if NB > 1:
            streams.append((project(1), 8))
        merge(*streams)
        if NB > 1:
            load(1)
        for b in range(NB):
            streams = [(attend(b), 82)]
            if b + 1 < NB:
                streams.append((maxima(b + 1), 65))
            if b >= 1:
                streams.append((finish(b - 1), 8))
            if b + 2 < NB:
                streams.append((self.delayed(project, b + 2, 4), 12))
            merge(*streams)
            if b + 2 < NB:
                load(b + 2)
        for _ in finish(NB - 1):
            pass

    def gating(self, tag, l, s_, w, ready, before, h_before, l_free):
        pr = self.pr
        v = lambda fn, *after: pr.op("vector", tag, fn, *after)
        G, X = 4, 2
        gl = l[:, :, 0:4]
        xl = l[:, :, 4:12].rearrange("p t (g x) -> p t g x", g=G)
        col = lambda k: s_[:, k, :, 0]
        wide = lambda k: s_[:, k, :, 0].unsqueeze(2).broadcast_to([P, NT, G])
        quad = lambda k: s_[:, k, :, :]
        qwide = lambda k: s_[:, k, :, :].unsqueeze(3).broadcast_to([P, NT, G, X])
        a1 = v(lambda e: e.tensor_reduce(col(0), gl, AX, ALU.max), ready, l_free)
        a2 = v(lambda e: e.tensor_reduce(quad(1), xl, AX, ALU.max), ready, l_free)
        a1 = v(lambda e: e.tensor_tensor(gl, gl, wide(0), ALU.subtract), a1)
        a2 = v(lambda e: e.tensor_tensor(xl, xl, qwide(1), ALU.subtract), a2)
        h = pr.op("scalar", tag + "_e", lambda e: e.activation(l[:, :, :], l[:, :, :], ACT.Exp), a1, a2)
        a1 = v(lambda e: e.tensor_reduce(col(2), gl, AX, ALU.add), h)
        a2 = v(lambda e: e.tensor_reduce(quad(3), xl, AX, ALU.add), h)
        a1 = v(lambda e: e.reciprocal(col(4), col(2)), a1)
        a2 = v(lambda e: e.reciprocal(quad(5), quad(3)), a2)
        a1 = v(lambda e: e.tensor_tensor(gl, gl, wide(4), ALU.mult), a1)
        a2 = v(lambda e: e.tensor_tensor(xl, xl, qwide(5), ALU.mult), a2)
        b1 = v(lambda e: e.tensor_reduce(col(6), gl, AX, ALU.max), a1)
        b2 = v(lambda e: e.tensor_tensor(quad(7), gl, wide(6), ALU.is_ge), b1)
        pairs = w.rearrange("p t (g x) -> p t g x", g=G)
        cnt = []
        for g in range(G):
            c = v(lambda e, g=g: e.tensor_tensor(s_[:, 9:13, :, g].rearrange("p j t -> p t j"), quad(7),
                                                 before[:, g, 0:G].unsqueeze(1).broadcast_to([P, NT, G]), ALU.mult), b2, h_before)
            cnt.append(c)
        for g in range(G):
            cnt[g] = v(lambda e, g=g: e.tensor_reduce(s_[:, 8, :, g], s_[:, 9:13, :, g].rearrange("p j t -> p t j"), AX, ALU.add), cnt[g])
        c = v(lambda e: e.tensor_scalar(quad(8), quad(8), 0.5, None, ALU.is_lt), cnt)
        c = v(lambda e: e.tensor_tensor(quad(7), quad(7), quad(8), ALU.mult), c)
        c = v(lambda e: e.tensor_tensor(quad(7), quad(7), wide(6), ALU.mult), c)
        d1 = v(lambda e: e.tensor_reduce(quad(1), xl, AX, ALU.max), a2)
        c = v(lambda e: e.tensor_tensor(quad(7), quad(7), quad(1), ALU.mult), c, d1)
        d2 = v(lambda e: e.tensor_tensor(quad(3), xl[:, :, :, 0], xl[:, :, :, 1], ALU.is_ge), a2)
        e1 = v(lambda e: e.tensor_tensor(pairs[:, :, :, 0], quad(7), quad(3), ALU.mult), c, d2)
        return [v(lambda e: e.tensor_tensor(pairs[:, :, :, 1], quad(7), pairs[:, :, :, 0], ALU.subtract), e1)]

    def phase3(self):
        self.pr.fence()
        nc, pr, ins, ps = self.nc, self.pr, self.ins, self.ps
        sb = Arena(nc, self.base, self.hi)
        E, F, NN = 8, 512, NB * NT
        NS = NN + E - 1
        I32 = mybir.dt.int32
        xsd = self.xsd
        ysd = nc.dram_tensor("ys_scratch", [NS * P, D], F32).ap()
        regs = {}

        def weight(name, shape, src, eng="sync"):
            t = sb("hw_" + name, shape)
            return t, pr.dma(eng, "hw_" + name, t[tuple(slice(None) for _ in shape)], src)

        x2 = sb("h_x2", [P, NN, D])
        h_x2 = [pr.dma("sync", f"h_x2{b}", x2[:, b * NT:(b + 1) * NT, :], self.x2d[b * NT:(b + 1) * NT].rearrange("t p d -> p t d"),
                       self.x2_done[b]) for b in range(NB)]
        wgx = sb("hw_gx", [P, 2, 12])
        bgx = sb("hw_bgx", [P, 12])
        h_gx = [pr.dma("scalar", "hw_g", wgx[:, :, 0:4], ins["w_group"].rearrange("(c p) g -> p c g", p=P)),
                pr.dma("scalar", "hw_bg", bgx[:, 0:4], self.row(ins["b_group"])),
                pr.dma("scalar", "hw_bx", bgx[:, 4:12], self.row(ins["b_expert"]))]
        h_gx += [pr.dma("scalar", "hw_x", wgx[:, c, 4 + 2 * g:6 + 2 * g], ins["w_expert"][g, c * P:(c + 1) * P, :])
                 for g in range(4) for c in range(2)]
        before, h_before = weight("before", [P, E, E], ins["c_before"], "scalar")
        upper, h_upper = weight("upper", [P, P], ins["c_upper"], "scalar")
        thr, h_thr = weight("thr", [P, NN], ins["c_thr"][:, 0:NN], "scalar")
        iota, h_iota = weight("iota", [P, NS], ins["c_iota"][:, 0:NS], "scalar")
        b1, h_b1 = weight("b1", [P, E * F], self.row(ins["b1"].rearrange("x f -> (x f)")), "scalar")
        b2, h_b2 = weight("b2", [P, E * D], self.row(ins["b2"].rearrange("x d -> (x d)")), "scalar")
        g2, h_g2 = weight("g2", [P, D], self.row(ins["ln2_g"]), "scalar")
        c2, h_c2 = weight("c2", [P, D], self.row(ins["ln2_b"]), "scalar")
        w1 = sb("hw_w1", [P, E, 2 * F])
        w2 = sb("hw_w2", [P, E, 4 * D])
        h_w1, h_w2 = [], []
        for x in range(E):
            h_w1.append(pr.dma("scalar", "hw_w1", w1[:, x, :].rearrange("p (c f) -> p c f", c=2),
                               ins["w1"][x].rearrange("(c p) f -> p c f", p=P)))
            h_w2.append(pr.dma("scalar", "hw_w2", w2[:, x, :].rearrange("p (c d) -> p c d", c=4),
                               ins["w2"][x].rearrange("(c p) d -> p c d", p=P)))
        xr = sb("h_xr", [P, NN, D])
        h_xr = [pr.dma("sync", f"h_xr{b}", xr[:, b * NT:(b + 1) * NT, :], self.x1d[b * NT:(b + 1) * NT].rearrange("t p d -> p t d"))
                for b in range(NB)]
        onesq = sb("h_ones", [P, P])
        h_ones = pr.op("vector", "h_ones", lambda e: e.memset(onesq[:, :], 1.0))
        xT = Ring([sb(f"h_xT{i}", [P, 2, S]) for i in range(2)])
        lg = Ring([sb(f"h_lg{i}", [P, NT, 12]) for i in range(2)])
        sm = Ring([sb(f"h_sm{i}", [P, 13, NT, 4]) for i in range(2)])
        cw = sb("h_cw", [P, NN, E])
        sT = Ring([sb(f"h_sT{i}", [P, 2, P]) for i in range(3)])
        xs = Ring([sb(f"h_xs{i}", [P, D]) for i in range(4)])
        hb = Ring([sb(f"h_hb{i}", [P, F]) for i in range(2)])
        hT = Ring([sb(f"h_hT{i}", [P, 4, P]) for i in range(2)])
        ys = Ring([sb(f"h_ys{i}", [P, D]) for i in range(3)])
        lnr = self.ln_make(sb, "h_ln", 2)
        rA, rH, rT, rD = self.banks(0, 1), self.banks(2, 3), self.banks(4, 5), self.banks(6, 7)

        def gates(b):
            xt = xT.take()
            ev = []
            for c in range(2):
                m = rA.take()
                for t in range(NT):
                    tr = pr.op("tensor", "h_tr", lambda e, c=c, t=t, m=m: e.transpose(
                        m.ap[:, t * P:(t + 1) * P], x2[:, b * NT + t, c * P:(c + 1) * P], self.ident[:, :]), h_x2[b], m.free)
                h = pr.op("scalar", "h_xT", lambda e, c=c, m=m: e.activation(xt.ap[:, c, :], m.ap, ACT.Copy), tr, xt.free)
                m.free = [h]
                ev.append(h)
            m = rH.take()
            for t in range(NT):
                for c in range(2):
                    mm = pr.op("tensor", "h_lg", lambda e, c=c, t=t: e.matmul(
                        m.ap[:, t * 12:(t + 1) * 12], xt.ap[:, c, t * P:(t + 1) * P], wgx[:, c, :], start=(c == 0), stop=(c == 1)),
                        ev, h_gx, m.free)
            xt.free = [mm]
            l, s_ = lg.take(), sm.take()
            h = pr.op("vector", "h_lgb", lambda e: e.tensor_tensor(
                l.ap[:, :, :], m.ap[:, 0:NT * 12].rearrange("p (t e) -> p t e", t=NT),
                bgx[:, :].unsqueeze(1).broadcast_to([P, NT, 12]), ALU.add), mm, h_gx, l.free)
            m.free = [h]
            hw = self.gating("h_gate", l.ap, s_.ap, cw[:, b * NT:(b + 1) * NT, :], h, before, h_before, [s_.free])
            s_.free, l.free = hw, hw
            return hw

        h_cw = [gates(b) for b in range(NB)]

        v = lambda fn, *after: pr.op("vector", "h_slot", fn, *after)
        oh = sb("h_oh", [P, NN, E])
        cum = [sb(f"h_cum{i}", [P, NN, E]) for i in range(2)]
        gsum = sb("h_gsum", [P, NN])
        more = sb("h_more", [P, E, NN])
        nt = sb("h_nt", [P, E])
        first = sb("h_first", [P, E])
        te = sb("h_te", [P, NS])
        tei = sb("h_tei", [P, NS], I32)
        pos = sb("h_pos", [P, NN])
        posi = sb("h_posi", [P, NN], I32)
        wide = lambda t: t[:, :].unsqueeze(1).broadcast_to([P, NN, E])
        flat = lambda t: t[:, :, :].rearrange("p t x -> p (t x)")
        h_oh = v(lambda e: e.tensor_scalar(flat(oh), flat(cw), 0.0, None, ALU.is_gt), h_cw)
        h_gs = v(lambda e: e.tensor_reduce(gsum[:, :], cw[:, :, :], AX, ALU.add), h_cw)
        mr, mt = rA.take(), rA.take()
        h_rank = pr.op("tensor", "h_rank", lambda e: e.matmul(mr.ap[:, 0:NN * E], upper[:, :], flat(oh), start=True, stop=True),
                       h_oh, h_upper, mr.free)
        h_tot = pr.op("tensor", "h_rank", lambda e: e.matmul(mt.ap[:, 0:NN * E], onesq[:, :], flat(oh), start=True, stop=True),
                      h_oh, h_ones, mt.free)
        a = v(lambda e: e.tensor_copy(flat(cum[0]), mt.ap[:, 0:NN * E]), h_tot)
        w, k = 0, 1
        while k < NN:
            p, q = cum[w], cum[1 - w]
            a1 = v(lambda e, p=p, q=q, k=k: e.tensor_copy(q[:, 0:k, :], p[:, 0:k, :]), a)
            a2 = v(lambda e, p=p, q=q, k=k: e.tensor_tensor(q[:, k:NN, :], p[:, k:NN, :], p[:, 0:NN - k, :], ALU.add), a)
            a, w, k = [a1, a2], 1 - w, 2 * k
        inc, exc = cum[w], cum[1 - w]
        b_ = v(lambda e: e.tensor_tensor(more[:, :, :], inc[:, NN - 1, :].unsqueeze(2).broadcast_to([P, E, NN]),
                                         thr[:, :].unsqueeze(1).broadcast_to([P, E, NN]), ALU.is_gt), a, h_thr)
        b_ = v(lambda e: e.tensor_reduce(nt[:, :], more[:, :, :], AX, ALU.add), b_)
        b_ = v(lambda e: e.tensor_tensor(more[:, :, 0:E], before[:, :, :], nt[:, :].unsqueeze(1).broadcast_to([P, E, E]), ALU.mult),
               b_, h_before)
        h_first = v(lambda e: e.tensor_reduce(first[:, :], more[:, :, 0:E], AX, ALU.add), b_)
        a = v(lambda e: e.tensor_tensor(flat(exc), flat(inc), mt.ap[:, 0:NN * E], ALU.subtract), a)
        mt.free = [a]
        a = v(lambda e: e.tensor_tensor(flat(exc), mr.ap[:, 0:NN * E], flat(exc), ALU.add), a, h_rank)
        mr.free = [a]
        b_ = v(lambda e: e.tensor_scalar(nt[:, :], first[:, :], 128.0, None, ALU.mult), h_first)
        a = v(lambda e: e.tensor_tensor(exc[:, :, :], exc[:, :, :], wide(nt), ALU.add), a, b_)
        a = v(lambda e: e.tensor_tensor(exc[:, :, :], exc[:, :, :], oh[:, :, :], ALU.mult), a)
        a = v(lambda e: e.tensor_reduce(pos[:, :], exc[:, :, :], AX, ALU.add), a)
        h_pos = v(lambda e: e.tensor_copy(posi[:, :], pos[:, :]), a)
        tmp = sb("h_tmp", [P, NS, E])
        a = v(lambda e: e.tensor_tensor(tmp[:, :, :], iota[:, :].unsqueeze(2).broadcast_to([P, NS, E]),
                                        first[:, :].unsqueeze(1).broadcast_to([P, NS, E]), ALU.is_ge), h_first, h_iota)
        a = v(lambda e: e.tensor_reduce(te[:, :], tmp[:, :, :], AX, ALU.add), a)
        a = v(lambda e: e.tensor_scalar(te[:, :], te[:, :], 1.0, None, ALU.subtract), a)
        h_te = v(lambda e: e.tensor_copy(tei[:, :], te[:, :]), a)

        def scatter(n):
            return pr.put("gpsimd", "h_sc", lambda e: e.indirect_dma_start(
                xsd, bass.IndirectOffsetOnAxis(ap=posi[:, n:n + 1], axis=0), x2[:, n, :], None), 16, h_pos, self.zeroed)

        h_sc = [scatter(n) for n in range(NN)]

        def load_reg(eng, j):
            def emit(e):
                regs[eng, j] = e.value_load(tei[0:1, j:j + 1], min_val=0, max_val=E - 1)
            pr.put(eng, None, emit, 0, h_te)

        def arrive(j):
            x = xs.take()
            h = pr.dma("sync", f"h_xs{j % 4}", x.ap[:, :], xsd[j * P:(j + 1) * P, :], h_sc, x.free)
            m = rA.take()
            for c in range(2):
                tr = pr.op("tensor", "h_sT_t", lambda e, c=c: e.transpose(
                    m.ap[:, c * P:(c + 1) * P], x.ap[:, c * P:(c + 1) * P], self.ident[:, :]), h, m.free)
            x.free = [tr]
            t = sT.take()
            h = pr.op("scalar", "h_sT", lambda e: e.activation(
                t.ap[:, :, :], m.ap[:, 0:D].rearrange("p (c k) -> p c k", c=2), ACT.Copy), tr, t.free)
            m.free = [h]
            return t, h

        def inner(j, t, h):
            load_reg("tensor", j)
            load_reg("vector", j)
            m = rH.take()
            for c in range(2):
                mm = pr.op("tensor", "h_h", lambda e, c=c: e.matmul(
                    m.ap, t.ap[:, c, :], w1[:, bass.ds(regs["tensor", j], 1), c * F:(c + 1) * F].rearrange("p o f -> p (o f)"),
                    start=(c == 0), stop=(c == 1)), h, h_w1, m.free)
            t.free = [mm]
            q = hb.take()
            a = pr.op("vector", "h_hb", lambda e: e.tensor_tensor(
                q.ap[:, :], m.ap, b1[:, bass.ds(regs["vector", j] * F, F)], ALU.add), mm, h_b1, q.free)
            m.free = [a]
            return q, a

        def outer(j, q, a):
            m = rT.take()
            for f in range(4):
                tr = pr.op("tensor", "h_hT_t", lambda e, f=f: e.transpose(
                    m.ap[:, f * P:(f + 1) * P], q.ap[:, f * P:(f + 1) * P], self.ident[:, :]), a, m.free)
            q.free = [tr]
            t = hT.take()
            h = pr.op("scalar", "h_relu", lambda e: e.activation(
                t.ap[:, :, :], m.ap.rearrange("p (f k) -> p f k", f=4), ACT.Relu), tr, t.free)
            m.free = [h]
            return t, h

        def leave(j, t, h):
            m = rD.take()
            for f in range(4):
                mm = pr.op("tensor", "h_o", lambda e, f=f: e.matmul(
                    m.ap[:, 0:D], t.ap[:, f, :], w2[:, bass.ds(regs["tensor", j], 1), f * D:(f + 1) * D].rearrange("p o f -> p (o f)"),
                    start=(f == 0), stop=(f == 3)), h, h_w2, m.free)
            t.free = [mm]
            y = ys.take()
            a = pr.op("vector", "h_yb", lambda e: e.tensor_tensor(
                y.ap[:, :], m.ap[:, 0:D], b2[:, bass.ds(regs["vector", j] * D, D)], ALU.add), mm, h_b2, y.free)
            m.free = [a]
            hd = pr.dma("sync", f"h_ys{j % 3}", ysd[j * P:(j + 1) * P, :], y.ap[:, :], a)
            y.free = [hd]
            return hd

        h_xrb = []
        stage = {}
        h_ys = []
        for j in range(NS + 3):
            if j < NS:
                stage["x", j] = arrive(j)
            if 0 <= j - 1 < NS:
                stage["h", j - 1] = inner(j - 1, *stage.pop(("x", j - 1)))
            if 0 <= j - 3 < NS:
                h_ys.append(leave(j - 3, *stage.pop(("t", j - 3))))
            if 0 <= j - 2 < NS:
                stage["t", j - 2] = outer(j - 2, *stage.pop(("h", j - 2)))
            if j < NN:
                h_xrb.append(pr.op("vector", "h_xrb", lambda e, j=j: e.tensor_tensor(
                    xr[:, j, :], xr[:, j, :], c2[:, :], ALU.add), h_xr[j // NT], h_c2))

        yg = Ring([sb(f"h_yg{i}", [P, D]) for i in range(8)])
        done = []
        gs = []
        for n in range(NN):
            y = yg.take()
            h = pr.put("gpsimd", f"h_yg{n % 8}", lambda e, n=n, y=y: e.indirect_dma_start(
                y.ap[:, :], None, ysd, bass.IndirectOffsetOnAxis(ap=posi[:, n:n + 1], axis=0)), 16, h_ys, y.free)
            h = pr.op("vector", "h_z", lambda e, n=n, y=y: e.scalar_tensor_tensor(
                x2[:, n, :], y.ap[:, :], gsum[:, n:n + 1], x2[:, n, :], ALU.mult, ALU.add), h, h_gs, h_sc)
            y.free = [h]
            gs.append(h)
            if n % NT == NT - 1:
                k = n - NT + 1
                hs = self.ln2(lnr, [x2[:, k + i, :] for i in range(NT)], gs[k:n + 1], g2, h_g2,
                              [xr[:, k + i, :] for i in range(NT)], h_xrb[k:n + 1])
                done.append(pr.dma("sync", "h_out", self.out[n // NT].rearrange("(t p) d -> p t d", p=P),
                                   xr[:, k:n + 1, :], hs))
        pr.wait("sync", done)

    def ln2(self, ring, zs, ready, g, h_g, rests, h_rest):
        pr, b = self.pr, ring.take()
        t, n = b.ap, len(zs)
        hs = [pr.op("vector", "h_ln_st", lambda e, i=i: e.bn_stats(t["st"][:, i, :], zs[i]), ready[i], b.free) for i in range(n)]
        ha = [pr.op("vector", "h_ln_ag", lambda e, i=i: e.bn_aggr(t["mv"][:, i, :], t["st"][:, i, :]), hs[i], b.free) for i in range(n)]
        hv = pr.op("vector", "h_ln_ve", lambda e: e.tensor_scalar(t["ve"][:, 0:n], t["mv"][:, 0:n, 1], EPS, None, ALU.add), ha, b.free)
        hp = pr.op("gpsimd", "h_ln_rs", lambda e: e.tensor_tensor(t["rs"][:, 0:n], t["ve"][:, 0:n], self.mhalf[:, 0:n], ALU.pow),
                   hv, self.h_mhalf, b.free)
        hc = [pr.op("vector", "h_ln_c", lambda e, i=i: e.scalar_tensor_tensor(
            zs[i], zs[i], t["mv"][:, i, 0:1], g[:, :], ALU.subtract, ALU.mult), ha[i], hs[i], h_g) for i in range(n)]
        out = [pr.op("vector", "h_ln_r", lambda e, i=i: e.scalar_tensor_tensor(
            rests[i], zs[i], t["rs"][:, i:i + 1], rests[i], ALU.mult, ALU.add), hc[i], hp, h_rest[i]) for i in range(n)]
        b.free = out
        return out


def build(nc, ins, out):
    with ExitStack() as ctx:
        k = Kernel(nc, ctx, ins, out)
        k.phase1()
        k.phase2()
        k.phase3()
        k.pr.issue(nc, ctx)


def constants():
    inv = (np.float32(1.0) / np.power(np.float32(10000.0), np.arange(0, 16, 2, dtype=np.float32) / np.float32(16))).astype(np.float32)
    ang = (np.arange(S, dtype=np.float32)[:, None] * inv[None, :]).astype(np.float32).astype(np.float64)
    cos, sin = np.cos(ang).astype(np.float32), np.sin(ang).astype(np.float32)
    cos2 = np.concatenate([cos, cos], 1).reshape(NT, P, 16).transpose(1, 0, 2)
    sin2 = np.concatenate([-sin, sin], 1).reshape(NT, P, 16).transpose(1, 0, 2)
    before = np.tril(np.ones((8, 8), np.float32), -1)
    wide = lambda v: np.ascontiguousarray(np.broadcast_to(v.astype(np.float32), (P, v.size)))
    return {
        "c_upper": np.triu(np.ones((P, P), np.float32), 1),
        "c_thr": wide(np.arange(NB * NT) * P),
        "c_iota": wide(np.arange(80)),
        "c_ident": np.eye(P, dtype=np.float32),
        "c_cos": np.ascontiguousarray(cos2),
        "c_sin": np.ascontiguousarray(sin2),
        "c_before": np.ascontiguousarray(np.broadcast_to(before, (P, 8, 8))),
    }


def layout(inputs):
    a = {k: np.ascontiguousarray(v) for k, v in inputs.items()}
    col = lambda v, n: np.ascontiguousarray(v.reshape(n, P).T)
    t = {
        "x": a["x"], "fside": a["fside_16xSxS_0"], "cond": a["cond_64"], "mask": a["mask_BxS_bk0"].view(np.int32),
        "g_in": col(a["L0_cond_g_in"], 2), "g_out": col(a["L0_cond_g_out"], 2),
        "null_bias": a["L0_cond_null_attn_bias"], "cond_wq": a["L0_cond_Wq"], "cond_wkv": a["L0_cond_Wkv"],
        "cond_wo": a["L0_cond_Wo"],
        "attn_wq": a["L0_attn_Wq"], "attn_bq": a["L0_attn_bq"], "attn_wdown": a["L0_attn_Wdown"],
        "attn_bdown": a["L0_attn_bdown"], "attn_wup": a["L0_attn_Wup"], "attn_bup": a["L0_attn_bup"],
        "attn_wout": a["L0_attn_Wout"], "attn_bout": a["L0_attn_bout"],
        "condT": np.ascontiguousarray(a["cond_64"].T),
        "moe_wt": np.ascontiguousarray(a["L0_cond2_wt"].T), "moe_wg": np.ascontiguousarray(a["L0_cond2_wg"].T),
        "moe_gate": a["L0_cond2_w_gate"], "moe_up": a["L0_cond2_w_up"], "moe_down": a["L0_cond2_w_down"],
        "sh_gate": a["L0_cond2_sw_gate"], "sh_up": a["L0_cond2_sw_up"], "sh_down": a["L0_cond2_sw_down"],
        "wi": np.ascontiguousarray(a["L0_ffn_in_proj_w"].T), "bi": a["L0_ffn_in_proj_b"],
        "bic": col(a["L0_ffn_in_proj_b"], 6),
        "wo2": np.ascontiguousarray(a["L0_ffn_out_proj_w"].T), "bo2": a["L0_ffn_out_proj_b"],
        "ln1_g": a["L0_ffn_ln1_g"], "ln1_b": a["L0_ffn_ln1_b"], "ln2_g": a["L0_ffn_ln2_g"], "ln2_b": a["L0_ffn_ln2_b"],
        "w_group": a["L0_ffn_w_group"], "b_group": a["L0_ffn_b_group"],
        "w_expert": a["L0_ffn_w_expert"], "b_expert": a["L0_ffn_b_expert"].reshape(8),
        "w1": a["L0_ffn_w1"], "b1": a["L0_ffn_b1"], "w2": a["L0_ffn_w2"], "b2": a["L0_ffn_b2"],
    }
    t.update(constants())
    return t


def kernel(**inputs):
    import concourse.bacc as bacc
    from concourse.bass_utils import run_bass_kernel_spmd

    arrays = layout({k: np.asarray(v) for k, v in inputs.items()})
    nc = bacc.Bacc("TRN2", target_bir_lowering=False, num_devices=1, dynamic_dma_scratch_size=2048)
    ins = {k: nc.dram_tensor("in_" + k, v.shape, mybir.dt.from_np(v.dtype), kind="ExternalInput").ap()
           for k, v in arrays.items()}
    out = nc.dram_tensor("out_y", (NB, S, D), F32, kind="ExternalOutput").ap()
    build(nc, ins, out)
    r = run_bass_kernel_spmd(nc, [{"in_" + k: v for k, v in arrays.items()}], core_ids=[0])
    return r.results[0]["out_y"]
```

```python
from contextlib import ExitStack

import numpy as np

import concourse.bass as bass
from concourse import mybir

F32 = mybir.dt.float32
BF16 = mybir.dt.bfloat16
U8 = mybir.dt.uint8
ALU = mybir.AluOpType
ACT = mybir.ActivationFunctionType
AX = mybir.AxisListType.X

P = 128
NB = 8
S = 512
NT = 4
D = 256
H = 16
DH = 64
EPS = 1e-5
NEG = -1.0e30
ENGINES = ("tensor", "vector", "scalar", "gpsimd", "sync")
CAUSAL = [0, 128, 384, 768, 1280]
KEYCOL = [0, 512, 896, 1152, 1280]
ON_DVE, ON_POOL = ("vector", "v"), ("gpsimd", "g")
HS_ENG = [[ON_POOL, ON_POOL, ON_POOL, ON_POOL], [ON_DVE, ON_POOL, ON_DVE, ON_POOL]]
HV_ENG = [[ON_POOL, ON_POOL, ON_POOL, ON_POOL], [ON_POOL, ON_DVE, ON_POOL, ON_DVE]]

EARLY_START, EARLY_RATE = -6.0, 1.0
EARLY_SHARED = 0


class Op:

    def __init__(self, eng, sem, emit, after, inc):
        self.eng, self.sem, self.emit, self.after, self.inc = eng, sem, emit, after, inc
        self.needed = inc == 16
        self.value = None
        self.slot = None


class Prog:

    def __init__(self):
        self.queues = {e: [] for e in ENGINES}
        self.phase = 0

    def fence(self):
        last = {}
        for q in self.queues.values():
            for op in q:
                if op.sem is not None and op.phase == self.phase:
                    last[op.sem] = op
        hs = list(last.values())
        for eng in ENGINES:
            self.wait(eng, hs)
        self.phase += 1

    def op(self, eng, sem, emit, *after):
        return self._put(Op(eng, sem, emit, self._flat(after), 1))

    def dma(self, eng, sem, out, in_, *after):
        return self._put(Op(eng, sem, lambda e: e.dma_start(out, in_), self._flat(after), 16))

    def put(self, eng, sem, emit, inc, *after):
        return self._put(Op(eng, sem, emit, self._flat(after), inc))

    def wait(self, eng, *after):
        self._put(Op(eng, None, None, self._flat(after), 0))

    def _put(self, op):
        for a in op.after:
            a.needed = True
        op.phase = self.phase
        self.queues[op.eng].append(op)
        return op

    def _flat(self, xs):
        out = []
        for x in xs:
            if isinstance(x, (list, tuple)):
                out += self._flat(x)
            elif x is not None:
                out.append(x)
        return out

    def issue(self, nc, ctx):
        count, owner, slots = [], {}, {}
        own = []
        for phase in range(self.phase + 1):
            used = 0
            for eng in ENGINES:
                for op in self.queues[eng]:
                    if op.phase != phase or op.sem is None or not op.needed:
                        continue
                    key = (phase, op.sem)
                    assert owner.setdefault(key, eng) == eng, op.sem
                    if key not in slots:
                        if eng == "gpsimd" and op.inc == 16:
                            slots[key] = len(count)
                            own.append(len(count))
                            count.append(0)
                        else:
                            while used in own:
                                used += 1
                            if used == len(count):
                                count.append(0)
                            slots[key] = used
                            used += 1
                    op.slot = slots[key]
                    count[op.slot] += op.inc
                    op.value = count[op.slot]
        sems = [ctx.enter_context(nc.semaphore(f"s{i}")) for i in range(len(count))]
        block = ctx.enter_context(nc.Block())

        def body(queue):
            def run(e):
                seen = {}
                for op in queue:
                    want = {}
                    for a in op.after:
                        if a.value > max(seen.get(a.slot, 0), want.get(a.slot, 0)):
                            want[a.slot] = a.value
                    for slot, value in want.items():
                        e.wait_ge(sems[slot], value)
                        seen[slot] = value
                    if op.emit is not None:
                        ins = op.emit(e)
                        if op.needed:
                            ins.then_inc(sems[op.slot], op.inc)
            return run

        block.tensor(body(self.queues["tensor"]))
        block.vector(body(self.queues["vector"]))
        block.scalar(body(self.queues["scalar"]))
        block.gpsimd(body(self.queues["gpsimd"]))
        block.sync(body(self.queues["sync"]))


class Buf:

    def __init__(self, ap):
        self.ap = ap
        self.held = False
        self._free = []

    @property
    def free(self):
        return self._free

    @free.setter
    def free(self, ops):
        self._free = ops
        self.held = False


class Ring:
    def __init__(self, aps):
        self.bufs = [Buf(a) for a in aps]
        self.n = 0

    def take(self):
        b = self.bufs[self.n % len(self.bufs)]
        self.n += 1
        assert not b.held, "taken again before its last reader was queued"
        b.held = True
        return b


def ring_of(*bufs):
    r = Ring([])
    r.bufs = list(bufs)
    return r


class Arena:
    def __init__(self, nc, start, end):
        self.nc, self.start, self.pos, self.end = nc, start, start, end
        self.high = start

    def __call__(self, name, shape, dt=F32):
        size = int(np.prod(shape[1:])) * mybir.dt.size(dt)
        at = (self.pos + 31) // 32 * 32
        self.pos = at + size
        self.high = max(self.high, self.pos)
        assert self.pos <= self.end, (name, self.pos, self.end)
        return self.nc.alloc_sbuf_tensor_at(name, list(shape), dt, offset=at)


class Spaces:

    def __init__(self, *arenas):
        self.arenas = arenas

    def __call__(self, name, shape, dt=F32):
        size = int(np.prod(shape[1:])) * mybir.dt.size(dt)
        for a in self.arenas:
            if (a.pos + 31) // 32 * 32 + size <= a.end:
                return a(name, shape, dt)
        raise AssertionError((name, size, [a.end - a.pos for a in self.arenas]))


def merge(*streams):
    done = [0] * len(streams)
    total = max(n for _, n in streams)
    for k in range(1, total + 1):
        for i, (g, n) in enumerate(streams):
            while done[i] < n * k // total:
                done[i] += 1
                next(g, None)
    for g, _ in streams:
        for _ in g:
            pass


def weave(*streams):
    done = [0] * len(streams)
    total = max(n for _, n in streams)
    for k in range(1, total + 1):
        for i, (g, n) in enumerate(streams):
            while done[i] < n * k // total:
                done[i] += 1
                next(g, None)
        yield
    for g, _ in streams:
        for _ in g:
            pass


def bc(ap, shape):
    return ap.broadcast_to(list(shape))


class Kernel:
    def __init__(self, nc, ctx, ins, out):
        self.nc, self.ins, self.out = nc, ins, out
        self.pr = Prog()
        self.ps = ctx.enter_context(nc.psum_tensor("ps", [P, 8, 512], F32))
        self.x1d = nc.dram_tensor("x1_scratch", [NB * NT, P, D], F32).ap()
        self.x2d = nc.dram_tensor("x2_scratch", [NB * NT, P, D], F32).ap()
        self.xsd = nc.dram_tensor("xs_scratch", [(NB * NT + 7) * P, D], F32).ap()
        self.xed = nc.dram_tensor("xe_scratch", [(2 * NB * NT + 8) * P, D], F32).ap()
        self.slotted = {}
        self.lo = nc.sbuf_base
        self.hi = nc.sbuf_usable_end
        sb = Arena(nc, self.lo, self.hi)
        pr = self.pr
        self.ident = sb("ident", [P, P])
        self.mhalf = sb("mhalf", [P, NT])
        self.h_ident = pr.dma("sync", "ident", self.ident[:, :], ins["c_ident"])
        self.h_mhalf = pr.op("gpsimd", "mhalf", lambda e: e.memset(self.mhalf[:, :], -0.5))
        self.epos = sb("e_pos2", [P, 2 * NB * NT], mybir.dt.int32)
        self.egate = sb("e_gate2", [P, 2 * NB * NT])
        self.base = sb.pos

    def clear_slots(self, zero):
        hz = self.pr.op("gpsimd", "zero", lambda e: e.memset(zero[:, :], 0.0))
        self.zeroed, self.ezeroed = [self.pr.dma(
            "sync", sem, d.rearrange("(n p) d -> p n d", p=P),
            zero[:, :].unsqueeze(1).broadcast_to([P, d.shape[0] // P, D]), hz) for sem, d in (("zx", self.xsd), ("ze", self.xed))]

    def banks(self, *ks):
        return Ring([self.ps[:, k, :] for k in ks])

    def load(self, eng, sem, dst, src, *after):
        return self.pr.dma(eng, sem, dst, src, *after)

    def ln_make(self, sb, tag, n):
        return Ring([dict(st=sb(f"{tag}st{i}", [P, NT, 6]), mv=sb(f"{tag}mv{i}", [P, NT, 2]),
                          ve=sb(f"{tag}ve{i}", [P, NT]), rs=sb(f"{tag}rs{i}", [P, NT])) for i in range(n)])

    def ln(self, tag, ring, srcs, outs, src_ready, out_free, later=False):
        pr, b = self.pr, ring.take()
        t, n = b.ap, len(srcs)
        hs = []
        for i, s in enumerate(srcs):
            hs.append(pr.op("vector", tag + "_st", lambda e, i=i, s=s: e.bn_stats(t["st"][:, i, :], s),
                            src_ready[i], b.free))
        ha = []
        for i in range(n):
            ha.append(pr.op("vector", tag + "_ag", lambda e, i=i: e.bn_aggr(t["mv"][:, i, :], t["st"][:, i, :]),
                            hs[i], b.free))
        hv = pr.op("vector", tag + "_ve",
                   lambda e: e.tensor_scalar(t["ve"][:, 0:n], t["mv"][:, 0:n, 1], EPS, None, ALU.add), ha, b.free)
        hp = pr.op("gpsimd", tag + "_rs",
                   lambda e: e.tensor_tensor(t["rs"][:, 0:n], t["ve"][:, 0:n], self.mhalf[:, 0:n], ALU.pow),
                   hv, self.h_mhalf, b.free)

        def scale():
            out = []
            for i in range(n):
                out.append(pr.op("vector", tag + "_xn",
                                 lambda e, i=i: e.tensor_scalar(outs[i], srcs[i], t["mv"][:, i, 0:1], t["rs"][:, i:i + 1],
                                                                ALU.subtract, ALU.mult),
                                 hp, out_free))
            b.free = [out[-1]]
            return out

        return scale if later else scale()

    def phase1(self):
        nc, pr, ins, ps = self.nc, self.pr, self.ins, self.ps
        self.split = (self.hi - 159744) // 32 * 32
        sb, top = Arena(nc, self.base, self.split), Arena(nc, self.split, self.hi)
        W = {}

        def weight(name, shape, src, eng="sync", dt=F32, where=sb):
            t = where("w_" + name, shape, dt)
            v = t[tuple(slice(None) for _ in shape)]
            W[name] = t
            return pr.dma(eng, "w_" + name, v, src)

        xin = Buf(sb("xin", [P, NT, D]))
        xv = ins["x"].rearrange("b (t p) d -> b p t d", p=P)
        h_x = {0: pr.dma("sync", "xin", xin.ap[:, :, :], xv[0])}
        h_gin = weight("gin", [P, 2], ins["g_in"])
        h_wq = weight("wq", [P, 2, 1024], ins["cond_wq"].rearrange("(c p) n -> p c n", p=P), where=top)
        wk = sb("w_wk", [P, 2, DH])
        wkv = ins["cond_wkv"].rearrange("(c p) n -> p c n", p=P)
        h_wk = pr.dma("sync", "w_wk", wk[:, :, :], wkv[:, :, 0:DH])
        h_wv = weight("wv", [P, 2, DH], wkv[:, :, DH:2 * DH])
        h_nk = weight("nk", [P, DH], ins["cond"][0:1, :].broadcast_to([P, DH]))
        h_nb = weight("nb", [P, NT, H], ins["null_bias"].rearrange("(o n h) -> o n h", o=1, n=1).broadcast_to([P, NT, H]))
        nv = sb("w_nv", [P, 1])
        nvc = ins["cond"][1:2, :].rearrange("a d -> d a")
        h_nv = [pr.dma("sync", f"w_nv{j}", nv[DH * j:DH * j + DH, :], nvc) for j in range(2)]
        mrow = Ring([sb(f"mrow{i}", [DH + 1, S], U8) for i in range(2)])
        bias = top("bias", [P, H, 1280])
        fv = ins["fside"].rearrange("h (t p) k -> t p h k", p=P)
        h_bias, h_bd = [], []
        for g in range(8):
            h_bd.append([pr.dma("scalar", f"bias{g}", bias[:, 2 * g:2 * g + 2, CAUSAL[t]:CAUSAL[t + 1]],
                                fv[t][:, 2 * g:2 * g + 2, 0:P * (t + 1)]) for t in range(NT)])

        def causal(g):
            hh = []
            for t in range(NT):
                diag = bias[:, 2 * g:2 * g + 2, CAUSAL[t] + P * t:CAUSAL[t + 1]]
                hh.append(pr.op("gpsimd", "causal",
                                lambda e, d=diag: e.affine_select(out=d, in_=d, compare_op=ALU.is_ge, fill=NEG, base=0,
                                                                  pattern=[[0, 2], [-1, P]], channel_multiplier=1),
                                h_bd[g]))
            h_bias.append(hh)

        h_wo = weight("wo", [P, 8, D], ins["cond_wo"].rearrange("(c p) n -> p c n", p=P), where=top)
        h_gout = weight("gout", [P, 2], ins["g_out"])
        h_awq = weight("awq", [P, 2, D], ins["attn_wq"].rearrange("(c p) n -> p c n", p=P))
        h_bq = weight("bq", [P, D], ins["attn_bq"].rearrange("(o n) -> o n", o=1).broadcast_to([P, D]))
        h_wd = weight("wd", [P, 2, DH], ins["attn_wdown"].rearrange("(c p) n -> p c n", p=P))
        h_bdn = weight("bd", [DH, 1], ins["attn_bdown"].rearrange("(n o) -> n o", o=1))
        wup = sb("w_wup", [DH + 1, 512])
        h_wup = [pr.dma("sync", "w_wup0", wup[0:DH, :], ins["attn_wup"]),
                 pr.dma("sync", "w_wup1", wup[DH:DH + 1, :], ins["attn_bup"].rearrange("(o n) -> o n", o=1))]
        h_wout = weight("wout", [P, 2, D], ins["attn_wout"].rearrange("(c p) n -> p c n", p=P))
        h_bout = weight("bout", [P, D], ins["attn_bout"].rearrange("(o n) -> o n", o=1).broadcast_to([P, D]))
        h_cos = weight("cos", [P, NT, 16], ins["c_cos"])
        h_sin = weight("sin", [P, NT, 16], ins["c_sin"])

        tmpA = sb("prod", [P, 3072])
        wnull = sb("wnull", [P, 2, H])
        nvwo = sb("nvwo", [H, D])
        h_wnull, h_nvwo = [], []

        xnTs = Ring([top(f"xnT{i}", [P, 2, S]) for i in range(2)])
        qring = Ring([top(f"qT{i}", [DH + 1, S]) for i in range(6)])
        oring = Ring([top(f"oTT{i}", [P, S]) for i in range(2)])
        kz = Ring([top(f"kz{i}", [DH + 1, S]) for i in range(2)])
        vt = Ring([top(f"vt{i}", [P, NT, DH]) for i in range(2)])
        snl = Ring([sb(f"snl{i}", [P, NT, H]) for i in range(2)])
        pbuf = Ring([top(f"pb{i}", [P, 1280]) for i in range(4)])
        ptb = Ring([top(f"ptb{i}", [P, 1280]) for i in range(2)])
        mst = Ring([sb(f"mst{i}", [P, 6, 2, NT]) for i in range(4)])
        pnns = Ring([sb(f"pnn{i}", [P, NT, H]) for i in range(2)])
        pnT = Buf(sb("pnT", [H, S]))
        hnb = Buf(sb("hn", [P, NT, D]))
        hT = Buf(sb("hT", [P, 2, S]))
        latT = Buf(sb("latT", [DH + 1, S]))
        qs = Ring([sb(f"qs{i}", [P, D]) for i in range(2)])
        kvs = Ring([sb(f"kvs{i}", [P, H, 32]) for i in range(3)])
        rp = Ring([sb(f"rp{i}", [P, 2, D]) for i in range(2)])
        rt = Buf(sb("rt", [P, D]))
        sc = Ring([sb(f"sc{i}", [P, D]) for i in range(2)])
        sm = Ring([sb(f"sm{i}", [P, 3, H]) for i in range(2)])
        ob = Ring([sb(f"ob{i}", [P, D]) for i in range(2)])
        oT = Ring([sb(f"oT{i}", [P, 2, P]) for i in range(2)])
        xr = Ring([sb(f"xr{i}", [P, D]) for i in range(2)])
        prod = Ring([tmpA[:, i * 1024:(i + 1) * 1024] for i in range(3)])
        lnx = self.ln_make(sb, "lnx", 1)
        lno = self.ln_make(sb, "lno", 2)
        nvb = ob.bufs[0].ap[:, 0:8 * H].rearrange("p (c h) -> p c h", c=8)
        for i, q in enumerate(qring.bufs):
            q.free = [pr.op("vector", "qones", lambda e, q=q: e.memset(q.ap[DH:DH + 1, :], 1.0))]
        self.high1 = sb.high
        self.high1t = top.high
        h_latones = pr.op("vector", "latones", lambda e: e.memset(latT.ap[DH:DH + 1, :], 1.0))

        rS = rT = self.banks(0, 1, 2, 3)
        rM = rO = self.banks(4, 7)
        acc = [Buf(ps[:, k, :]) for k in (5, 6)]
        self.ident_ready = self.h_ident
        state = {}
        flip = [0]

        def fold_key():
            for c in range(2):
                t3 = tmpA[:, c * 1024:(c + 1) * 1024].rearrange("p (h d) -> p h d", h=H)
                q3 = W["wq"][:, c, :].rearrange("p (h d) -> p h d", h=H)
                a = pr.op("vector", "wn0", lambda e, t3=t3, q3=q3: e.tensor_tensor(
                    t3, q3, W["nk"][:, :].unsqueeze(1).broadcast_to([P, H, DH]), ALU.mult), h_wq, h_nk)
                b = pr.op("vector", "wn1", lambda e, t3=t3, c=c: e.tensor_reduce(wnull[:, c, :], t3, AX, ALU.add), a)
                h_wnull.append(pr.op("vector", "wn2", lambda e, c=c: e.tensor_scalar(wnull[:, c, :], wnull[:, c, :], 0.125, None,
                                                                                ALU.mult), b))

        def fold_value():
            h0 = pr.op("vector", "nvb0", lambda e: e.memset(nvb, 0.0))
            hb = []
            for c in range(8):
                for j in range(2):
                    hb.append(pr.op("vector", "nvb", lambda e, c=c, j=j: e.tensor_copy(
                        nvb[DH * j:DH * j + DH, c, 2 * c + j:2 * c + j + 1], nv[DH * j:DH * j + DH, :]), h0, h_nv))
            m = rM.take()
            for c in range(8):
                mm = pr.op("tensor", "nvwo_mm", lambda e, c=c: e.matmul(m.ap[0:H, 0:D], nvb[:, c, :], W["wo"][:, c, :],
                                                                        start=(c == 0), stop=(c == 7)), hb, h_wo, m.free)
            h = pr.op("vector", "nvwo", lambda e: e.tensor_copy(nvwo[:, :], m.ap[0:H, 0:D]), mm)
            m.free = [h]
            ob.bufs[0].free = [mm]
            h_nvwo.append(h)

        def copy_out(sem, out, in_, *after, again=False):
            flip[0] += 0 if again else 1
            if flip[0] % 2:
                return pr.op("vector", sem + "_v", lambda e: e.tensor_copy(out, in_), *after)
            return pr.op("scalar", sem + "_a", lambda e: e.activation(out, in_, ACT.Copy), *after)

        def stage_pre(b):
            st = state[b] = {}
            x = xin.ap
            hx = h_x[b]
            scale = self.ln("lnx", lnx, [x[:, t, :] for t in range(NT)], [x[:, t, :] for t in range(NT)], [hx] * NT, [], later=True)
            yield
            hxn = scale()
            yield
            ev = []
            tr_all = []
            xnT = st["xnT"] = xnTs.take()
            for c in range(2):
                m = rM.take()
                tr = None
                for t in range(NT):
                    tr = pr.op("tensor", "xT", lambda e, c=c, t=t, m=m: e.transpose(
                        m.ap[:, t * P:(t + 1) * P], x[:, t, c * P:(c + 1) * P], self.ident[:, :]),
                        hxn[t], self.h_ident, m.free)
                tr_all.append(tr)
                h = pr.op("scalar", "xnT", lambda e, c=c, m=m: e.activation(
                    xnT.ap[:, c, :], m.ap, ACT.Identity, scale=W["gin"][:, c:c + 1]), tr, h_gin, xnT.free)
                m.free = [h]
                ev.append(h)
                yield
            if b + 1 < NB:
                h_x[b + 1] = pr.dma("sync", "xin", xin.ap[:, :, :], xv[b + 1], tr_all)
            users = []
            i = mrow.n % 2
            m8, k = mrow.take(), kz.take()
            m8r = m8.ap[DH:DH + 1, :]
            hm8 = pr.dma("sync", f"mrow{i}", m8r, ins["mask"][b:b + 1, :].bitcast(U8), m8.free)
            hmk = pr.op("vector", "maskm", lambda e, k=k: e.tensor_scalar(
                k.ap[DH:DH + 1, :], m8r, 1.0, -NEG, ALU.subtract, ALU.mult), hm8, k.free)
            m8.free = [hmk]
            m = rM.take()
            for c in range(2):
                mm = pr.op("tensor", "kmm", lambda e, c=c, m=m: e.matmul(
                    m.ap[0:DH, :], wk[:, c, :], xnT.ap[:, c, :], start=(c == 0), stop=(c == 1)), ev, h_wk, m.free)
            users.append(mm)
            hk = [pr.op("scalar", "kcp", lambda e, m=m, k=k: e.activation(k.ap[0:DH, :], m.ap[0:DH, :], ACT.Copy), mm, k.free)]
            m.free = hk
            st["k"], st["hk"] = k, hk + [hmk]
            yield
            m = rM.take()
            for t in range(NT):
                for c in range(2):
                    mm = pr.op("tensor", "vmm", lambda e, c=c, t=t, m=m: e.matmul(
                        m.ap[:, t * DH:(t + 1) * DH], xnT.ap[:, c, t * P:(t + 1) * P], W["wv"][:, c, :],
                        start=(c == 0), stop=(c == 1)), ev, h_wv, m.free)
                for c in range(2):
                    mm = pr.op("tensor", "vmm", lambda e, c=c, t=t, m=m: e.matmul(
                        m.ap[:, 256 + t * H:256 + (t + 1) * H], xnT.ap[:, c, t * P:(t + 1) * P], wnull[:, c, :],
                        start=(c == 0), stop=(c == 1)), h_wnull)
            users.append(mm)
            v, sn = vt.take(), snl.take()
            hv = pr.op("vector", "vcp", lambda e, m=m, v=v: e.tensor_copy(v.ap[:, :, :], m.ap[:, 0:256]), mm, v.free)
            hs = pr.op("vector", "snl", lambda e, m=m, sn=sn: e.tensor_tensor(
                sn.ap[:, :, :], m.ap[:, 256:256 + NT * H], W["nb"][:, :, :], ALU.add), mm, h_nb, sn.free)
            m.free = [hv, hs]
            st["v"], st["hv"], st["sn"], st["hs"] = v, hv, sn, hs
            yield
            st["ev"], st["q"], st["hq"], st["users"] = ev, [], [], users
            st["pnn"], st["hpnn"], st["kuse"], st["snuse"] = pnns.take(), [], [], []

        def queries(b, p):
            st = state[b]
            xnT = st["xnT"]
            m = rM.take()
            for c in range(2):
                mm = pr.op("tensor", "qmm", lambda e, c=c: e.matmul(
                    m.ap, W["wq"][:, c, p * P:(p + 1) * P], xnT.ap[:, c, :], start=(c == 0), stop=(c == 1)),
                    st["ev"], h_wq, m.free)
            m.free = []
            flip[0] += 1
            for j in range(2):
                q = qring.take()
                if j == 0:
                    h = pr.op("vector", "qcp_v", lambda e, q=q: e.tensor_scalar(
                        q.ap[0:DH, :], m.ap[0:DH, :], 0.125, None, ALU.mult), mm, q.free)
                else:
                    h = pr.op("scalar", "qcp_a", lambda e, q=q: e.activation(
                        q.ap[0:DH, :], m.ap[DH:P, :], ACT.Copy, scale=0.125), mm, q.free)
                q.free = [h]
                m.free.append(h)
                st["q"].append(q)
                st["hq"].append(h)
            if p == 7:
                xnT.free = st["users"] + [mm]

        def scores(b, h):
            st = state[b]
            p, j = h // 2, h % 2
            if j == 0:
                st["ms", p] = mst.take()
            ms = st["ms", p]
            mx, nm, dn, pn, rs, rc = [ms.ap[:, i, :, :] for i in range(6)]
            pb = pbuf.take()
            k, sn, q = st["k"], st["sn"], st["q"][h]
            hm = []
            for t in range(NT):
                n = P * (t + 1)
                m = rS.take()
                mm = pr.op("tensor", "S", lambda e, t=t, n=n, m=m: e.matmul(
                    m.ap[:, 0:n], q.ap[:, t * P:(t + 1) * P], k.ap[:, 0:n], start=True, stop=True),
                    st["hq"][h], st["hk"], m.free)
                hh = pr.op("vector", "ttr", lambda e, t=t, n=n, m=m: e.tensor_tensor_reduce(
                    pb.ap[:, CAUSAL[t]:CAUSAL[t + 1]], m.ap[:, 0:n], bias[:, h, CAUSAL[t]:CAUSAL[t + 1]],
                    1.0, sn.ap[:, t, h:h + 1], ALU.add, ALU.max, mx[:, j, t:t + 1]),
                    mm, h_bias[h // 2], st["hs"], pb.free, ms.free)
                m.free = [hh]
                hm.append(hh)
                if t < NT - 1:
                    yield
            q.free = [mm]
            if h == H - 1:
                k.free = [mm]
            hn_ = pr.op("vector", "nm", lambda e: e.tensor_scalar(nm[:, j, :], mx[:, j, :], -1.0, None, ALU.mult), hm, ms.free)
            hd = pr.op("vector", "dn", lambda e: e.tensor_tensor(dn[:, j, :], sn.ap[:, :, h], nm[:, j, :], ALU.add), hn_, ms.free)
            if h == H - 1:
                sn.free = [hd]
            he = [pr.op("scalar", "exp", lambda e, t=t: e.activation(
                pb.ap[:, CAUSAL[t]:CAUSAL[t + 1]], pb.ap[:, CAUSAL[t]:CAUSAL[t + 1]], ACT.Exp,
                bias=nm[:, j, t:t + 1], accum_out=rs[:, j, t:t + 1]), hm, hn_, ms.free) for t in range(NT)]
            hp = pr.op("scalar", "pn", lambda e: e.activation(pn[:, j, :], dn[:, j, :], ACT.Exp), hd, ms.free)
            st["P", h] = (pb, he, hp)
            yield

        def normal(b, h):
            st = state[b]
            p, j = h // 2, h % 2
            ms = st["ms", p]
            mx, nm, dn, pn, rs, rc = [ms.ap[:, i, :, :] for i in range(6)]
            pb, he, hp = st["P", h]
            h1 = pr.op("vector", "den", lambda e: e.tensor_tensor(dn[:, j, :], rs[:, j, :], pn[:, j, :], ALU.add), he, hp)
            h2 = pr.op("vector", "rden", lambda e: e.reciprocal(rc[:, j, :], dn[:, j, :]), h1, ms.free if j == 0 else [])
            h3 = pr.op("vector", "pnn", lambda e: e.tensor_tensor(st["pnn"].ap[:, :, h], pn[:, j, :], rc[:, j, :], ALU.mult),
                       h2, st["pnn"].free)
            st["hpnn"].append(h3)
            hg = [pr.op("scalar", "pnorm", lambda e, t=t: e.activation(
                pb.ap[:, CAUSAL[t]:CAUSAL[t + 1]], pb.ap[:, CAUSAL[t]:CAUSAL[t + 1]], ACT.Identity,
                scale=rc[:, j, t:t + 1]), h2) for t in range(NT)]
            st["hg", h] = hg
            if j == 1:
                ms.free = [st["h3", p], h3, st["hg", h - 1], hg]
            else:
                st["h3", p] = h3

        def turn(b, h):
            st = state[b]
            pb = st["P", h][0]
            hg = st["hg", h]
            pt = ptb.take()
            out = []
            tr = None
            for lot in ([(0, t) for t in range(4)], [(1, t) for t in range(1, 4)] + [(3, 3)], [(2, 2), (2, 3)]):
                m = rT.take()
                for i, (kt, t) in enumerate(lot):
                    tr = pr.op("tensor", "PT", lambda e, i=i, kt=kt, t=t, m=m: e.transpose(
                        m.ap[:, i * P:(i + 1) * P], pb.ap[:, CAUSAL[t] + kt * P:CAUSAL[t] + (kt + 1) * P],
                        self.ident[:, :]), hg[t], self.h_ident, m.free)
                kt0, t0 = lot[0]
                n0 = len([1 for kt, _ in lot if kt == kt0]) * P
                ho = [copy_out("ptc", pt.ap[:, KEYCOL[kt0]:KEYCOL[kt0] + n0], m.ap[:, 0:n0], tr, pt.free)]
                if n0 < len(lot) * P:
                    ho.append(copy_out("ptc", pt.ap[:, KEYCOL[3]:KEYCOL[4]], m.ap[:, n0:n0 + P], tr, pt.free, again=True))
                m.free = ho
                out += ho
                yield
            pb.free = [tr]
            st["PT", h] = (pt, out)

        def values(b, p):
            st = state[b]
            m = rO.take()
            v = st["v"]
            mm = None
            last = []
            for kt in range(NT):
                for j in range(2):
                    pt, hp = st["PT", 2 * p + j]
                    mm = pr.op("tensor", "O", lambda e, kt=kt, j=j, pt=pt, m=m: e.matmul(
                        m.ap[DH * j:DH * j + DH, kt * P:S], v.ap[:, kt, :], pt.ap[:, KEYCOL[kt]:KEYCOL[kt + 1]],
                        start=(kt == 0), stop=(kt == NT - 1), tile_position=(0, DH * j)), hp, st["hv"], m.free)
            for j in range(2):
                st["PT", 2 * p + j][0].free = [mm]
            if p == 7:
                v.free = [mm]
            o = oring.take()
            h = copy_out("oc", o.ap[:, :], m.ap, mm, o.free)
            m.free = [h]
            st["O", p] = (o, h)

        def project(b, p):
            o, h = state[b]["O", p]
            for t in range(NT):
                a = acc[t // 2]
                mm = pr.op("tensor", "wo", lambda e, t=t, a=a: e.matmul(
                    a.ap[:, t % 2 * D:(t % 2 + 1) * D], o.ap[:, t * P:(t + 1) * P], W["wo"][:, p, :],
                    start=(p == 0 and t % 2 == 0), stop=False, skip_group_check=True), h, h_wo, a.free)
            o.free = [mm]

        def finish(b):
            st = state[b]
            pnn = st["pnn"]
            m = rM.take()
            for t in range(NT):
                tr = pr.op("tensor", "pnT_t", lambda e, t=t: e.transpose(
                    m.ap[0:H, t * P:(t + 1) * P], pnn.ap[:, t, :], self.ident[:, :]), st["hpnn"], m.free)
            pnn.free = [tr]
            hp = pr.op("vector", "pnT", lambda e: e.tensor_copy(pnT.ap[:, :], m.ap[0:H, :]), tr, pnT.free)
            m.free = [hp]
            yield
            st["hn"], scale = [], []
            for u in range(2):
                a = acc[u]
                for i in range(2):
                    mm = pr.op("tensor", "wo", lambda e, t=2 * u + i, i=i, a=a: e.matmul(
                        a.ap[:, i * D:(i + 1) * D], pnT.ap[:, t * P:(t + 1) * P], nvwo[:, :], start=False, stop=True,
                        skip_group_check=True), hp, h_nvwo)
                scale.append(self.ln("lno", lno, [a.ap[:, 0:D], a.ap[:, D:2 * D]],
                                     [hnb.ap[:, 2 * u, :], hnb.ap[:, 2 * u + 1, :]], [mm, mm], hnb.free, later=True))
                yield
            for u in range(2):
                acc[u].free = scale[u]()
                st["hn"] += acc[u].free
                yield
            pnT.free = [mm]

        def step(n):
            at = lambda k: (k // H, k % H)
            none = iter(())
            sc_ = scores(*at(n)) if n < NB * H else none
            pt_ = turn(*at(n - 3)) if 3 <= n and n - 3 < NB * H else none
            if n < H // 2:
                causal(n)
            next(sc_, None)
            if n % 2 == 1 and n >= 5 and n - 4 < NB * H:
                b, h = at(n - 4)
                values(b, h // 2)
            yield
            next(sc_, None)
            next(pt_, None)
            yield
            if n % 2 == 0 and n + 4 < NB * H:
                b, h = at(n + 4)
                queries(b, h // 2)
            yield
            if 1 <= n <= NB * H:
                normal(*at(n - 1))
            next(sc_, None)
            next(pt_, None)
            yield
            next(sc_, None)
            if n % 2 == 0 and n >= 6 and n - 5 < NB * H:
                b, h = at(n - 5)
                project(b, h // 2)
                if h == H - 1:
                    yield from finish(b)
            yield
            for _ in sc_:
                pass
            for _ in pt_:
                pass
            yield

        def stage_heads(b):
            st = state[b]
            ev, trs = [], []
            for c in range(2):
                m = rM.take()
                for t in range(NT):
                    tr = pr.op("tensor", "hT_t", lambda e, c=c, t=t, m=m: e.transpose(
                        m.ap[:, t * P:(t + 1) * P], hnb.ap[:, t, c * P:(c + 1) * P], self.ident[:, :]), st["hn"], m.free)
                h = pr.op("scalar", "hT", lambda e, c=c, m=m: e.activation(
                    hT.ap[:, c, :], m.ap, ACT.Identity, scale=W["gout"][:, c:c + 1]), tr, h_gout, hT.free)
                m.free = [h]
                ev.append(h)
                yield
            hnb.free = [tr]
            m = rM.take()
            for c in range(2):
                mm = pr.op("tensor", "lat", lambda e, c=c, m=m: e.matmul(
                    m.ap[0:DH, :], W["wd"][:, c, :], hT.ap[:, c, :], start=(c == 0), stop=(c == 1)), ev, h_wd, m.free)
            hl = pr.op("scalar", "latT", lambda e, m=m: e.activation(
                latT.ap[0:DH, :], m.ap[0:DH, :], ACT.Identity, bias=W["bd"][:, :]), mm, h_bdn, latT.free)
            m.free = [hl]
            yield
            ho = []
            W_ = {}

            def front(t):
                m = rM.take()
                for c in range(2):
                    mq = pr.op("tensor", "q2", lambda e, c=c: e.matmul(
                        m.ap[:, 0:D], hT.ap[:, c, t * P:(t + 1) * P], W["awq"][:, c, :], start=(c == 0), stop=(c == 1)),
                        ev, h_awq, m.free)
                q = qs.take()
                hq = pr.op("vector", "q2b", lambda e, m=m: e.tensor_tensor(
                    q.ap[:, :], m.ap[:, 0:D], W["bq"][:, :], ALU.add), mq, h_bq, q.free)
                m.free = [hq]
                yield
                m2 = rM.take()
                mk = pr.op("tensor", "kv2", lambda e: e.matmul(
                    m2.ap, latT.ap[:, t * P:(t + 1) * P], wup[:, :], start=True, stop=True), hl, h_latones, h_wup, m2.free)
                kv = kvs.take()
                hkv = pr.op("scalar", "kv2c", lambda e: e.activation(kv.ap[:, :, :], m2.ap, ACT.Copy), mk, kv.free)
                m2.free = [hkv]
                W_["mq"], W_["mk"] = mq, mk
                yield
                r = rp.take()
                cosb = W["cos"][:, t, :].unsqueeze(1).broadcast_to([P, H, 16])
                sin = W["sin"][:, t, :]
                rot = []
                t2 = rt.ap[:, :].rearrange("p (h d) -> p h d", h=H)
                for i, (src, ready) in enumerate(((q.ap[:, :].rearrange("p (h d) -> p h d", h=H), hq),
                                                  (kv.ap[:, :, 0:16], hkv))):
                    t1 = r.ap[:, i, :].rearrange("p (h d) -> p h d", h=H)
                    a = pr.op("gpsimd", "rot1", lambda e, t1=t1, src=src: e.tensor_tensor(t1, src, cosb, ALU.mult),
                              ready, h_cos, r.free)
                    bb = [pr.op("gpsimd", "rot2", lambda e, src=src, u=u: e.tensor_tensor(
                        t2[:, :, 8 * u:8 * u + 8], src[:, :, 8 - 8 * u:16 - 8 * u],
                        sin[:, 8 * u:8 * u + 8].unsqueeze(1).broadcast_to([P, H, 8]), ALU.mult),
                        ready, h_sin, rt.free) for u in range(2)]
                    rot.append(pr.op("gpsimd", "rot3", lambda e, t1=t1: e.tensor_tensor(t1, t1, t2, ALU.add), a, bb))
                    rt.free = [rot[-1]]
                    yield
                q.free, r.free, kv.free = [rot[0]], [], [rot[1]]
                W_[t] = dict(kv=kv, hkv=hkv, r=r, rot=rot)

            def middle(t):
                w = W_[t]
                kv, hkv, r, rot = w["kv"], w["hkv"], w["r"], w["rot"]
                q3 = r.ap[:, 0, :].rearrange("p (h d) -> p h d", h=H)
                k3 = r.ap[:, 1, :].rearrange("p (h d) -> p h d", h=H)
                s, mm_ = sc.take(), sm.take()
                s3 = s.ap[:, :].rearrange("p (h g) -> p h g", h=H)
                hr, late = [], None
                for u in range(4):
                    pv = prod.take()
                    pva = pv.ap.rearrange("p (h g d) -> p h g d", h=4, g=H)
                    eng, sem = HS_ENG[b == NB - 1][u]
                    hm = pr.op(eng, "hs_m" + sem, lambda e, u=u, pva=pva: e.tensor_tensor(
                        pva, q3[:, 4 * u:4 * u + 4, :].unsqueeze(2).broadcast_to([P, 4, H, 16]),
                        k3.unsqueeze(1).broadcast_to([P, 4, H, 16]), ALU.mult), rot, pv.free)
                    r.free.append(hm)

                    def reduce(u=u, pv=pv, pva=pva, hm=hm):
                        hr.append(pr.op("vector", "hs_r", lambda e: e.tensor_reduce(
                            s3[:, 4 * u:4 * u + 4, :], pva, AX, ALU.add), hm, s.free))
                        pv.free = [hr[-1]]

                    if late:
                        late()
                    late = reduce
                    yield
                late()
                a = pr.op("vector", "hs_x", lambda e: e.tensor_reduce(mm_.ap[:, 0, :], s3, AX, ALU.max), hr, mm_.free)
                a = pr.op("vector", "hs_d", lambda e: e.tensor_tensor(
                    s3, s3, mm_.ap[:, 0, :].unsqueeze(2).broadcast_to([P, H, H]), ALU.subtract), a)
                he = pr.op("scalar", "hs_e", lambda e: e.activation(s.ap[:, :], s.ap[:, :], ACT.Exp, scale=0.25), a)
                yield
                a = pr.op("vector", "hs_s", lambda e: e.tensor_reduce(mm_.ap[:, 1, :], s3, AX, ALU.add), he, mm_.free)
                hrc = pr.op("vector", "hs_c", lambda e: e.reciprocal(mm_.ap[:, 2, :], mm_.ap[:, 1, :]), a, mm_.free)
                yield
                v3 = kv.ap[:, :, 16:32].rearrange("p g d -> p d g")
                o = ob.take()
                o3 = o.ap[:, :].rearrange("p (h d) -> p h d", h=H)
                hr, late = [], None
                s.free = [a]
                for u in range(4):
                    pg = prod.take()
                    pga = pg.ap.rearrange("p (h d g) -> p h d g", h=4, g=H)
                    eng, sem = HV_ENG[b == NB - 1][u]
                    hm = pr.op(eng, "hv_m" + sem, lambda e, u=u, pga=pga: e.tensor_tensor(
                        pga, s3[:, 4 * u:4 * u + 4, :].unsqueeze(2).broadcast_to([P, 4, 16, H]),
                        v3.unsqueeze(1).broadcast_to([P, 4, 16, H]), ALU.mult), he, hkv, pg.free)
                    s.free.append(hm)
                    kv.free.append(hm)

                    def reduce(u=u, pg=pg, pga=pga, hm=hm):
                        hr.append(pr.op("vector", "hv_r", lambda e: e.tensor_reduce(
                            o3[:, 4 * u:4 * u + 4, :], pga, AX, ALU.add), hm, o.free))
                        pg.free = [hr[-1]]

                    if late:
                        late()
                    late = reduce
                    yield
                late()
                hn_ = pr.op("vector", "hv_n", lambda e: e.tensor_tensor(
                    o3, o3, mm_.ap[:, 2, :].unsqueeze(2).broadcast_to([P, H, 16]), ALU.mult), hr, hrc)
                mm_.free = [hn_]
                o.free = []
                w["o"], w["hn"] = o, hn_

            def back(t):
                w = W_[t]
                o, hn_ = w["o"], w["hn"]
                m = rM.take()
                for c in range(2):
                    tr = pr.op("tensor", "oT_t", lambda e, c=c: e.transpose(
                        m.ap[:, c * P:(c + 1) * P], o.ap[:, c * P:(c + 1) * P], self.ident[:, :]), hn_, m.free)
                o.free = [tr]
                ot = oT.take()
                hc = pr.op("scalar", "oT", lambda e, m=m: e.activation(
                    ot.ap[:, :, :], m.ap[:, 0:D].rearrange("p (c k) -> p c k", c=2), ACT.Copy), tr, ot.free)
                m.free = [hc]
                xb = xr.take()
                i = b * NT + t
                hx = pr.dma("sync", f"xr{i % 2}", xb.ap[:, :], ins["x"][b, t * P:(t + 1) * P, :], xb.free)
                hx = pr.op("gpsimd", "xb", lambda e: e.tensor_tensor(xb.ap[:, :], xb.ap[:, :], W["bout"][:, :], ALU.add),
                           hx, h_bout)
                yield
                yield
                m2 = rM.take()
                for c in range(2):
                    mm = pr.op("tensor", "wout", lambda e, c=c: e.matmul(
                        m2.ap[:, 0:D], ot.ap[:, c, :], W["wout"][:, c, :], start=(c == 0), stop=(c == 1)),
                        hc, h_wout, m2.free)
                ot.free = [mm]
                h1 = pr.op("vector", "x1", lambda e: e.tensor_tensor(
                    xb.ap[:, :], m2.ap[:, 0:D], xb.ap[:, :], ALU.add), mm, hx)
                m2.free = [h1]
                hd = pr.dma("sync", f"x1d{i % 2}", self.x1d[i], xb.ap[:, :], h1)
                xb.free = [hd]
                ho.append(hd)
                yield

            for i in range(NT + 2):
                parts = []
                if i >= 2:
                    parts.append((back(i - 2), 3))
                if i < NT:
                    parts.append((front(i), 4))
                if 1 <= i <= NT:
                    parts.append((middle(i - 1), 11))
                yield from weave(*parts)
            mq, mk = W_["mq"], W_["mk"]
            hT.free = [mq]
            latT.free = [mk]
            self.x1_done[b] = ho

        self.x1_done = {}
        first = stage_pre(0)
        next(first)
        next(first)
        fold_key()
        for _ in first:
            pass
        fold_value()
        queries(0, 0)
        queries(0, 1)
        side, heads = [], None
        for n in range(NB * H + 6):
            if n == H:
                self.clear_slots(ob.bufs[1].ap)
                ob.bufs[1].free = [self.zeroed, self.ezeroed]
            if n % H == 1 and n // H + 1 < NB:
                side.append([stage_pre(n // H + 1), 0.18, 0.0])
            if n >= H + 5 and (n - 5) % H == 0:
                for _ in heads[0] if heads else ():
                    pass
                heads = [stage_heads((n - 5) // H - 1), 0.5, 0.0]
                side.append(heads)
            for _ in step(n):
                for x in side:
                    x[2] += x[1]
                    while x[2] >= 1.0:
                        x[2] -= 1.0
                        next(x[0], None)
        pr.fence()
        self.moe = self.experts()
        next(self.moe)
        early, due = True, EARLY_START
        for _ in heads[0]:
            due += EARLY_RATE
            while early and due >= 1.0:
                due -= 1.0
                early = next(self.moe) != "all tokens"
        while early:
            early = next(self.moe) != "all tokens"

    def row(self, v):
        return v.rearrange("(o n) -> o n", o=1).broadcast_to([P, v.shape[0]])

    def phase2(self):
        self.pr.fence()
        for _ in self.moe:
            pass
        self.pr.fence()
        self.mha()

    def experts(self):
        nc, pr, ins, ps = self.nc, self.pr, self.ins, self.ps
        E, M, NN = 8, 128, NB * NT
        NS = 2 * NN + E
        sb, low = Arena(nc, self.split, self.hi), Arena(nc, self.base + 17 * 1024, self.split)
        I32 = mybir.dt.int32
        self.yd = nc.dram_tensor("y_scratch", [NN, P, D], F32).ap()
        self.yed = nc.dram_tensor("ye_scratch", [NS * P, D], F32).ap()
        regs = {}

        def weight(name, sem, shape, src):
            t = sb("ew_" + name, shape)
            return t, pr.dma("scalar", sem, t[tuple(slice(None) for _ in shape)], src)

        wt, h1 = weight("wt", "ew_r", [P, 2, E], ins["moe_wt"].rearrange("(c p) e -> p c e", p=P))
        wg, h2 = weight("wg", "ew_r", [DH, E], ins["moe_wg"])
        cT, h3 = weight("cT", "ew_r", [DH, NB], ins["condT"][:, 0:NB])
        before, h4 = weight("before", "ew_r", [P, E, E], ins["c_before"])
        h_router = [h1, h2, h3, h4]
        x1 = sb("e_x1", [P, NN, D])
        h_x1 = {}

        def fetch_x1(eng, b):
            h_x1[b] = pr.dma(eng, f"e_x1{b}", x1[:, b * NT:(b + 1) * NT, :], self.x1d[b * NT:(b + 1) * NT].rearrange("t p d -> p t d"),
                             self.x1_done[b])

        for b in range(NB - 1):
            fetch_x1("scalar", b)
        sg, h1 = weight("sg", "ew_s", [P, 2, 2 * M], ins["sh_gate"].rearrange("(c p) m -> p c m", p=P))
        su, h2 = weight("su", "ew_s", [P, 2, 2 * M], ins["sh_up"].rearrange("(c p) m -> p c m", p=P))
        sd, h3 = weight("sd", "ew_s", [P, 2, D], ins["sh_down"].rearrange("(c p) m -> p c m", p=P))
        h_shared = [h1, h2, h3]
        upper, h1 = weight("upper", "ew_t", [P, P], ins["c_upper"])
        thr, h2 = weight("thr", "ew_t", [P, 2 * NN], ins["c_thr"][:, 0:2 * NN])
        iota, h3 = weight("iota", "ew_t", [P, NS], ins["c_iota"][:, 0:NS])
        h_tables = [h1, h2, h3]
        gu = sb("ew_gu", [P, E, 2 * 2 * M])
        dn = sb("ew_dn", [P, E, D])
        h_gu, h_dn = [], []
        yield
        ones = sb("e_ones", [P, P])
        h_ones = pr.op("vector", "e_ones", lambda e: e.memset(ones[:, :], 1.0))
        xT = sb("e_xT", [P, NB, 2, S])
        GB = max(1, NB // 2)
        GT = GB * NT
        lg = sb("e_lg", [P, NN, E])
        sm = sb("e_sm", [P, 4, NN])
        cmp_ = sb("e_cmp", [P, 2, GT, E, E])
        gt = sb("e_gt", [P, NN, E])
        oh = sb("e_oh", [P, 2, NN, E])
        lk = Ring([sb(f"e_lk{i}", [P, 2, S]) for i in range(2)])
        aT = Ring([sb(f"e_aT{i}", [P, S]) for i in range(3)])
        yb = Ring([sb(f"e_y{i}", [P, NT, D]) for i in range(2)])
        tei = low("e_tei", [P, NS], I32)
        xs = Ring([low(f"e_xs{i}", [P, 2, D]) for i in range(4)])
        sT = Ring([low(f"e_sT{i}", [P, 2, 2, P]) for i in range(3)])
        kk = Ring([low(f"e_kk{i}", [P, 2, 2, M]) for i in range(3)])
        aS = Ring([low(f"e_aS{i}", [P, 2, P]) for i in range(3)])
        ys = Ring([low(f"e_ys{i}", [P, 2, D]) for i in range(3)])
        bank = [Buf(ps[:, k, :]) for k in range(8)]
        rR, rL, rG, rU, rD = ring_of(bank[0]), ring_of(bank[2]), ring_of(bank[1], bank[3]), ring_of(bank[5], bank[6]), ring_of(bank[0])
        state = {}
        lgT = Ring([sb(f"e_lgT{i}", [E, S]) for i in range(2)])
        cs = sb("e_cs", [E, NB])
        m = rR.take()
        mm = pr.op("tensor", "e_cs", lambda e: e.matmul(m.ap[0:E, 0:NB], wg[:, :], cT[:, :], start=True, stop=True), h_router)
        h_cs = pr.op("scalar", "e_csc", lambda e: e.activation(cs[:, :], m.ap[0:E, 0:NB], ACT.Copy, scale=0.5), mm)
        m.free = [h_cs]
        h_oh, h_cmp, late = [], [], []

        def turn(b):
            ev = []
            for c in range(2):
                m = rR.take()
                for t in range(NT):
                    tr = pr.op("tensor", "e_tr", lambda e, c=c, t=t, m=m: e.transpose(
                        m.ap[:, t * P:(t + 1) * P], x1[:, b * NT + t, c * P:(c + 1) * P], self.ident[:, :]), h_x1[b], m.free)
                h = pr.op("scalar", "e_xT", lambda e, c=c, m=m: e.activation(xT[:, b, c, :], m.ap, ACT.Copy), tr)
                m.free = [h]
                ev.append(h)
            state[b] = ev

        def score(b):
            m = rR.take()
            for c in range(2):
                mm = pr.op("tensor", "e_lg", lambda e, c=c: e.matmul(
                    m.ap[0:E, :], wt[:, c, :], xT[:, b, c, :], start=(c == 0), stop=(c == 1)), state[b], h_router, m.free)
            l = lgT.take()
            h = pr.op("scalar", "e_lgT", lambda e: e.activation(
                l.ap[:, :], m.ap[0:E, :], ACT.Identity, bias=cs[:, b:b + 1], scale=0.5), mm, h_cs, l.free)
            m.free = [h]
            return l, h

        def score_back(l, h, k, m):
            for t in range(NT):
                tr = pr.op("tensor", "e_lgb", lambda e, t=t: e.transpose(
                    m.ap[:, (k * NT + t) * E:(k * NT + t + 1) * E], l.ap[:, t * P:(t + 1) * P], self.ident[0:E, 0:E]), h, m.free)
            l.free = [tr]
            return tr

        def route(k):
            m = rL.take()
            for i in range(GB):
                b = k * GB + i
                if b == NB - 1:
                    yield "all tokens"
                    fetch_x1("sync", b)
                    for r, ks in ((rR, (0, 4)), (rD, (7, 0))):
                        r.bufs, r.n = [bank[x] for x in ks], 0
                turn(b)
                yield
                l, h = score(b)
                yield
                tr = score_back(l, h, i, m)
                yield
            n0, n1 = k * GT, (k + 1) * GT
            lv, gv = lg[:, n0:n1, :], gt[:, n0:n1, :]
            h = pr.op("vector", "e_lgc", lambda e: e.tensor_copy(
                lv, m.ap[:, 0:GT * E].rearrange("p (t e) -> p t e", t=GT)), tr)
            m.free = [h]
            yield
            yield from choose(k, lv, gv, h)

        def choose(k, lv, gv, h):
            n0, n1 = k * GT, (k + 1) * GT
            v = lambda fn, *after: pr.op("vector", "e_r", fn, *after)
            col = lambda i: sm[:, i, n0:n1]
            wide = lambda i: sm[:, i, n0:n1].unsqueeze(2).broadcast_to([P, GT, E])
            a = v(lambda e: e.tensor_reduce(col(0), lv, AX, ALU.max), h)
            a = v(lambda e: e.tensor_tensor(lv, lv, wide(0), ALU.subtract), a)
            h = pr.op("scalar", "e_exp", lambda e: e.activation(lv, lv, ACT.Exp), a)
            yield
            a = v(lambda e: e.tensor_reduce(col(1), lv, AX, ALU.add), h)
            a = v(lambda e: e.reciprocal(col(2), col(1)), a)
            a = v(lambda e: e.tensor_tensor(lv, lv, wide(2), ALU.mult), a)
            c0, c1 = cmp_[:, 0, :, :, :], cmp_[:, 1, :, :, :]
            oth = lv.unsqueeze(2).broadcast_to([P, GT, E, E])
            own = lv.unsqueeze(3).broadcast_to([P, GT, E, E])
            prior = before[:, :, :].unsqueeze(1).broadcast_to([P, GT, E, E])
            k2 = v(lambda e: e.tensor_tensor(c1, oth, own, ALU.is_equal), a, h_cmp)
            k1 = v(lambda e: e.tensor_tensor(c0, oth, own, ALU.is_gt), a, h_cmp)
            yield
            k3 = v(lambda e: e.tensor_tensor(c1, c1, prior, ALU.mult), k2, h_router)
            k4 = v(lambda e: e.tensor_tensor(c0, c0, c1, ALU.add), k1, k3)
            a = v(lambda e: e.tensor_reduce(gv, c0, AX, ALU.add), k4)
            h_cmp[:] = [a]
            yield
            o1, o2 = oh[:, 0, n0:n1, :], oh[:, 1, n0:n1, :]
            h1 = v(lambda e: e.tensor_scalar(o1, gv, 0.5, None, ALU.is_lt), a)
            h2 = v(lambda e: e.tensor_scalar(o2, gv, 1.0, None, ALU.is_equal), a)
            h_oh.extend([h1, h2])
            late.append((k, lv, gv, h1, h2))
            yield

        def gate(k, lv, gv, h1, h2):
            n0, n1 = k * GT, (k + 1) * GT
            v = lambda fn, *after: pr.op("vector", "e_r", fn, *after)
            o1, o2 = oh[:, 0, n0:n1, :], oh[:, 1, n0:n1, :]
            col = lambda i: sm[:, i, n0:n1]
            gates = [self.egate[:, u * NN + n0:u * NN + n1] for u in range(2)]
            a = []
            for u, o in enumerate((o1, o2)):
                a = v(lambda e, o=o: e.tensor_tensor(gv, o, lv, ALU.mult), h1, h2, a)
                a = v(lambda e, u=u: e.tensor_reduce(gates[u], gv, AX, ALU.add), a)
            a = v(lambda e: e.tensor_tensor(col(3), gates[0], gates[1], ALU.add), a)
            a = v(lambda e: e.tensor_scalar(col(3), col(3), 1e-20, None, ALU.add), a)
            a = v(lambda e: e.reciprocal(col(2), col(3)), a)
            for u in range(2):
                v(lambda e, u=u: e.tensor_tensor(gates[u], gates[u], col(2), ALU.mult), a)

        def shared():
            gated, parts = {}, {}

            def products(i):
                b, u = i // 2, i % 2
                mg, mu = rG.take(), rU.take()
                for w, m in ((sg, mg), (su, mu)):
                    for c in range(2):
                        mm = pr.op("tensor", "e_sh", lambda e, c=c, w=w, m=m: e.matmul(
                            m.ap, w[:, c, u * M:(u + 1) * M], xT[:, b, c, :], start=(c == 0), stop=(c == 1)),
                            state[b], h_shared, m.free)
                k = lk.take()
                h = pr.op("scalar", "e_lk", lambda e: e.activation(k.ap[:, 0, :], mg.ap, ACT.Copy, scale=0.01), mm, k.free)
                gated[i] = mg, mu, k, mm, h

            def gating(i):
                mg, mu, k, mm, h = gated.pop(i)
                a = aT.take()
                h = pr.op("vector", "e_mx", lambda e: e.tensor_tensor(k.ap[:, 1, :], mg.ap, k.ap[:, 0, :], ALU.max), h)
                mg.free = [h]
                h = pr.op("vector", "e_ml", lambda e: e.tensor_tensor(a.ap[:, :], mu.ap, k.ap[:, 1, :], ALU.mult), mm, h, a.free)
                mu.free, k.free = [h], [h]
                parts[i] = a, h

            def output(b):
                two = [parts.pop(2 * b + u) for u in range(2)]
                y = yb.take()
                hy = []
                for v in range(2):
                    m = rD.take()
                    for i in range(2):
                        for u in range(2):
                            a, ha = two[u]
                            mm = pr.op("tensor", "e_d", lambda e, a=a, t=2 * v + i, i=i, u=u, m=m: e.matmul(
                                m.ap[:, i * D:(i + 1) * D], a.ap[:, t * P:(t + 1) * P], sd[:, u, :], start=(u == 0), stop=(u == 1)),
                                ha, h_shared, m.free)
                    h = pr.op("scalar", "e_y0", lambda e, v=v, m=m: e.activation(
                        y.ap[:, 2 * v:2 * v + 2, :], m.ap.rearrange("p (t d) -> p t d", t=2), ACT.Copy), mm, y.free)
                    m.free = [h]
                    hy.append(h)
                for a, _ in two:
                    a.free = [mm]
                hd = pr.dma("sync", f"e_yd{b % 2}", self.yd[b * NT:(b + 1) * NT].rearrange("t p d -> p t d"), y.ap[:, :, :], hy)
                y.free = [hd]
                self.y_done[b] = [hd]

            for i in range(2 * NB + 2):
                if i < 2 * NB:
                    products(i)
                if 1 <= i <= 2 * NB:
                    gating(i - 1)
                if i >= 3 and i % 2 == 1:
                    output((i - 3) // 2)
                yield

        self.y_done = {}
        after = shared()
        GR = NB // GB
        for k in range(GR - 1):
            yield from route(k)
        last = route(GR - 1)
        for x in last:
            if x == "all tokens":
                break
            yield
        for _ in range(min(EARLY_SHARED, 2 * NB - 2)):
            next(after)
            yield
        for x in range(E):
            g4 = gu[:, x, :].rearrange("p (c k m) -> p c k m", c=2, k=2)
            h_gu += [pr.dma("scalar", "ew_g", g4[:, :, 0, :], ins["moe_gate"][x].rearrange("(c p) m -> p c m", p=P)),
                     pr.dma("scalar", "ew_g", g4[:, :, 1, :], ins["moe_up"][x].rearrange("(c p) m -> p c m", p=P))]
            h_dn.append(pr.dma("scalar", "ew_d", dn[:, x, :], ins["moe_down"][x]))
        yield "all tokens"
        for _ in range(4):
            next(last)
        for _ in last:
            next(after, None)
        flat_oh = oh[:, :, :, :].rearrange("p u t x -> p (u t) x")
        for _ in self.slots(low, "e", flat_oh, h_oh, 2 * NN, self.epos, tei, rR, (upper, h_tables), (ones, h_ones),
                            (before, h_router), (thr, h_tables), (iota, h_tables)):
            next(after, None)
        h_pos, h_te = self.slotted["e"]
        last = pr.op("vector", "e_te1", lambda e: e.tensor_copy(tei[:, NS - 1:NS], tei[:, NS - 2:NS - 1]), h_te)
        h_te = [h_te, last]
        h_sc = [pr.put("gpsimd", "e_sc", lambda e, n=n, u=u: e.indirect_dma_start(
            self.xed, bass.IndirectOffsetOnAxis(ap=self.epos[:, u * NN + n:u * NN + n + 1], axis=0), x1[:, n, :], None),
            16, h_pos, self.ezeroed) for n in range(NN) for u in range(2)]
        for g in late:
            gate(*g)
        for _ in after:
            pass
        rD.bufs, rD.n = [bank[7], bank[2]], 0
        self.fetch_mha(Arena(nc, self.base, self.base + 17 * 1024))

        def fetch(j):
            x = xs.take()
            h = pr.dma("sync", f"e_xs{j % 4}", x.ap[:, :, :], self.xed[2 * j * P:2 * (j + 1) * P, :].rearrange("(u p) d -> p u d", p=P),
                       h_sc, x.free)
            return x, h

        def arrive(j, x, h):
            m = rR.take()
            for u in range(2):
                for c in range(2):
                    tr = pr.op("tensor", "e_sT_t", lambda e, c=c, u=u: e.transpose(
                        m.ap[:, (2 * u + c) * P:(2 * u + c + 1) * P], x.ap[:, u, c * P:(c + 1) * P], self.ident[:, :]), h, m.free)
            x.free = [tr]
            t = sT.take()
            h = pr.op("scalar", "e_sT", lambda e: e.activation(
                t.ap[:, :, :, :], m.ap.rearrange("p (u c k) -> p u c k", u=2, c=2), ACT.Copy), tr, t.free)
            m.free = [h]
            return t, h

        def inner(j, t, h):
            for u in range(2):
                def emit(e, u=u):
                    regs[j, u] = e.value_load(tei[0:1, 2 * j + u:2 * j + u + 1], min_val=0, max_val=E - 1)
                pr.put("tensor", None, emit, 0, h_te)
            m = rG.take()
            for u in range(2):
                for c in range(2):
                    mm = pr.op("tensor", "e_gu", lambda e, c=c, u=u: e.matmul(
                        m.ap[:, u * D:(u + 1) * D], t.ap[:, u, c, :],
                        gu[:, bass.ds(regs[j, u], 1), c * D:(c + 1) * D].rearrange("p o f -> p (o f)"),
                        start=(c == 0), stop=(c == 1)), h, h_gu, m.free)
            t.free = [mm]
            q = kk.take()
            m4 = m.ap.rearrange("p (u k m) -> p u k m", u=2, k=2)
            h1 = pr.op("scalar", "e_lk", lambda e: e.activation(q.ap[:, 0, :, :], m4[:, :, 0, :], ACT.Copy, scale=0.01), mm, q.free)
            h2 = pr.op("vector", "e_mx", lambda e: e.tensor_tensor(q.ap[:, 1, :, :], m4[:, :, 0, :], q.ap[:, 0, :, :], ALU.max), h1, q.free)
            h3 = pr.op("vector", "e_ml", lambda e: e.tensor_tensor(q.ap[:, 0, :, :], m4[:, :, 1, :], q.ap[:, 1, :, :], ALU.mult), h2)
            m.free = [h3]
            return q, h3

        def outer(j, q, h):
            m = rU.take()
            for u in range(2):
                tr = pr.op("tensor", "e_aT_t", lambda e, u=u: e.transpose(
                    m.ap[:, u * P:(u + 1) * P], q.ap[:, 0, u, :], self.ident[:, :]), h, m.free)
            q.free = [tr]
            a = aS.take()
            h = pr.op("scalar", "e_aS", lambda e: e.activation(
                a.ap[:, :, :], m.ap[:, 0:2 * P].rearrange("p (u k) -> p u k", u=2), ACT.Copy), tr, a.free)
            m.free = [h]
            return a, h

        def leave(j, a, h):
            m = rD.take()
            for u in range(2):
                mm = pr.op("tensor", "e_o", lambda e, u=u: e.matmul(
                    m.ap[:, u * D:(u + 1) * D], a.ap[:, u, :], dn[:, bass.ds(regs[j, u], 1), :].rearrange("p o f -> p (o f)"),
                    start=True, stop=True), h, h_dn, m.free)
            a.free = [mm]
            y = ys.take()
            h = pr.op("vector", "e_yc", lambda e: e.tensor_copy(y.ap[:, :, :], m.ap.rearrange("p (u d) -> p u d", u=2)), mm, y.free)
            m.free = [h]
            hd = pr.dma("sync", f"e_ys{j % 3}", self.yed[2 * j * P:2 * (j + 1) * P, :].rearrange("(u p) d -> p u d", p=P),
                        y.ap[:, :, :], h)
            y.free = [hd]
            return hd

        stage = {}
        self.ye_done = []
        for j in range(NS // 2 + 3):
            if j == 0:
                for k in range(3):
                    stage["f", k] = fetch(k)
            if j < NS // 2:
                stage["x", j] = arrive(j, *stage.pop(("f", j)))
            if j + 3 < NS // 2:
                stage["f", j + 3] = fetch(j + 3)
            if 0 <= j - 1 < NS // 2:
                stage["h", j - 1] = inner(j - 1, *stage.pop(("x", j - 1)))
            if 0 <= j - 3 < NS // 2:
                self.ye_done.append(leave(j - 3, *stage.pop(("t", j - 3))))
            if 0 <= j - 2 < NS // 2:
                stage["t", j - 2] = outer(j - 2, *stage.pop(("h", j - 2)))
        self.high2 = sb.high
        self.high2l = low.high

    def fetch_mha(self, sb):
        pr, ins = self.pr, self.ins
        t = self.attn = {}

        def weight(name, shape, src):
            t[name] = sb("mw_" + name, shape)
            pr.dma("scalar", "mw", t[name][tuple(slice(None) for _ in shape)], src)

        weight("wi", [P, 2, 3 * D], ins["wi"].rearrange("(c p) n -> p c n", p=P))
        weight("bic", [P, 6], ins["bic"])
        weight("bv", [P, D], self.row(ins["bi"][2 * D:3 * D]))
        weight("wo", [P, 2, D], ins["wo2"].rearrange("(c p) n -> p c n", p=P))
        weight("bo", [P, D], self.row(ins["bo2"]))
        weight("g1", [P, D], self.row(ins["ln1_g"]))
        weight("b1", [P, D], self.row(ins["ln1_b"]))
        t["x"] = Buf(sb("m_x", [P, NT, D]))
        t["hx"] = pr.dma("scalar", "m_x0", t["x"].ap[:, :, :], self.yd[0:NT].rearrange("t p d -> p t d"), self.y_done[0])
        t["end"] = sb.pos

    def gather(self, tag, ring, n):
        got = []
        for u in range(2):
            k = ring.n % len(ring.bufs)
            y = ring.take()
            got.append((y, self.pr.put("gpsimd", f"{tag}_g{k}", lambda e, u=u, y=y: e.indirect_dma_start(
                y.ap[:, :], None, self.yed,
                bass.IndirectOffsetOnAxis(ap=self.epos[:, u * NB * NT + n:u * NB * NT + n + 1], axis=0)),
                16, self.ye_done, y.free)))
        return got

    def blend(self, tag, got, n, dst, ready):
        for u, (y, h) in enumerate(got):
            k = u * NB * NT + n
            ready = self.pr.op("vector", tag + "_ga", lambda e, k=k, y=y: e.scalar_tensor_tensor(
                dst, y.ap[:, :], self.egate[:, k:k + 1], dst, ALU.mult, ALU.add), h, ready)
            y.free = [ready]
        return ready

    def mha(self):
        nc, pr, ins, ps = self.nc, self.pr, self.ins, self.ps
        sb = Arena(nc, self.attn["end"], self.hi)
        F32R = mybir.dt.float32r
        scr = nc.dram_tensor("qk_scratch", [2, 4, D, S], F32).ap()

        t = self.attn
        wi, bic, bv, wo, bo, g1, b1, xb = (t[k] for k in ("wi", "bic", "bv", "wo", "bo", "g1", "b1", "x"))
        bq = sb("m_bq", [P, 2])
        h_bq = pr.op("vector", "m_bq", lambda e: e.tensor_scalar(bq[:, :], bic[:, 0:2], 0.25, None, ALU.mult))
        G4 = 4
        KS = 66
        at_x = (sb.pos + 31) // 32 * 32
        yT = Buf(sb("m_yT", [P, 2, S]))
        yg = Ring([sb(f"m_yg{i}", [P, D]) for i in range(4)])
        full = Buf(sb("m_full", [P, S]))
        part = Ring([sb(f"m_part{i}", [P, 2, S], F32R) for i in range(2)])
        end_x = at_q = (sb.pos + 31) // 32 * 32
        qst = [Buf(sb(f"m_qs{i}", [KS, G4, S], F32R)) for i in range(8)]
        at_k = (sb.pos + 31) // 32 * 32
        kst = [Buf(sb(f"m_ks{i}", [KS, G4, S], F32R)) for i in range(8)]
        va = Ring([sb(f"m_va{i}", [P, NT, H, 32]) for i in range(3)])
        mx = Ring([sb(f"m_mx{i}", [P, NT, H]) for i in range(2)])
        mhl = Buf(sb("m_mhl", [4, 2, S], F32R))
        pt = Ring([sb(f"m_pt{i}", [P, G4, S]) for i in range(2)])
        of = Ring([sb(f"m_of{i}", [P, S]) for i in range(1)])
        rc = Ring([sb(f"m_rc{i}", [P, NT, G4]) for i in range(1)])
        ots = Ring([sb(f"m_ot{i}", [P, NT, H, 16]) for i in range(2)])
        oT = Ring([sb(f"m_oT{i}", [P, 2, P]) for i in range(2)])
        zb = Ring([sb(f"m_z{i}", [P, D]) for i in range(2)])
        lnr = self.ln_make(sb, "m_ln", 1)
        self.high3 = sb.high
        ones = part.bufs[0].ap[0:2, 0, :]
        o1 = pr.op("vector", "m_one", lambda e: e.memset(ones.bitcast(F32), 1.0))
        o1 = pr.op("vector", "m_one", lambda e: e.tensor_copy(ones, ones.bitcast(F32)), o1)
        for i, k in enumerate(kst):
            k.free = [pr.dma("sync", f"m_kone{i}", k.ap[64:66, j, :].bitcast(F32), ones.bitcast(F32), o1) for j in range(G4)]
        part.bufs[0].free = [h for k in kst for h in k.free]
        for i, v in enumerate(va.bufs):
            v.free = [pr.op("vector", "m_va1", lambda e, v=v: e.memset(v.ap[:, :, :, :], 1.0))]
        rM, rS, rE, rO = self.banks(0, 6), self.banks(1, 2, 3), self.banks(4, 5), self.banks(7)
        state = {}

        def project(b):
            st = state[b] = {}
            hx = self.attn["hx"] if b == 0 else pr.dma(
                "sync", "m_x", xb.ap[:, :, :], self.yd[b * NT:(b + 1) * NT].rearrange("t p d -> p t d"), xb.free, self.y_done[b])
            yield
            hs = []
            got = self.gather("m", yg, b * NT)
            for t in range(NT):
                nxt = self.gather("m", yg, b * NT + t + 1) if t + 1 < NT else None
                yield
                hs.append(self.blend("m", got, b * NT + t, xb.ap[:, t, :], hx))
                got = nxt
            hx = hs
            hyd = pr.dma("sync", "m_yd", self.yd[b * NT:(b + 1) * NT].rearrange("t p d -> p t d"), xb.ap[:, :, :], hx)
            self.y_done[b] = [hyd]
            yield
            yield
            ev = []
            for c in range(2):
                m = rM.take()
                for t in range(NT):
                    tr = pr.op("tensor", "m_tr", lambda e, c=c, t=t, m=m: e.transpose(
                        m.ap[:, t * P:(t + 1) * P], xb.ap[:, t, c * P:(c + 1) * P], self.ident[:, :]), hx, m.free)
                h = pr.op("scalar", "m_yT", lambda e, c=c, m=m: e.activation(yT.ap[:, c, :], m.ap, ACT.Copy), tr, yT.free)
                m.free = [h]
                ev.append(h)
                yield
            xb.free = [tr, hyd]
            hst = []
            for w in range(2):
                hi, lo = part.take(), part.take()
                for c in range(2):
                    m = rM.take()
                    for k in range(2):
                        mm = pr.op("tensor", "m_qk", lambda e, c=c, k=k, w=w, m=m: e.matmul(
                            m.ap, wi[:, k, w * D + c * P:w * D + (c + 1) * P], yT.ap[:, k, :], start=(k == 0), stop=(k == 1)),
                            ev, m.free)
                    if w == 0:
                        h = pr.op("scalar", "m_qc", lambda e, c=c, m=m: e.activation(
                            full.ap[:, :], m.ap, ACT.Identity, bias=bq[:, c:c + 1], scale=0.25), mm, h_bq, full.free)
                    else:
                        h = pr.op("scalar", "m_kc", lambda e, c=c, m=m: e.activation(
                            full.ap[:, :], m.ap, ACT.Identity, bias=bic[:, 2 + c:3 + c]), mm, full.free)
                    m.free = [h]
                    hh = pr.op("gpsimd", "m_hi", lambda e, c=c, hi=hi: e.tensor_scalar(
                        hi.ap[:, c, :], full.ap[:, :], 1.0, 1.0, ALU.mult, ALU.mult), h, hi.free)
                    hl = pr.op("gpsimd", "m_lo", lambda e, c=c, hi=hi, lo=lo: e.tensor_tensor(
                        lo.ap[:, c, :], full.ap[:, :], hi.ap[:, c, :].bitcast(F32), ALU.subtract), hh, lo.free)
                    full.free = [hl]
                    yield
                for i, (u, hu) in enumerate(((hi, [hh, hl]), (lo, [hl]))):
                    hd = pr.dma("sync", f"m_sc{2 * w + i}", scr[b % 2, 2 * w + i].rearrange("(c p) t -> p c t", p=P),
                                u.ap[:, :, :].bitcast(F32), hu, state[b - 2]["loaded"] if b >= 2 else [])
                    u.free = [hd]
                    hst.append(hd)
            st["stored"] = hst
            v = va.take()
            hv = []
            for u in range(2):
                m = rM.take()
                for i in range(2):
                    for k in range(2):
                        mm = pr.op("tensor", "m_v", lambda e, t=2 * u + i, i=i, k=k, m=m: e.matmul(
                            m.ap[:, i * D:(i + 1) * D], yT.ap[:, k, t * P:(t + 1) * P], wi[:, k, 2 * D:3 * D],
                            start=(k == 0), stop=(k == 1)), ev, m.free)
                h = [pr.op("vector", "m_vc", lambda e, t=2 * u + i, i=i, m=m: e.tensor_tensor(
                    v.ap[:, t, :, 0:16], m.ap[:, i * D:(i + 1) * D].rearrange("p (h d) -> p h d", h=H),
                    bv[:, :].rearrange("p (h d) -> p h d", h=H), ALU.add), mm, v.free) for i in range(2)]
                m.free = h
                hv += h
                yield
            yT.free = [mm]
            v.free = []
            st["v"], st["hv"] = v, hv

        def load(b, g):
            st = state[b]
            i = (b % 2) * 4 + g
            hs = []
            for bufs, order in ((qst, (0, 0, 1, 1)), (kst, (2, 3, 2, 3))):
                for s_, p_ in enumerate(order):
                    hs.append(pr.dma("sync", f"m_st{i}", bufs[i].ap[16 * s_:16 * s_ + 16, :, :].bitcast(F32),
                                     scr[b % 2, p_, 64 * g:64 * g + 64].rearrange("(h d) t -> d h t", d=16),
                                     st["stored"], bufs[i].free))
            kst[i].free, qst[i].free = [], []
            st.setdefault("stack", {})[g] = hs
            st.setdefault("loaded", []).extend(hs)

        def maxima(b):
            st = state[b]
            x = mx.take()
            st["neg"] = {}
            tr = []

            def negate(g, hm, mm):
                i = (b % 2) * 4 + g
                m = rM.take()
                for t in range(NT):
                    h = pr.op("tensor", "m_mT", lambda e, t=t: e.transpose(
                        m.ap[0:G4, t * P:(t + 1) * P], x.ap[:, t, G4 * g:G4 * g + G4], self.ident[:, :]), hm, m.free)
                tr.append(h)
                h1 = pr.op("vector", "m_nhi", lambda e: e.tensor_scalar(
                    mhl.ap[:, 0, :], m.ap[0:G4, :], -1.0, None, ALU.mult), h, mhl.free)
                h2 = pr.op("vector", "m_nlo", lambda e: e.scalar_tensor_tensor(
                    mhl.ap[:, 1, :], m.ap[0:G4, :], -1.0, mhl.ap[:, 0, :].bitcast(F32), ALU.mult, ALU.subtract), h1)
                m.free = [h2]
                mhl.free = [pr.dma("sync", f"m_mr{i}", qst[i].ap[64 + u:65 + u, :, :].bitcast(F32),
                                   mhl.ap[:, u, :].bitcast(F32), h2, mm) for u in range(2)]
                st["neg"][g] = mhl.free

            ready = None
            for h in range(H):
                i = (b % 2) * 4 + h // 4
                if h % 4 == 0:
                    hm = []
                for t in range(NT):
                    m = rS.take()
                    mm = pr.op("tensor", "m_S", lambda e, h=h, t=t, i=i, m=m: e.matmul(
                        m.ap, qst[i].ap[0:64, h % 4, t * P:(t + 1) * P], kst[i].ap[0:64, h % 4, :], start=True, stop=True),
                        st["stack"][h // 4], m.free)
                    r = pr.op("vector", "m_max", lambda e, h=h, t=t, m=m: e.tensor_reduce(
                        x.ap[:, t, h:h + 1], m.ap, AX, ALU.max), mm, x.free)
                    m.free = [r]
                    hm.append(r)
                    yield
                    if ready and t == 2:
                        negate(*ready)
                        ready = None
                if h % 4 == 3:
                    ready = (h // 4, hm, mm)
            negate(*ready)
            x.free = tr
            yield

        def turn_back(g, f, h, ot, ho):
            m = rM.take()
            for t in range(NT):
                tr = pr.op("tensor", "m_ofT", lambda e, t=t: e.transpose(
                    m.ap[:, t * P:(t + 1) * P], f.ap[:, t * P:(t + 1) * P], self.ident[:, :]), h, m.free)
            f.free = [tr]
            r = rc.take()
            m4 = m.ap.rearrange("p (t h d) -> p t h d", t=NT, h=G4)
            hr = pr.op("vector", "m_rc", lambda e: e.reciprocal(r.ap[:, :, :], m4[:, :, :, 16]), tr, r.free)
            hn = pr.op("vector", "m_on", lambda e: e.tensor_tensor(
                ot.ap[:, :, 4 * g:4 * g + 4, :], m4[:, :, :, 0:16],
                r.ap[:, :, :].unsqueeze(3).broadcast_to([P, NT, G4, 16]), ALU.mult), hr, ot.free)
            m.free = [hn]
            r.free = [hn]
            ho.append(hn)
            yield

        def attend(b):
            st = state[b]
            v = st["v"]
            ot = ots.take()
            ho = []
            later = None
            for g in range(4):
                i = (b % 2) * 4 + g
                o = rO.take()
                pend = []
                for kt in range(NT + 1):
                    if kt in (1, 2) and later is not None:
                        next(later, None)
                    if kt < NT:
                        p = pt.take()
                        he = []
                        for j in range(4):
                            m = rE.take()
                            mm = pr.op("tensor", "m_ST", lambda e, kt=kt, j=j, m=m, i=i: e.matmul(
                                m.ap, kst[i].ap[:, j, kt * P:(kt + 1) * P], qst[i].ap[:, j, :],
                                start=True, stop=True), st["stack"][g], st["neg"][g], m.free)
                            h = pr.op("scalar", "m_exp", lambda e, j=j, m=m, p=p: e.activation(
                                p.ap[:, j, :], m.ap, ACT.Exp), mm, p.free)
                            m.free = [h]
                            he.append(h)
                            yield
                        p.free = []
                        pend.append((kt, p, he))
                    if kt >= 1:
                        k0, p0, h0 = pend.pop(0)
                        for j in range(4):
                            av = pr.op("tensor", "m_AV", lambda e, k0=k0, p0=p0, j=j, o=o, g=g: e.matmul(
                                o.ap[32 * j:32 * j + 32, :], v.ap[:, k0, 4 * g + j, :], p0.ap[:, j, :],
                                start=(k0 == 0), stop=(k0 == NT - 1), tile_position=(0, 32 * j)), h0, st["hv"], o.free)
                        p0.free = [av]
                        yield
                qst[i].free, kst[i].free = [mm], [mm]
                f = of.take()
                h = pr.op("vector", "m_of", lambda e, f=f, o=o: e.tensor_copy(f.ap[:, :], o.ap), av, f.free)
                o.free = [h]
                f.free = []
                later = turn_back(g, f, h, ot, ho)
                if b + 2 < NB and g >= 1:
                    load(b + 2, g - 1)
                yield
            for _ in later:
                yield
            v.free = [av]
            ot.free = []
            st["ot"], st["ho"] = ot, ho

        def finish(b):
            st = state[b]
            ot, ho = st["ot"], st["ho"]
            done, held = [], {}
            for k in range(NT + 1):
                if k < NT:
                    m = rM.take()
                    for c in range(2):
                        tr = pr.op("tensor", "m_oT_t", lambda e, c=c, t=k, m=m: e.transpose(
                            m.ap[:, c * P:(c + 1) * P], ot.ap[:, t, 8 * c:8 * c + 8, :], self.ident[:, :]), ho, m.free)
                    q = oT.take()
                    h = pr.op("scalar", "m_oT", lambda e, q=q, m=m: e.activation(
                        q.ap[:, :, :], m.ap[:, 0:D].rearrange("p (c k) -> p c k", c=2), ACT.Copy), tr, q.free)
                    m.free = [h]
                    q.free = []
                    z = zb.take()
                    n = b * NT + k
                    hz = pr.dma("sync", f"m_z{n % 2}", z.ap[:, :], self.yd[n], z.free, self.y_done[b])
                    hz = pr.op("gpsimd", "m_zb", lambda e, z=z: e.tensor_tensor(z.ap[:, :], z.ap[:, :], bo[:, :], ALU.add), hz)
                    z.free = []
                    held[k] = (q, h, z, hz)
                    yield
                if k >= 1:
                    t = k - 1
                    q, h, z, hz = held.pop(t)
                    n = b * NT + t
                    m = rM.take()
                    for c in range(2):
                        mm = pr.op("tensor", "m_wo", lambda e, c=c, q=q, m=m: e.matmul(
                            m.ap[:, 0:D], q.ap[:, c, :], wo[:, c, :], start=(c == 0), stop=(c == 1)), h, m.free)
                    q.free = [mm]
                    a = pr.op("vector", "m_zs", lambda e, z=z, m=m: e.tensor_tensor(
                        z.ap[:, :], m.ap[:, 0:D], z.ap[:, :], ALU.add), mm, hz)
                    m.free = [a]
                    a = self.ln("m_ln", lnr, [z.ap[:, :]], [z.ap[:, :]], [a], [])
                    a = pr.op("gpsimd", "m_lg", lambda e, z=z: e.tensor_tensor(z.ap[:, :], z.ap[:, :], g1[:, :], ALU.mult), a)
                    a = pr.op("gpsimd", "m_lb", lambda e, z=z: e.tensor_tensor(z.ap[:, :], z.ap[:, :], b1[:, :], ALU.add), a)
                    hd = pr.dma("sync", f"m_x2{n % 2}", self.x2d[n], z.ap[:, :], a)
                    z.free = [hd]
                    done.append(hd)
                    yield
            ot.free = [tr]
            self.x2_done[b] = done

        def fetch_grouped():
            E, F, half = 8, 512, 4 * G4 * S * 4
            i = NB % 2 * 4
            w1, w2, bb = at_q + i // 4 * half, at_k + i // 4 * half, at_x
            arenas = [Arena(nc, w1, w1 + half), Arena(nc, w2, w2 + half), Arena(nc, bb, end_x)]
            t = self.grouped = dict(w1=arenas[0]("hw_w1", [P, E, 2 * F]), w2=arenas[1]("hw_w2", [P, E, 4 * D]),
                                    b1=arenas[2]("hw_b1", [P, E * F]))
            q0, k0 = at_q + half - i // 4 * half, at_k + half - i // 4 * half
            self.spare = [Arena(nc, q0, q0 + half), Arena(nc, arenas[2].pos, end_x), Arena(nc, self.base, at_x),
                          Arena(nc, k0, k0 + half), Arena(nc, at_k + 2 * half, self.hi)]
            yield
            for _ in range(3):
                yield
            free = [x.free for y in (qst, kst) for x in y[i:i + 4]]
            for x in range(E):
                pr.dma("scalar", "hw_w", t["w1"][:, x, :].rearrange("p (c f) -> p c f", c=2),
                       ins["w1"][x].rearrange("(c p) f -> p c f", p=P), free)
                yield
                pr.dma("scalar", "hw_w", t["w2"][:, x, :].rearrange("p (c d) -> p c d", c=4),
                       ins["w2"][x].rearrange("(c p) d -> p c d", p=P), free)
                yield
            pr.dma("scalar", "hw_w", t["b1"][:, :], self.row(ins["b1"].rearrange("x f -> (x f)")),
                   xb.free, yT.free, full.free, [x.free for y in (yg, part) for x in y.bufs])

        self.x2_done = {}
        for _ in project(0):
            pass
        for g in range(4):
            load(0, g)
        streams = [(maxima(0), 65)]
        if NB > 1:
            streams.append((project(1), 15))
        merge(*streams)
        if NB > 1:
            for g in range(4):
                load(1, g)
        for b in range(NB):
            streams = [(attend(b), 86)]
            if b + 1 < NB:
                streams.append((maxima(b + 1), 65))
            if b >= 1:
                streams.append((finish(b - 1), 8))
            if b + 2 < NB:
                streams.append((project(b + 2), 34))
            if b == NB - 1:
                streams.append((fetch_grouped(), 21))
            merge(*streams)
            if b + 2 < NB:
                load(b + 2, 3)
        for _ in finish(NB - 1):
            pass

    def slots(self, sb, tag, oh, h_oh, n, posi, tei, banks, upper, ones, before, thr, iota):
        pr, E, ns = self.pr, 8, n + 7
        v = lambda fn, *after: pr.op("vector", tag + "_slot", fn, *after)
        cum = [sb(f"{tag}_cum{i}", [P, n, E]) for i in range(2)]
        more = sb(tag + "_more", [P, E, n])
        nt = sb(tag + "_nt", [P, E])
        first = sb(tag + "_first", [P, E])
        te = sb(tag + "_te", [P, ns])
        pos = sb(tag + "_pos", [P, n])
        tmp = sb(tag + "_tmp", [P, ns, E])
        (upper, h_upper), (ones, h_ones), (before, h_before), (thr, h_thr), (iota, h_iota) = upper, ones, before, thr, iota
        flat = lambda t: t[:, :, :].rearrange("p t x -> p (t x)")
        wide = lambda t: t[:, :].unsqueeze(1).broadcast_to([P, n, E])
        mr, mt = banks.take(), banks.take()
        h_rank = pr.op("tensor", tag + "_rank", lambda e: e.matmul(mr.ap[:, 0:n * E], upper[:, :], flat(oh), start=True, stop=True),
                       h_oh, h_upper, mr.free)
        h_tot = pr.op("tensor", tag + "_rank", lambda e: e.matmul(mt.ap[:, 0:n * E], ones[:, :], flat(oh), start=True, stop=True),
                      h_oh, h_ones, mt.free)
        a = v(lambda e: e.tensor_copy(flat(cum[0]), mt.ap[:, 0:n * E]), h_tot)
        w, k = 0, 1
        while k < n:
            p, q = cum[w], cum[1 - w]
            a1 = v(lambda e, p=p, q=q, k=k: e.tensor_copy(q[:, 0:k, :], p[:, 0:k, :]), a)
            a2 = v(lambda e, p=p, q=q, k=k: e.tensor_tensor(q[:, k:n, :], p[:, k:n, :], p[:, 0:n - k, :], ALU.add), a)
            a, w, k = [a1, a2], 1 - w, 2 * k
        inc, exc = cum[w], cum[1 - w]
        b_ = v(lambda e: e.tensor_tensor(more[:, :, :], inc[:, n - 1, :].unsqueeze(2).broadcast_to([P, E, n]),
                                         thr[:, 0:n].unsqueeze(1).broadcast_to([P, E, n]), ALU.is_gt), a, h_thr)
        b_ = v(lambda e: e.tensor_reduce(nt[:, :], more[:, :, :], AX, ALU.add), b_)
        b_ = v(lambda e: e.tensor_tensor(more[:, :, 0:E], before[:, :, :], nt[:, :].unsqueeze(1).broadcast_to([P, E, E]), ALU.mult),
               b_, h_before)
        h_first = v(lambda e: e.tensor_reduce(first[:, :], more[:, :, 0:E], AX, ALU.add), b_)
        a = v(lambda e: e.tensor_tensor(flat(exc), flat(inc), mt.ap[:, 0:n * E], ALU.subtract), a)
        mt.free = [a]
        a = v(lambda e: e.tensor_tensor(flat(exc), mr.ap[:, 0:n * E], flat(exc), ALU.add), a, h_rank)
        mr.free = [a]
        yield
        b_ = v(lambda e: e.tensor_scalar(nt[:, :], first[:, :], 128.0, None, ALU.mult), h_first)
        a = v(lambda e: e.tensor_tensor(exc[:, :, :], exc[:, :, :], wide(nt), ALU.add), a, b_)
        a = v(lambda e: e.tensor_tensor(exc[:, :, :], exc[:, :, :], oh[:, :, :], ALU.mult), a)
        a = v(lambda e: e.tensor_reduce(pos[:, :], exc[:, :, :], AX, ALU.add), a)
        h_pos = v(lambda e: e.tensor_copy(posi[:, :], pos[:, :]), a)
        a = v(lambda e: e.tensor_tensor(tmp[:, :, :], iota[:, 0:ns].unsqueeze(2).broadcast_to([P, ns, E]),
                                        first[:, :].unsqueeze(1).broadcast_to([P, ns, E]), ALU.is_ge), h_first, h_iota)
        a = v(lambda e: e.tensor_reduce(te[:, :], tmp[:, :, :], AX, ALU.add), a)
        a = v(lambda e: e.tensor_scalar(te[:, :], te[:, :], 1.0, None, ALU.subtract), a)
        h_te = v(lambda e: e.tensor_copy(tei[:, 0:ns], te[:, :]), a)
        self.slotted[tag] = h_pos, h_te
        yield

    def gating(self, tag, l, s_, w, n, ready, before, h_before):
        pr = self.pr
        v = lambda fn, *after: pr.op("vector", tag, fn, *after)
        G, X = 4, 2
        gl = l[:, :, 0:4]
        xl = l[:, :, 4:12].rearrange("p t (g x) -> p t g x", g=G)
        col = lambda k: s_[:, k, :, 0]
        wide = lambda k: s_[:, k, :, 0].unsqueeze(2).broadcast_to([P, n, G])
        quad = lambda k: s_[:, k, :, :]
        qwide = lambda k: s_[:, k, :, :].unsqueeze(3).broadcast_to([P, n, G, X])
        a1 = v(lambda e: e.tensor_reduce(col(0), gl, AX, ALU.max), ready)
        a2 = v(lambda e: e.tensor_reduce(quad(1), xl, AX, ALU.max), ready)
        a1 = v(lambda e: e.tensor_tensor(gl, gl, wide(0), ALU.subtract), a1)
        a2 = v(lambda e: e.tensor_tensor(xl, xl, qwide(1), ALU.subtract), a2)
        h = pr.op("scalar", tag + "_e", lambda e: e.activation(l[:, :, :], l[:, :, :], ACT.Exp), a1, a2)
        a1 = v(lambda e: e.tensor_reduce(col(2), gl, AX, ALU.add), h)
        a2 = v(lambda e: e.tensor_reduce(quad(3), xl, AX, ALU.add), h)
        a1 = v(lambda e: e.reciprocal(col(4), col(2)), a1)
        a2 = v(lambda e: e.reciprocal(quad(5), quad(3)), a2)
        a1 = v(lambda e: e.tensor_tensor(gl, gl, wide(4), ALU.mult), a1)
        a2 = v(lambda e: e.tensor_tensor(xl, xl, qwide(5), ALU.mult), a2)
        b1 = v(lambda e: e.tensor_reduce(col(6), gl, AX, ALU.max), a1)
        b2 = v(lambda e: e.tensor_tensor(quad(7), gl, wide(6), ALU.is_ge), b1)
        pairs = w.rearrange("p t (g x) -> p t g x", g=G)
        cnt = []
        for g in range(G):
            c = v(lambda e, g=g: e.tensor_tensor(s_[:, 9:13, :, g].rearrange("p j t -> p t j"), quad(7),
                                                 before[:, g, 0:G].unsqueeze(1).broadcast_to([P, n, G]), ALU.mult), b2, h_before)
            cnt.append(c)
        for g in range(G):
            cnt[g] = v(lambda e, g=g: e.tensor_reduce(s_[:, 8, :, g], s_[:, 9:13, :, g].rearrange("p j t -> p t j"), AX, ALU.add), cnt[g])
        c = v(lambda e: e.tensor_scalar(quad(8), quad(8), 0.5, None, ALU.is_lt), cnt)
        c = v(lambda e: e.tensor_tensor(quad(7), quad(7), quad(8), ALU.mult), c)
        c = v(lambda e: e.tensor_tensor(quad(7), quad(7), wide(6), ALU.mult), c)
        d1 = v(lambda e: e.tensor_reduce(quad(1), xl, AX, ALU.max), a2)
        c = v(lambda e: e.tensor_tensor(quad(7), quad(7), quad(1), ALU.mult), c, d1)
        d2 = v(lambda e: e.tensor_tensor(quad(3), xl[:, :, :, 0], xl[:, :, :, 1], ALU.is_ge), a2)
        e1 = v(lambda e: e.tensor_tensor(pairs[:, :, :, 0], quad(7), quad(3), ALU.mult), c, d2)
        return [v(lambda e: e.tensor_tensor(pairs[:, :, :, 1], quad(7), pairs[:, :, :, 0], ALU.subtract), e1)]

    def phase3(self):
        self.pr.fence()
        nc, pr, ins, ps = self.nc, self.pr, self.ins, self.ps
        sb = Spaces(*self.spare)
        E, F, NN = 8, 512, NB * NT
        NS = NN + E - 1
        I32 = mybir.dt.int32
        xsd = self.xsd
        ysd = nc.dram_tensor("ys_scratch", [NS * P, D], F32).ap()
        regs = {}

        def weight(name, shape, src, eng="sync"):
            t = sb("hw_" + name, shape)
            return t, pr.dma(eng, "hw_" + name, t[tuple(slice(None) for _ in shape)], src)

        x2 = sb("h_x2", [P, NN, D])
        h_x2 = [pr.dma("sync", f"h_x2{b}", x2[:, b * NT:(b + 1) * NT, :], self.x2d[b * NT:(b + 1) * NT].rearrange("t p d -> p t d"),
                       self.x2_done[b]) for b in range(NB)]
        wgx = sb("hw_gx", [P, 2, 12])
        bgx = sb("hw_bgx", [12, 1])
        h_gx = [pr.dma("scalar", "hw_g", wgx[:, :, 0:4], ins["w_group"].rearrange("(c p) g -> p c g", p=P)),
                pr.dma("scalar", "hw_bg", bgx[0:4, :], ins["b_group"].rearrange("(n o) -> n o", o=1)),
                pr.dma("scalar", "hw_bx", bgx[4:12, :], ins["b_expert"].rearrange("(n o) -> n o", o=1))]
        h_gx += [pr.dma("scalar", "hw_x", wgx[:, c, 4 + 2 * g:6 + 2 * g], ins["w_expert"][g, c * P:(c + 1) * P, :])
                 for g in range(4) for c in range(2)]
        before, h_before = weight("before", [P, E, E], ins["c_before"], "scalar")
        upper, h_upper = weight("upper", [P, P], ins["c_upper"], "scalar")
        thr, h_thr = weight("thr", [P, NN], ins["c_thr"][:, 0:NN], "scalar")
        iota, h_iota = weight("iota", [P, NS], ins["c_iota"][:, 0:NS], "scalar")
        b2, h_b2 = weight("b2", [P, E * D], self.row(ins["b2"].rearrange("x d -> (x d)")), "scalar")
        g2, h_g2 = weight("g2", [P, D], self.row(ins["ln2_g"]), "scalar")
        c2, h_c2 = weight("c2", [P, D], self.row(ins["ln2_b"]), "scalar")
        w1, w2, b1 = self.grouped["w1"], self.grouped["w2"], self.grouped["b1"]
        xr = sb("h_xr", [P, NN, D])
        h_xr = [pr.dma("sync", f"h_xr{b}", xr[:, b * NT:(b + 1) * NT, :], self.x1d[b * NT:(b + 1) * NT].rearrange("t p d -> p t d"),
                       h_x2) for b in range(NB)]
        onesq = sb("h_ones", [P, P])
        h_ones = pr.op("vector", "h_ones", lambda e: e.memset(onesq[:, :], 1.0))
        xT = Ring([sb(f"h_xT{i}", [P, 2, S]) for i in range(2)])
        lgT = Ring([sb(f"h_lgT{i}", [12, S]) for i in range(2)])
        lg = sb("h_lg", [P, NN, 12])
        sm = sb("h_sm", [P, 13, NN, 4])
        cw = sb("h_cw", [P, NN, E])
        sT = Ring([sb(f"h_sT{i}", [P, 2, P]) for i in range(3)])
        xs = Ring([sb(f"h_xs{i}", [P, D]) for i in range(4)])
        hb = Ring([sb(f"h_hb{i}", [P, F]) for i in range(2)])
        hT = Ring([sb(f"h_hT{i}", [P, 4, P]) for i in range(2)])
        ys = Ring([sb(f"h_ys{i}", [P, D]) for i in range(3)])
        lnr = self.ln_make(sb, "h_ln", 2)
        self.high4 = [a.end - a.pos for a in sb.arenas]
        rA, rH, rT, rD = self.banks(0, 1), self.banks(2, 3), self.banks(4, 5), self.banks(6, 7)

        oh = sb("h_oh", [P, NN, E])
        gsum = sb("h_gsum", [P, NN])
        posi = sb("h_posi", [P, NN], I32)
        tei = sb("h_tei", [P, NS], I32)

        def turn(b):
            xt = xT.take()
            ev = []
            for c in range(2):
                m = rA.take()
                for t in range(NT):
                    tr = pr.op("tensor", "h_tr", lambda e, c=c, t=t, m=m: e.transpose(
                        m.ap[:, t * P:(t + 1) * P], x2[:, b * NT + t, c * P:(c + 1) * P], self.ident[:, :]), h_x2[b], m.free)
                h = pr.op("scalar", "h_xT", lambda e, c=c, m=m: e.activation(xt.ap[:, c, :], m.ap, ACT.Copy), tr, xt.free)
                m.free = [h]
                ev.append(h)
            xt.free = []
            return xt, ev

        def score(xt, ev):
            m = rH.take()
            for c in range(2):
                mm = pr.op("tensor", "h_lg", lambda e, c=c: e.matmul(
                    m.ap[0:12, :], wgx[:, c, :], xt.ap[:, c, :], start=(c == 0), stop=(c == 1)), ev, h_gx, m.free)
            xt.free = [mm]
            l = lgT.take()
            h = pr.op("scalar", "h_lgT", lambda e: e.activation(
                l.ap[:, :], m.ap[0:12, :], ACT.Identity, bias=bgx[:, 0:1]), mm, h_gx, l.free)
            m.free = [h]
            return l, h

        def score_back(l, h, k, m):
            for t in range(NT):
                tr = pr.op("tensor", "h_lgb", lambda e, t=t: e.transpose(
                    m.ap[:, (k * NT + t) * 12:(k * NT + t + 1) * 12], l.ap[:, t * P:(t + 1) * P], self.ident[0:12, 0:12]),
                    h, m.free)
            l.free = [tr]
            return tr

        def gates(k):
            m = rT.take()
            turned, held = {}, {}
            for i in range(GB + 2):
                if i < GB:
                    turned[i] = turn(k * GB + i)
                if 1 <= i <= GB:
                    held[i - 1] = score(*turned.pop(i - 1))
                if i >= 2:
                    tr = score_back(*held.pop(i - 2), i - 2, m)
            n0, n1 = k * GT, (k + 1) * GT
            h = pr.op("vector", "h_lgc", lambda e: e.tensor_copy(
                lg[:, n0:n1, :], m.ap[:, 0:GT * 12].rearrange("p (t e) -> p t e", t=GT)), tr)
            m.free = [h]
            return self.gating("h_gate", lg[:, n0:n1, :], sm[:, :, n0:n1, :], cw[:, n0:n1, :], GT, h, before, h_before)

        GB = max(1, NB // 2)
        GT = GB * NT
        h_cw = [gates(k) for k in range(NB // GB)]

        h_oh = pr.op("vector", "h_oh", lambda e: e.tensor_scalar(
            oh[:, :, :].rearrange("p t x -> p (t x)"), cw[:, :, :].rearrange("p t x -> p (t x)"), 0.0, None, ALU.is_gt), h_cw)
        h_gs = pr.op("vector", "h_gs", lambda e: e.tensor_reduce(gsum[:, :], cw[:, :, :], AX, ALU.add), h_cw)
        for _ in self.slots(sb, "h", oh, h_oh, NN, posi, tei, rA, (upper, h_upper), (onesq, h_ones), (before, h_before),
                            (thr, h_thr), (iota, h_iota)):
            pass
        h_pos, h_te = self.slotted["h"]

        def scatter(n):
            return pr.put("gpsimd", "h_sc", lambda e: e.indirect_dma_start(
                xsd, bass.IndirectOffsetOnAxis(ap=posi[:, n:n + 1], axis=0), x2[:, n, :], None), 16, h_pos, self.zeroed)

        h_sc = [scatter(n) for n in range(NN)]

        def load_reg(eng, j):
            def emit(e):
                regs[eng, j] = e.value_load(tei[0:1, j:j + 1], min_val=0, max_val=E - 1)
            pr.put(eng, None, emit, 0, h_te)

        def fetch(j):
            x = xs.take()
            return x, pr.dma("sync", f"h_xs{j % 4}", x.ap[:, :], xsd[j * P:(j + 1) * P, :], h_sc, x.free)

        def arrive(j, x, h):
            m = rA.take()
            for c in range(2):
                tr = pr.op("tensor", "h_sT_t", lambda e, c=c: e.transpose(
                    m.ap[:, c * P:(c + 1) * P], x.ap[:, c * P:(c + 1) * P], self.ident[:, :]), h, m.free)
            x.free = [tr]
            t = sT.take()
            h = pr.op("scalar", "h_sT", lambda e: e.activation(
                t.ap[:, :, :], m.ap[:, 0:D].rearrange("p (c k) -> p c k", c=2), ACT.Copy), tr, t.free)
            m.free = [h]
            return t, h

        def inner(j, t, h):
            load_reg("tensor", j)
            load_reg("vector", j)
            m = rH.take()
            for c in range(2):
                mm = pr.op("tensor", "h_h", lambda e, c=c: e.matmul(
                    m.ap, t.ap[:, c, :], w1[:, bass.ds(regs["tensor", j], 1), c * F:(c + 1) * F].rearrange("p o f -> p (o f)"),
                    start=(c == 0), stop=(c == 1)), h, m.free)
            t.free = [mm]
            q = hb.take()
            a = pr.op("vector", "h_hb", lambda e: e.tensor_tensor(
                q.ap[:, :], m.ap, b1[:, bass.ds(regs["vector", j] * F, F)], ALU.add), mm, q.free)
            m.free = [a]
            return q, a

        def outer(j, q, a):
            m = rT.take()
            for f in range(4):
                tr = pr.op("tensor", "h_hT_t", lambda e, f=f: e.transpose(
                    m.ap[:, f * P:(f + 1) * P], q.ap[:, f * P:(f + 1) * P], self.ident[:, :]), a, m.free)
            q.free = [tr]
            t = hT.take()
            h = pr.op("scalar", "h_relu", lambda e: e.activation(
                t.ap[:, :, :], m.ap.rearrange("p (f k) -> p f k", f=4), ACT.Relu), tr, t.free)
            m.free = [h]
            return t, h

        def leave(j, t, h):
            m = rD.take()
            for f in range(4):
                mm = pr.op("tensor", "h_o", lambda e, f=f: e.matmul(
                    m.ap[:, 0:D], t.ap[:, f, :], w2[:, bass.ds(regs["tensor", j], 1), f * D:(f + 1) * D].rearrange("p o f -> p (o f)"),
                    start=(f == 0), stop=(f == 3)), h, m.free)
            t.free = [mm]
            y = ys.take()
            a = pr.op("vector", "h_yb", lambda e: e.tensor_tensor(
                y.ap[:, :], m.ap[:, 0:D], b2[:, bass.ds(regs["vector", j] * D, D)], ALU.add), mm, h_b2, y.free)
            m.free = [a]
            hd = pr.dma("sync", f"h_ys{j % 3}", ysd[j * P:(j + 1) * P, :], y.ap[:, :], a)
            y.free = [hd]
            return hd

        h_xrb = []
        stage = {}
        h_ys = []
        for j in range(NS + 3):
            if j == 0:
                for k in range(3):
                    stage["f", k] = fetch(k)
            if j < NS:
                stage["x", j] = arrive(j, *stage.pop(("f", j)))
            if j + 3 < NS:
                stage["f", j + 3] = fetch(j + 3)
            if 0 <= j - 1 < NS:
                stage["h", j - 1] = inner(j - 1, *stage.pop(("x", j - 1)))
            if 0 <= j - 3 < NS:
                h_ys.append(leave(j - 3, *stage.pop(("t", j - 3))))
            if 0 <= j - 2 < NS:
                stage["t", j - 2] = outer(j - 2, *stage.pop(("h", j - 2)))
            if j < NN:
                h_xrb.append(pr.op("vector", "h_xrb", lambda e, j=j: e.tensor_tensor(
                    xr[:, j, :], xr[:, j, :], c2[:, :], ALU.add), h_xr[j // NT], h_c2))

        yg = Ring([sb(f"h_yg{i}", [P, D]) for i in range(8)])
        dg = Ring([sb(f"h_dg{i}", [P, P]) for i in range(8)])
        rZ = ring_of(*[m for r in (rA, rH, rT, rD) for m in r.bufs])
        done = []

        def collect(n):
            y, g = yg.take(), dg.take()
            hy = pr.put("gpsimd", f"h_yg{n % 8}", lambda e: e.indirect_dma_start(
                y.ap[:, :], None, ysd, bass.IndirectOffsetOnAxis(ap=posi[:, n:n + 1], axis=0)), 16, h_ys, y.free)
            hg = pr.op("scalar", "h_dg", lambda e: e.activation(
                g.ap[:, :], self.ident[:, :], ACT.Copy, scale=gsum[:, n:n + 1]), h_gs, g.free)
            return y, hy, g, hg

        def residual(n, y, hy, g, hg):
            m = rZ.take()
            pr.op("tensor", "h_z", lambda e: e.matmul(m.ap[:, 0:D], self.ident[:, :], x2[:, n, :], start=True, stop=False), m.free)
            h = pr.op("tensor", "h_z", lambda e: e.matmul(m.ap[:, 0:D], g.ap[:, :], y.ap[:, :], start=False, stop=True), hy, hg)
            y.free, g.free = [h], [h]
            return m, h

        got = [collect(n) for n in range(NT)]
        for b in range(NB):
            ns = range(b * NT, (b + 1) * NT)
            zs = [residual(n, *g) for n, g in zip(ns, got)]
            if b + 1 < NB:
                got = [collect(n + NT) for n in ns]
            hc, hs = self.ln2(lnr, [m.ap[:, 0:D] for m, _ in zs], [x2[:, n, :] for n in ns], [h for _, h in zs],
                              g2, h_g2, [xr[:, n, :] for n in ns], [h_xrb[n] for n in ns], h_sc)
            for (m, _), h in zip(zs, hc):
                m.free = [h]
            done.append(pr.dma("sync", "h_out", self.out[b].rearrange("(t p) d -> p t d", p=P),
                               xr[:, b * NT:(b + 1) * NT, :], hs))
        pr.wait("sync", done)

    def ln2(self, ring, zs, cs, ready, g, h_g, rests, h_rest, c_free):
        pr, b = self.pr, ring.take()
        t, n = b.ap, len(zs)
        hs = [pr.op("vector", "h_ln_st", lambda e, i=i: e.bn_stats(t["st"][:, i, :], zs[i]), ready[i], b.free) for i in range(n)]
        ha = [pr.op("vector", "h_ln_ag", lambda e, i=i: e.bn_aggr(t["mv"][:, i, :], t["st"][:, i, :]), hs[i], b.free) for i in range(n)]
        hv = pr.op("vector", "h_ln_ve", lambda e: e.tensor_scalar(t["ve"][:, 0:n], t["mv"][:, 0:n, 1], EPS, None, ALU.add), ha, b.free)
        hp = pr.op("gpsimd", "h_ln_rs", lambda e: e.tensor_tensor(t["rs"][:, 0:n], t["ve"][:, 0:n], self.mhalf[:, 0:n], ALU.pow),
                   hv, self.h_mhalf, b.free)
        hc = [pr.op("vector", "h_ln_c", lambda e, i=i: e.scalar_tensor_tensor(
            cs[i], zs[i], t["mv"][:, i, 0:1], g[:, :], ALU.subtract, ALU.mult), ha[i], hs[i], h_g, c_free) for i in range(n)]
        out = [pr.op("vector", "h_ln_r", lambda e, i=i: e.scalar_tensor_tensor(
            rests[i], cs[i], t["rs"][:, i:i + 1], rests[i], ALU.mult, ALU.add), hc[i], hp, h_rest[i]) for i in range(n)]
        b.free = out
        return hc, out


def build(nc, ins, out):
    with ExitStack() as ctx:
        k = Kernel(nc, ctx, ins, out)
        k.phase1()
        k.phase2()
        k.phase3()
        k.pr.issue(nc, ctx)


def constants():
    inv = (np.float32(1.0) / np.power(np.float32(10000.0), np.arange(0, 16, 2, dtype=np.float32) / np.float32(16))).astype(np.float32)
    ang = (np.arange(S, dtype=np.float32)[:, None] * inv[None, :]).astype(np.float32).astype(np.float64)
    cos, sin = np.cos(ang).astype(np.float32), np.sin(ang).astype(np.float32)
    cos2 = np.concatenate([cos, cos], 1).reshape(NT, P, 16).transpose(1, 0, 2)
    sin2 = np.concatenate([-sin, sin], 1).reshape(NT, P, 16).transpose(1, 0, 2)
    before = np.tril(np.ones((8, 8), np.float32), -1)
    wide = lambda v: np.ascontiguousarray(np.broadcast_to(v.astype(np.float32), (P, v.size)))
    return {
        "c_upper": np.triu(np.ones((P, P), np.float32), 1),
        "c_thr": wide(np.arange(2 * NB * NT) * P),
        "c_iota": wide(np.arange(80)),
        "c_ident": np.eye(P, dtype=np.float32),
        "c_cos": np.ascontiguousarray(cos2),
        "c_sin": np.ascontiguousarray(sin2),
        "c_before": np.ascontiguousarray(np.broadcast_to(before, (P, 8, 8))),
    }


def layout(inputs):
    a = {k: np.ascontiguousarray(v) for k, v in inputs.items()}
    col = lambda v, n: np.ascontiguousarray(v.reshape(n, P).T)
    t = {
        "x": a["x"], "fside": a["fside_16xSxS_0"], "cond": a["cond_64"], "mask": a["mask_BxS_bk0"].view(np.int32),
        "g_in": col(a["L0_cond_g_in"], 2), "g_out": col(a["L0_cond_g_out"], 2),
        "null_bias": a["L0_cond_null_attn_bias"], "cond_wq": a["L0_cond_Wq"], "cond_wkv": a["L0_cond_Wkv"],
        "cond_wo": a["L0_cond_Wo"],
        "attn_wq": a["L0_attn_Wq"], "attn_bq": a["L0_attn_bq"], "attn_wdown": a["L0_attn_Wdown"],
        "attn_bdown": a["L0_attn_bdown"], "attn_wup": a["L0_attn_Wup"], "attn_bup": a["L0_attn_bup"],
        "attn_wout": a["L0_attn_Wout"], "attn_bout": a["L0_attn_bout"],
        "condT": np.ascontiguousarray(a["cond_64"].T),
        "moe_wt": np.ascontiguousarray(a["L0_cond2_wt"].T), "moe_wg": np.ascontiguousarray(a["L0_cond2_wg"].T),
        "moe_gate": a["L0_cond2_w_gate"], "moe_up": a["L0_cond2_w_up"], "moe_down": a["L0_cond2_w_down"],
        "sh_gate": a["L0_cond2_sw_gate"], "sh_up": a["L0_cond2_sw_up"], "sh_down": a["L0_cond2_sw_down"],
        "wi": np.ascontiguousarray(a["L0_ffn_in_proj_w"].T), "bi": a["L0_ffn_in_proj_b"],
        "bic": col(a["L0_ffn_in_proj_b"], 6),
        "wo2": np.ascontiguousarray(a["L0_ffn_out_proj_w"].T), "bo2": a["L0_ffn_out_proj_b"],
        "ln1_g": a["L0_ffn_ln1_g"], "ln1_b": a["L0_ffn_ln1_b"], "ln2_g": a["L0_ffn_ln2_g"], "ln2_b": a["L0_ffn_ln2_b"],
        "w_group": a["L0_ffn_w_group"], "b_group": a["L0_ffn_b_group"],
        "w_expert": a["L0_ffn_w_expert"], "b_expert": a["L0_ffn_b_expert"].reshape(8),
        "w1": a["L0_ffn_w1"], "b1": a["L0_ffn_b1"], "w2": a["L0_ffn_w2"], "b2": a["L0_ffn_b2"],
    }
    t.update(constants())
    return t


def kernel(**inputs):
    import concourse.bacc as bacc
    from concourse.bass_utils import run_bass_kernel_spmd

    arrays = layout({k: np.asarray(v) for k, v in inputs.items()})
    nc = bacc.Bacc("TRN2", target_bir_lowering=False, num_devices=1, dynamic_dma_scratch_size=2048)
    ins = {k: nc.dram_tensor("in_" + k, v.shape, mybir.dt.from_np(v.dtype), kind="ExternalInput").ap()
           for k, v in arrays.items()}
    out = nc.dram_tensor("out_y", (NB, S, D), F32, kind="ExternalOutput").ap()
    build(nc, ins, out)
    r = run_bass_kernel_spmd(nc, [{"in_" + k: v for k, v in arrays.items()}], core_ids=[0])
    return r.results[0]["out_y"]
```
